# Optimizing a Trainium2 kernel written in Bass

```python
import numpy as np
import jax
import jax.numpy as jnp

def _softmax(x, axis=-1):
    return jax.nn.softmax(x, axis=axis)

def _gelu(x):
    return jax.nn.gelu(x, approximate=True)

def _silu(x):
    return jax.nn.silu(x)

def _sigmoid(x):
    return jax.nn.sigmoid(x)

def _layernorm(x, axis=-1, eps=1e-05):
    m = jnp.mean(x, axis=axis, keepdims=True)
    v = jnp.var(x, axis=axis, keepdims=True)
    return (x - m) / jnp.sqrt(v + eps)

def _scatter_add(tgt, idx, src, axis=0):
    return tgt.at[idx].add(src)

def _segment_sum(src, seg, n):
    return jax.ops.segment_sum(src, seg, n)
kernel_name = 'mk_gps_d1_gnn_r8_0906a6'

def setup_inputs(seed: int=0):
    np.random.seed(seed)
    _w = jnp.asarray

    def _rec_inputs():
        import jax
        import jax.numpy as jnp
        _gk = jax.random.key(seed)
        x = -5.39e-05 + 0.9998 * jax.random.normal(jax.random.fold_in(_gk, 1), (12500, 256), jnp.float32)
        _s = jax.random.randint(jax.random.fold_in(_gk, 2), (100000,), 0, 12500, jnp.int32)
        _d = jax.random.randint(jax.random.fold_in(_gk, 3), (100000,), 0, 12500, jnp.int32)
        _loop = jnp.arange(12500, dtype=jnp.int32)
        src = jnp.concatenate([_s, _d, _loop])
        dst = jnp.concatenate([_d, _s, _loop])
        _o = jnp.argsort(dst, stable=True)
        src = src[_o]
        dst = dst[_o]
        return (x, src, dst)
    x, src, dst = _rec_inputs()

    def _L0_gnn_setup():
        import jax, jax.numpy as jnp
        import numpy as np
        NUM_NODES = 12500
        IN_CH = 256
        HIDDEN = 128
        OUT_CH = 256
        NUM_EDGES = 400000

        def gcn_conv(x, W, b, src, dst, num_nodes):
            h = x @ W
            loop = jnp.arange(num_nodes, dtype=src.dtype)
            s = jnp.concatenate([src, loop])
            d = jnp.concatenate([dst, loop])
            deg = jax.ops.segment_sum(jnp.ones_like(d, dtype=h.dtype), d, num_segments=num_nodes)
            dinv = jnp.where(deg > 0, jax.lax.rsqrt(deg), 0.0)
            norm = dinv[s] * dinv[d]
            msg = h[s] * norm[:, None]
            out = jax.ops.segment_sum(msg, d, num_segments=num_nodes)
            return out + b
        key = jax.random.key(seed)
        k1, k2, k3, k4 = jax.random.split(key, 4)
        edge_index = jax.random.randint(k1, (2, NUM_EDGES), 0, NUM_NODES, dtype=jnp.int64)
        node_features = jax.random.normal(k2, (NUM_NODES, IN_CH), dtype=jnp.float32)
        W1 = jax.random.normal(k3, (IN_CH, HIDDEN), dtype=jnp.float32) * (1.0 / np.sqrt(IN_CH))
        b1 = jnp.zeros((HIDDEN,), dtype=jnp.float32)
        W2 = jax.random.normal(k4, (HIDDEN, OUT_CH), dtype=jnp.float32) * (1.0 / np.sqrt(HIDDEN))
        b2 = jnp.zeros((OUT_CH,), dtype=jnp.float32)
        return {'node_features': node_features, 'W1': W1, 'b1': b1, 'W2': W2, 'b2': b2, 'edge_index': edge_index}
    _L0_gnn_all = _L0_gnn_setup()
    _L0_gnn_in = {k: v for k, v in _L0_gnn_all.items() if k in ('W1', 'b1', 'W2', 'b2')}
    del _L0_gnn_all

    def _L0_mix_setup():
        import jax, jax.numpy as jnp
        import numpy as np
        BN_EPS = 1e-05
        key = jax.random.key(seed)
        ks = jax.random.split(key, 4)
        B, N, D = (8, 1024, 256)
        outD = 256
        s = 1.0 / np.sqrt(D)
        return {'feature': jax.random.normal(ks[0], (B, N, D), dtype=jnp.float32), 'W_qk': jax.random.normal(ks[1], (2, D, D), dtype=jnp.float32) * s, 'b_qk': jnp.zeros((2, D), dtype=jnp.float32), 'W_v': jax.random.normal(ks[2], (D, outD), dtype=jnp.float32) * s, 'b_v': jnp.zeros((outD,), dtype=jnp.float32), 'gamma': jnp.ones((D,), dtype=jnp.float32), 'beta': jnp.zeros((D,), dtype=jnp.float32)}
    _L0_mix_all = _L0_mix_setup()
    _L0_mix_in = {k: v for k, v in _L0_mix_all.items() if k in ('W_qk', 'b_qk', 'W_v', 'b_v', 'gamma', 'beta')}
    del _L0_mix_all

    def _L0_ffn_setup():
        import jax, jax.numpy as jnp
        import numpy as np
        B, S, D = (8, 512, 256)
        H = 4 * D
        CAPACITY = 0.5
        key = jax.random.key(seed)
        ks = jax.random.split(key, 6)
        x = jax.random.normal(ks[0], (B, S, D), dtype=jnp.float32)
        attention_mask = jnp.zeros((B, 1, 1, S), dtype=jnp.float32)
        wr = jax.random.normal(ks[1], (D, 1), dtype=jnp.float32) * 0.02
        br = jnp.zeros((1,), dtype=jnp.float32)
        w1 = jax.random.normal(ks[2], (D, H), dtype=jnp.float32) * 0.02
        b1 = jnp.zeros((H,), dtype=jnp.float32)
        w2 = jax.random.normal(ks[3], (H, D), dtype=jnp.float32) * 0.02
        b2 = jnp.zeros((D,), dtype=jnp.float32)
        return {'x': x, 'attention_mask': attention_mask, 'wr': wr, 'br': br, 'w1': w1, 'b1': b1, 'w2': w2, 'b2': b2}
    _L0_ffn_all = _L0_ffn_setup()
    _L0_ffn_in = {k: v for k, v in _L0_ffn_all.items() if k in ('attention_mask', 'wr', 'br', 'w1', 'b1', 'w2', 'b2')}
    del _L0_ffn_all
    return {'x': x, 'src': src, 'dst': dst, 'L0_gnn_W1': _L0_gnn_in['W1'], 'L0_gnn_b1': _L0_gnn_in['b1'], 'L0_gnn_W2': _L0_gnn_in['W2'], 'L0_gnn_b2': _L0_gnn_in['b2'], 'L0_mix_W_qk': _L0_mix_in['W_qk'], 'L0_mix_b_qk': _L0_mix_in['b_qk'], 'L0_mix_W_v': _L0_mix_in['W_v'], 'L0_mix_b_v': _L0_mix_in['b_v'], 'L0_mix_gamma': _L0_mix_in['gamma'], 'L0_mix_beta': _L0_mix_in['beta'], 'L0_ffn_attention_mask': _L0_ffn_in['attention_mask'], 'L0_ffn_wr': _L0_ffn_in['wr'], 'L0_ffn_br': _L0_ffn_in['br'], 'L0_ffn_w1': _L0_ffn_in['w1'], 'L0_ffn_b1': _L0_ffn_in['b1'], 'L0_ffn_w2': _L0_ffn_in['w2'], 'L0_ffn_b2': _L0_ffn_in['b2']}

def reference(x, src, dst, L0_gnn_W1, L0_gnn_b1, L0_gnn_W2, L0_gnn_b2, L0_mix_W_qk, L0_mix_b_qk, L0_mix_W_v, L0_mix_b_v, L0_mix_gamma, L0_mix_beta, L0_ffn_attention_mask, L0_ffn_wr, L0_ffn_br, L0_ffn_w1, L0_ffn_b1, L0_ffn_w2, L0_ffn_b2):
    import jax
    import jax.numpy as jnp

    def _L0_gnn_ref(node_features, W1, b1, W2, b2, edge_index):
        import jax, jax.numpy as jnp
        import numpy as np
        NUM_NODES = 12500
        IN_CH = 256
        HIDDEN = 128
        OUT_CH = 256
        NUM_EDGES = 400000

        def gcn_conv(x, W, b, src, dst, num_nodes):
            h = x @ W
            loop = jnp.arange(num_nodes, dtype=src.dtype)
            s = jnp.concatenate([src, loop])
            d = jnp.concatenate([dst, loop])
            deg = jax.ops.segment_sum(jnp.ones_like(d, dtype=h.dtype), d, num_segments=num_nodes)
            dinv = jnp.where(deg > 0, jax.lax.rsqrt(deg), 0.0)
            norm = dinv[s] * dinv[d]
            msg = h[s] * norm[:, None]
            out = jax.ops.segment_sum(msg, d, num_segments=num_nodes)
            return out + b
        src, dst = (edge_index[0], edge_index[1])
        x = gcn_conv(node_features, W1, b1, src, dst, NUM_NODES)
        x = jax.nn.relu(x)
        x = gcn_conv(x, W2, b2, src, dst, NUM_NODES)
        return x

    def _L0_mix_ref(feature, W_qk, b_qk, W_v, b_v, gamma, beta):
        import jax, jax.numpy as jnp
        import numpy as np
        BN_EPS = 1e-05
        QK = jnp.einsum('bnd,kde->bkne', feature, W_qk) + b_qk[None, :, None, :]
        value = jnp.einsum('bnd,de->bne', feature, W_v) + b_v
        query = QK[:, 0]
        key = QK[:, 1]
        sm = jax.nn.softmax(key, axis=1)
        lam = jnp.einsum('bnd,bne->bde', sm, value)
        mean = jnp.mean(lam, axis=(0, 2), keepdims=True)
        var = jnp.var(lam, axis=(0, 2), keepdims=True)
        bn = (lam - mean) * jax.lax.rsqrt(var + BN_EPS)
        bn = bn * gamma[None, :, None] + beta[None, :, None]
        return jnp.einsum('bnd,bde->bne', query, bn)

    def _L0_ffn_ref(x, attention_mask, wr, br, w1, b1, w2, b2):
        import jax, jax.numpy as jnp
        import numpy as np
        B, S, D = (8, 512, 256)
        H = 4 * D
        CAPACITY = 0.5
        b, s, d = x.shape
        weights = (jnp.einsum('bsd,do->bso', x, wr) + br)[..., 0]
        k = max(1, int(CAPACITY * s))
        kk = k - 1 if k > 1 else 1
        _, idx = jax.lax.top_k(weights, k)
        sel_idx = idx[:, :kk]
        sel = jnp.take_along_axis(x, sel_idx[:, :, None], axis=1)
        h = jax.nn.gelu(jnp.einsum('bkd,dh->bkh', sel, w1) + b1)
        y = jnp.einsum('bkh,hd->bkd', h, w2) + b2
        w_sel = jnp.take_along_axis(weights, sel_idx, axis=1)
        y = y * w_sel[..., None]
        batch_idx = jnp.arange(b)[:, None]
        processed = jnp.zeros_like(x).at[batch_idx, sel_idx].set(y)
        return processed + x
    edge_index = jnp.stack([src, dst])
    xn = _layernorm(x, axis=-1)
    x = x + _L0_gnn_ref(xn, L0_gnn_W1, L0_gnn_b1, L0_gnn_W2, L0_gnn_b2, edge_index) + _L0_mix_ref(xn[None], L0_mix_W_qk, L0_mix_b_qk, L0_mix_W_v, L0_mix_b_v, L0_mix_gamma, L0_mix_beta)[0]
    x = x + _L0_ffn_ref(_layernorm(x, axis=-1)[None], L0_ffn_attention_mask, L0_ffn_wr, L0_ffn_br, L0_ffn_w1, L0_ffn_b1, L0_ffn_w2, L0_ffn_b2)[0]
    return x

_drawn_inputs = setup_inputs


def setup_inputs(seed=0):
    import zlib

    import numpy as np

    out = dict(_drawn_inputs(seed))
    spreads = {'L0_gnn_b1': (0.0, 0.8),
     'L0_gnn_b2': (0.0, 0.8),
     'L0_mix_b_qk': (0.0, 0.1),
     'L0_mix_b_v': (0.0, 0.1),
     'L0_mix_gamma': (1.0, 0.2),
     'L0_mix_beta': (0.0, 0.1),
     'L0_ffn_b1': (0.0, 0.8),
     'L0_ffn_b2': (0.0, 0.8)}
    factors = {'L0_gnn_W1': 8.0, 'L0_gnn_W2': 7.446, 'L0_ffn_wr': 8.0, 'L0_ffn_w1': 8.0, 'L0_ffn_w2': 8.0}
    for name, (base, spread) in spreads.items():
        noise = np.random.default_rng([zlib.crc32(name.encode()), seed]).standard_normal(out[name].shape)
        drawn = base * np.exp(spread * noise) if base else spread * noise
        out[name] = jnp.asarray(drawn.astype(out[name].dtype))
    for name, factor in factors.items():
        out[name] = (out[name] * factor).astype(out[name].dtype)
    return out
```

```python
import concourse.bass as bass
from concourse import mybir
from contextlib import ExitStack
import math


def gps_layer_kernel(nc, x, src, dst, W1, b1, W2, b2, W_qk, b_qk, W_v, b_v, gamma, beta, attention_mask, wr, br,
                     w1, fb1, w2, fb2, out):
    f32, bf16, i32 = mybir.dt.float32, mybir.dt.bfloat16, mybir.dt.int32
    ALU, ACT, AX = mybir.AluOpType, mybir.ActivationFunctionType, mybir.AxisListType
    ds = bass.ds

    P = 128
    N, D = x.shape
    F = W1.shape[1]
    HID = w1.shape[1]
    E = src.shape[0]
    TILES = math.ceil(N / P)
    LAST = N - (TILES - 1) * P
    KD, KH = D // P, HID // P
    HALF = 8
    PAIR = 2 * HALF
    PAIRS = 2 * math.ceil(math.ceil(E / (PAIR * P)) / 2)
    ROW = PAIR * P
    CHUNKS = PAIRS * PAIR
    EDGES_IN_LAST = E - (PAIRS - 1) * ROW
    PAD_NODE = TILES * P - 1
    GROUP = 14
    GROUPS = TILES // GROUP
    KSEL = max(1, int(0.5 * N)) - 1
    EPS = 1e-5
    assert D == KD * P and F == P and HID == KH * P and GROUPS * GROUP == TILES and PAIRS <= P
    assert 0 < EDGES_IN_LAST <= ROW and PAD_NODE >= N

    ctx = ExitStack()
    with ctx:
        def sb(name, shape, dt=f32):
            return ctx.enter_context(nc.sbuf_tensor(name, shape, dt))

        def sem(name):
            return ctx.enter_context(nc.semaphore(name))

        table = [nc.dram_tensor(f"table{i}", [TILES * P, F], f32).ap() for i in range(2)]
        base_rows = nc.dram_tensor("base_rows", [TILES * P, D], f32).ap()

        xs = sb("xs", [P, TILES, D])
        acc = sb("acc", [P, TILES, F])
        src_idx = sb("src_idx", [P, CHUNKS + PAIR], i32)
        dst_of = sb("dst_of", [P, CHUNKS])
        idx_now = sb("idx_now", [P, 2, PAIR], i32)
        ident = sb("ident", [P, P])
        iota_n = sb("iota_n", [P, P])
        tile_base = sb("tile_base", [P, TILES])
        rstd = sb("rstd", [P, TILES])
        nmr = sb("nmr", [P, TILES])
        dinv = sb("dinv", [P, TILES])
        wts = sb("wts", [P, TILES])
        ctl = sb("ctl", [1, PAIRS, 6], i32)
        released = sb("released", [1, PAIRS + 1], i32)
        gW1 = sb("gW1", [P, KD, F])
        gW2 = sb("gW2", [P, D])
        Pmix = sb("Pmix", [P, KD, D])
        crow = sb("crow", [P, D])
        b1row = sb("b1row", [P, F])
        wrrow = sb("wrrow", [P, D])
        fb2row = sb("fb2row", [P, D])
        fb1col = sb("fb1col", [P, KH])
        brcol = sb("brcol", [P, 1])
        epscol = sb("epscol", [P, 1])
        drel = sb("drel", [P, HALF])
        sm = sb("sm", [P, 64])

        ARENA = 10300
        arena = sb("arena", [P, ARENA])
        at = [0]

        def carve(*dims, dt=f32, start=None):
            if start is not None:
                at[0] = start
            n = math.prod(dims)
            words = n if dt != bf16 else n // 2
            v = arena[:, at[0]:at[0] + words]
            at[0] += words
            assert at[0] <= ARENA, at[0]
            if dt != f32:
                v = v.bitcast(dt)
            names = " ".join("abcd"[:len(dims)])
            sizes = {"abcd"[i]: dims[i] for i in range(len(dims))}
            return v if len(dims) == 1 else v.rearrange(f"p ({names}) -> p {names}", **sizes)

        oh_r = carve(2, PAIR, P, dt=bf16, start=0)
        oh_q = carve(2, PAIR, TILES, dt=bf16)
        r_of = carve(CHUNKS)
        q_of = carve(CHUNKS)
        xnA = carve(2, D)
        xTA = carve(2, D)
        ring = carve(PAIR, F, start=0)
        S = carve(HALF, P)
        after_S = at[0]
        Wk = carve(KD, D)
        Wv = carve(KD, D)
        Wq = carve(KD, D)
        WqT = carve(KD, D)
        xn = carve(D)
        xT = carve(KD, P)
        ET = carve(KD, P)
        En = carve(KD, P)
        Gs = carve(KD, D)
        GT = carve(KD, D)
        lam = carve(KD, D)
        bvrow = carve(D)
        bqb = carve(KD, P)
        fw1 = carve(KD, HID, start=after_S)
        fw2 = carve(KH, D)
        xnD = carve(D)
        x1 = carve(D)
        ln = carve(D)
        base = carve(D)
        aggs = carve(F)
        T3 = carve(3, P)
        H = carve(KH, P)
        prod = H[:, 0:2, :]
        ones_m = carve(P, start=0)
        lower = carve(P)
        cmp_ = carve(TILES)
        gt = carve(TILES)
        eq = carve(TILES)
        colsum = carve(TILES)
        before = carve(TILES)
        selw = carve(TILES)
        zer = carve(TILES)
        accf = acc[:, :, :].rearrange("p t f -> p (t f)")
        src_rows_i = accf[:, 0:ROW].bitcast(i32)
        src_rows = accf[:, ROW:2 * ROW]
        dst_rows_i = accf[:, 2 * ROW:3 * ROW].bitcast(i32)
        dst_rows = accf[:, 3 * ROW:4 * ROW]
        HG = GROUP // 2
        STEPS = TILES // HG
        SLOTS = TILES * F // (HG * D)
        tail = accf.rearrange("p (s j d) -> p s j d", s=SLOTS, j=HG)
        rng = sm[:, 0:4]
        rng_i = sb("rng_i", [P, 4], i32)
        rrow = accf[0:1, 4 * ROW:4 * ROW + 16 * PAIRS].rearrange("p (r n) -> p r n", r=8)
        stats = sb("stats", [P, 6])
        stats2 = sb("stats2", [P, 2, 6])
        mv = sb("mv", [P, 2])
        statsA = sb("statsA", [P, GROUP, 6])
        mean2 = sb("mean2", [P, GROUP])
        ssq = sb("ssq", [P, GROUP])
        dif = sb("dif", [P, GROUP])

        bank = [ctx.enter_context(nc.psum_tensor(f"bank{i}", [P, 512], f32)) for i in range(8)]
        visit_sum = [bank[0], bank[1]]
        pT, pK, pE, pG = bank[2], bank[3], bank[4], bank[5]
        pY1, pY = bank[3], bank[4]
        pH = [bank[5], bank[6]]
        pDeg = bank[7]

        s_tail_zero = sem("x_tail_zeroed")
        s_xtail = sem("x_tail_loaded")
        s_x = sem("x_group_loaded")
        s_pad = sem("edge_padding_set")
        s_edges = sem("edges_loaded")
        s_small = sem("small_inputs_loaded")
        s_const = sem("constants_made")
        s_rowsf = sem("edge_rows_as_float")
        s_eT = sem("edges_transposed")
        s_eTe = sem("transposed_edges_evacuated")
        s_rngdone = sem("ranges_ready")
        s_rngT = sem("ranges_transposed")
        s_mvA = sem("x_stats_ready")
        s_sdA = sem("x_deviation_ready")
        s_rstd = sem("x_rstd_ready")
        s_xnA = sem("xn_ready_first_pass")
        s_TA = sem("xn_transposed_first_pass")
        s_TAe = sem("xnT_evacuated_first_pass")
        s_hA = sem("h1_ready")
        s_hAe = sem("h1_evacuated")
        s_oh = sem("one_hots_ready")
        s_ohu = sem("one_hots_used")
        s_sq = sem("sqrt_degrees_ready")
        s_scaled = sem("table1_tiles_ready")
        s_tab1 = sem("table1_written")
        s_ctl = sem("control_table_ready")
        s_idx = sem("indices_ready")
        s_issue = sem("gathers_issued")
        s_dve = sem("vector_chain")
        s_bn = sem("x_stats_chain")
        s_passed_sp = sem("group_waits_passed")
        s_passed = sem("waits_passed")
        s_free = [sem(f"ring_half_free{i}") for i in range(2)]
        s_gath = [[sem(f"gathered{i}_{h}") for h in range(2)] for i in range(2)]
        s_drel = [sem(f"relative_dst{i}") for i in range(2)]
        s_S = [[sem(f"S_ready{i}_{q}") for q in range(2)] for i in range(2)]
        s_Su = [[sem(f"S_free{i}_{q}") for q in range(2)] for i in range(2)]
        s_sum = [sem(f"visit_summed{i}") for i in range(2)]
        s_fl = [sem(f"visits_added{i}") for i in range(2)]
        s_fin = sem("table2_tile_ready")
        s_fin0 = sem("table2_tile_biased")
        s_tab2 = sem("table2_written")
        s_mxn = sem("mix_xn_ready")
        s_mT = sem("mix_xn_transposed")
        s_mTe = sem("mix_xnT_evacuated")
        s_mK = sem("mix_keys_ready")
        s_mch = sem("mix_max_chain")
        s_mb = sem("mix_bias_ready")
        s_mE = sem("mix_exps_ready")
        s_mET = sem("mix_exps_transposed")
        s_mEe = sem("mix_exps_evacuated")
        s_mG = sem("mix_sums_ready")
        s_mu = sem("mix_sums_added")
        s_mch2 = sem("mix_sum_chain")
        s_mz = sem("mix_weights_loaded")
        s_m1, s_m2, s_m3 = sem("lambda_pe"), sem("lambda_evacuated"), sem("lambda_dve")
        s_mixed = sem("mixer_folded")
        s_fw = sem("ff_weights_loaded")
        s_aggs = sem("agg_scaled")
        s_dxn = sem("ff_xn_ready")
        s_dT = sem("ff_first_transposed")
        s_dTe = sem("ff_first_evacuated")
        s_y1 = sem("mixed_rows_ready")
        s_dch = sem("ff_vector_chain")
        s_var = sem("ff_variance_ready")
        s_sd = sem("ff_deviation_ready")
        s_ln = sem("ff_ln_ready")
        s_lT = sem("ff_ln_transposed")
        s_lTe = sem("ff_lnT_evacuated")
        s_h = sem("ff_hidden_ready")
        s_H = sem("ff_gelu_ready")
        s_y = sem("ff_rows_ready")
        s_base = sem("base_rows_ready")
        s_basew = sem("base_rows_written")
        s_wd = sem("weighted_rows_ready")
        s_cnt = sem("selection_counts")
        s_sel = sem("selection_chain")
        s_tl = [sem(f"base_back{i}") for i in range(SLOTS)]
        s_to = [sem(f"sums_out{i}") for i in range(SLOTS)]
        s_tf = sem("tail_rows_ready")

        block = ctx.enter_context(nc.Block())

        x_tiles = x[0:(TILES - 1) * P, :].rearrange("(t p) d -> p t d", p=P)
        base_t = base_rows.rearrange("(t p) d -> p t d", p=P)
        table_t = [t.rearrange("(t p) f -> p t f", p=P) for t in table]
        out_t = out[0:(TILES - 1) * P, :].rearrange("(t p) d -> p t d", p=P)
        SMALL_LOADS = 14

        def row(ap, n=P):
            return ap.rearrange("(a n) -> a n", a=1).broadcast_to([n, ap.shape[0]])

        def bc(ap, shape):
            return ap.broadcast_to(shape)

        def read_ctl(eng, g, h):
            lo = eng.value_load(ctl[0:1, ds(g, 1), 3 * h], min_val=0, max_val=TILES - 1)
            hi = eng.value_load(ctl[0:1, ds(g, 1), 3 * h + 1], min_val=1, max_val=TILES)
            v0 = eng.value_load(ctl[0:1, ds(g, 1), 3 * h + 2], min_val=0, max_val=2 * PAIRS * TILES)
            return lo, hi, v0

        def read_released(eng, g):
            a = eng.value_load(released[0:1, ds(g, 1)], min_val=0, max_val=TILES - 1)
            b = eng.value_load(released[0:1, ds(g + 1, 1)], min_val=0, max_val=TILES - 1)
            return a, b

        @block.sync
        def _(sp):
            sp.wait_ge(s_pad, 2)
            full = (PAIRS - 1) * ROW
            for rows_i, e in ((dst_rows_i, dst), (src_rows_i, src)):
                sp.dma_start(rows_i[0:PAIRS - 1, :], e[0:full].rearrange("(p e) -> p e", e=ROW)).then_inc(s_edges, 16)
                sp.dma_start(rows_i[PAIRS - 1:PAIRS, 0:EDGES_IN_LAST],
                             e[full:E].rearrange("(a e) -> a e", a=1)).then_inc(s_edges, 16)
            sp.wait_ge(s_tail_zero, 1)
            sp.dma_start(xs[0:LAST, TILES - 1, :], x[(TILES - 1) * P:N, :]).then_inc(s_xtail, 16)
            with sp.Fori(0, GROUPS - 1) as g:
                sp.dma_start(xs[:, ds(g * GROUP, GROUP), :], x_tiles[:, ds(g * GROUP, GROUP), :]).then_inc(s_x, 16)
                sp.wait_ge(s_x, g * 16 + 16)
                sp.sem_inc(s_passed_sp, 1)
            sp.dma_start(xs[:, TILES - GROUP:TILES - 1, :],
                         x_tiles[:, TILES - GROUP:TILES - 1, :]).then_inc(s_x, 16)
            with sp.Fori(0, GROUPS) as g:
                sp.wait_ge(s_scaled, g + 1)
                sp.dma_start(table_t[0][:, ds(g * GROUP, GROUP), :], acc[:, ds(g * GROUP, GROUP), :]).then_inc(s_tab1, 16)
            with sp.Fori(0, TILES) as t:
                sp.wait_ge(s_fin, t + 1)
                sp.dma_start(table_t[1][:, ds(t, 1), :], acc[:, ds(t, 1), :]).then_inc(s_tab2, 16)
            sp.wait_ge(s_mixed, 1)
            sp.dma_start(fw1, w1.rearrange("(k p) h -> p k h", p=P)).then_inc(s_fw, 16)
            sp.dma_start(fw2, w2.rearrange("(k p) d -> p k d", p=P)).then_inc(s_fw, 16)
            sp.sem_inc(s_basew, 16)
            with sp.Fori(0, TILES) as t:
                sp.wait_ge(s_base, t + 1)
                sp.dma_start(base_t[:, ds(t, 1), :], base.rearrange("p (a d) -> p a d", a=1)).then_inc(s_basew, 16)
            sp.wait_ge(s_basew, 16 * (TILES + 1))
            sp.wait_ge(s_wd, TILES)

            def load_base(i):
                if i >= SLOTS:
                    sp.wait_ge(s_to[i % SLOTS], 16)
                sp.dma_start(tail[:, i % SLOTS, :, :], base_t[:, i * HG:(i + 1) * HG, :]).then_inc(s_tl[i % SLOTS], 16)

            for i in range(SLOTS):
                load_base(i)
            for j in range(STEPS):
                sp.wait_ge(s_tf, j + 1)
                if j < STEPS - 1:
                    sp.dma_start(out_t[:, j * HG:(j + 1) * HG, :], tail[:, j % SLOTS, :, :])\
                      .then_inc(s_to[j % SLOTS], 16)
                else:
                    sp.dma_start(out_t[:, j * HG:TILES - 1, :], tail[:, j % SLOTS, 0:HG - 1, :])\
                      .then_inc(s_to[j % SLOTS], 16)
                    sp.dma_start(out[(TILES - 1) * P:N, :], tail[0:LAST, j % SLOTS, HG - 1, :])\
                      .then_inc(s_to[j % SLOTS], 16)
                if 2 <= j and j - 2 + SLOTS < STEPS:
                    load_base(j - 2 + SLOTS)
            for i in range(SLOTS):
                steps_here = len(range(i, STEPS, SLOTS))
                sp.wait_ge(s_to[i], 16 * (steps_here + (i == (STEPS - 1) % SLOTS)))

        @block.gpsimd
        def _(pool):
            pool.memset(dst_rows_i[0:PAIRS, EDGES_IN_LAST:ROW], PAD_NODE).then_inc(s_pad, 1)
            pool.memset(src_rows_i[0:PAIRS, EDGES_IN_LAST:ROW], 0).then_inc(s_pad, 1)
            pool.memset(xs[:, TILES - 1, :], 0.0).then_inc(s_tail_zero, 1)
            pool.memset(ident[:, :], 0.0).then_inc(s_issue, 1)
            pool.wait_ge(s_issue, 1)
            pool.affine_select(out=ident[:, :], in_=ident[:, :], compare_op=ALU.not_equal, fill=1.0, base=0,
                               pattern=[[-1, P]], channel_multiplier=1).then_inc(s_const, 1)
            pool.iota(iota_n[:, :], [[1, P]], base=0, channel_multiplier=0,
                      allow_small_or_imprecise_dtypes=True).then_inc(s_const, 1)
            pool.iota(tile_base[:, :], [[P, TILES]], base=0, channel_multiplier=0,
                      allow_small_or_imprecise_dtypes=True).then_inc(s_const, 1)
            pool.memset(src_idx[:, CHUNKS:CHUNKS + PAIR], 0).then_inc(s_const, 1)

            def gather_layer(layer):
                with pool.Fori(0, PAIRS // 2) as gg:
                    for par in range(2):
                        pool.wait_ge(s_idx, gg * 2 + (layer * (PAIRS + 1) + par + 1))
                        pool.sem_inc(s_issue, 1)
                        for h in range(2):
                            pool.wait_ge(s_free[layer], gg * 4 + (2 * par + h + 1))
                            pool.sem_inc(s_issue, 1)
                            for k in range(HALF):
                                c = h * HALF + k
                                pool.indirect_dma_start(
                                    ring[:, c, :], None, table[layer],
                                    bass.IndirectOffsetOnAxis(ap=idx_now[:, par, c:c + 1], axis=0),
                                ).then_inc(s_gath[layer][h], 16)

            pool.wait_ge(s_tab1, 16 * GROUPS)
            gather_layer(0)
            pool.wait_ge(s_tab2, 16 * TILES)
            gather_layer(1)

        @block.scalar
        def _(act):
            act.dma_start(gW1[:, :, :], W1.rearrange("(k p) f -> p k f", p=P)).then_inc(s_small, 16)
            act.dma_start(gW2[:, :], W2).then_inc(s_small, 16)
            act.dma_start(b1row[:, :], row(b1)).then_inc(s_small, 16)
            act.dma_start(crow[:, :], row(b2)).then_inc(s_small, 16)
            act.dma_start(wrrow[:, :], row(wr.rearrange("d o -> (d o)"))).then_inc(s_small, 16)
            act.dma_start(fb2row[:, :], row(fb2)).then_inc(s_small, 16)
            act.dma_start(brcol[:, :], row(br)).then_inc(s_small, 16)
            with nc.allow_non_contiguous_dma("per-partition biases"):
                act.dma_start(fb1col[:, :], fb1.rearrange("(k p) -> p k", p=P)).then_inc(s_small, 16)
                act.dma_start(sm[:, 8:10], gamma.rearrange("(k p) -> p k", p=P)).then_inc(s_small, 16)
                act.dma_start(sm[:, 10:12], beta.rearrange("(k p) -> p k", p=P)).then_inc(s_small, 16)
                act.dma_start(sm[:, 12:14], b_qk[0, :].rearrange("(k p) -> p k", p=P)).then_inc(s_small, 16)
                act.dma_start(sm[:, 14:16], b_qk[1, :].rearrange("(k p) -> p k", p=P)).then_inc(s_small, 16)
            for e in range(2):
                for b in range(PAIR // 4):
                    i = e * (PAIR // 4) + b
                    act.wait_ge(s_eT, i + 1)
                    view = bank[i % 2][:, 0:4 * PAIRS].rearrange("p (c g) -> p g c", g=PAIRS)
                    to = (dst_of if e == 0 else src_idx)[:, 0:CHUNKS].rearrange("p (g c) -> p g c", c=PAIR)
                    act.activation(to[:, :, 4 * b:4 * b + 4], view, ACT.Copy).then_inc(s_eTe, 1)

            def tile_a(g, j, first):
                n = g * GROUP + j
                if not (first and j < 2):
                    act.wait_ge(s_TA, n - 1)
                act.activation(xnA[:, j % 2, :], xs[:, ds(n, 1), :].rearrange("p a d -> p (a d)"), ACT.Identity,
                               bias=nmr[:, ds(n, 1)], scale=rstd[:, ds(n, 1)]).then_inc(s_xnA, 1)

            def tile_b(g, j, first):
                n = g * GROUP + j
                act.wait_ge(s_TA, n + 1)
                if not (first and j < 2):
                    act.wait_ge(s_hA, n - 1)
                act.activation(xTA[:, j % 2, :], bank[2 + j % 2][:, 0:D], ACT.Copy).then_inc(s_TAe, 1)

            def tile_c(g, j):
                n = g * GROUP + j
                act.wait_ge(s_hA, n + 1)
                act.activation(acc[:, ds(n, 1), :].rearrange("p a d -> p (a d)"), bank[4 + j % 2][:, 0:F],
                               ACT.Copy).then_inc(s_hAe, 1)

            def group(g, first):
                act.wait_ge(s_mvA, g + 1)
                act.activation(rstd[:, ds(g * GROUP, GROUP)], ssq[:, :], ACT.Sqrt, bias=epscol[:, 0:1],
                               scale=1.0 / D).then_inc(s_sdA, 1)
                act.wait_ge(s_rstd, g + 1)
                for j in range(GROUP + 2):
                    if j < GROUP:
                        tile_a(g, j, first)
                    if 1 <= j <= GROUP:
                        tile_b(g, j - 1, first)
                    if j >= 2:
                        tile_c(g, j - 2)

            group(0, True)
            with act.Fori(1, GROUPS) as g:
                group(g, False)
            act.wait_ge(s_ohu, PAIRS)
            act.activation(dinv[:, :], pDeg[:, 0:TILES], ACT.Sqrt, bias=1.0).then_inc(s_sq, 1)

            act.wait_ge(s_scaled, 1)
            act.dma_start(Wk, W_qk[1].rearrange("(k p) e -> p k e", p=P)).then_inc(s_mz, 16)
            act.dma_start(Wq, W_qk[0].rearrange("(k p) e -> p k e", p=P)).then_inc(s_mz, 16)
            act.dma_start(Wv, W_v.rearrange("(k p) e -> p k e", p=P)).then_inc(s_mz, 16)
            act.dma_start(bvrow, row(b_v)).then_inc(s_mz, 16)

            def mix(t, n):
                act.wait_ge(s_mG, t + 1)
                act.activation(xn, xs[:, ds(t, 1), :].rearrange("p a d -> p (a d)"), ACT.Identity,
                               bias=nmr[:, ds(t, 1)], scale=rstd[:, ds(t, 1)]).then_inc(s_mxn, 1)
                act.wait_ge(s_mT, t + 1)
                act.activation(xT.rearrange("p k n -> p (k n)"), pT[:, 0:D], ACT.Copy).then_inc(s_mTe, 1)
                act.wait_ge(s_mb, t + 1)
                act.activation(sm[:, 22:24], sm[:, 20:22], ACT.Exp)
                for k in range(KD):
                    last = act.activation(ET[:, k, 0:n], pK[:, k * P:k * P + n], ACT.Exp, bias=sm[:, 24 + k:25 + k],
                                          accum_out=sm[:, 26 + k:27 + k])
                last.then_inc(s_mE, 1)
                act.wait_ge(s_mET, t + 1)
                act.activation(En.rearrange("p k n -> p (k n)"), pE[:, 0:D], ACT.Copy).then_inc(s_mEe, 1)

            with act.Fori(0, TILES - 1) as t:
                mix(t, P)
            mix(TILES - 1, LAST)
            for i, (dsts, srcs) in enumerate(((GT, pT), (WqT, pK))):
                act.wait_ge(s_m1, i + 1)
                act.activation(dsts.rearrange("p k d -> p (k d)"), srcs[:, :], ACT.Copy).then_inc(s_m2, 1)
            act.wait_ge(s_m3, 2)
            act.activation(sm[:, 34:36], sm[:, 32:34], ACT.Sqrt, bias=epscol[:, 0:1]).then_inc(s_m2, 1)
            act.wait_ge(s_m1, 4)
            act.activation(Pmix[:, :, :].rearrange("p k d -> p (k d)"), pG[:, :], ACT.Copy).then_inc(s_m2, 1)

            act.wait_ge(s_mixed, 1)
            with act.Fori(0, TILES) as t:
                act.activation(xnD, xs[:, ds(t, 1), :].rearrange("p a d -> p (a d)"), ACT.Identity,
                               bias=nmr[:, ds(t, 1)], scale=rstd[:, ds(t, 1)]).then_inc(s_dxn, 1)
                act.wait_ge(s_dT, t + 1)
                act.activation(T3.rearrange("p k n -> p (k n)"), pT[:, 0:3 * P], ACT.Copy).then_inc(s_dTe, 1)
                act.wait_ge(s_var, t + 1)
                act.activation(sm[:, 40:41], mv[:, 1:2], ACT.Sqrt, bias=epscol[:, 0:1]).then_inc(s_sd, 1)
                act.wait_ge(s_lT, t + 1)
                act.activation(T3[:, 0:KD, :].rearrange("p k n -> p (k n)"), pT[:, 0:D], ACT.Copy).then_inc(s_lTe, 1)
                act.wait_ge(s_h, t + 1)
                for k in range(KH):
                    last = act.activation(H[:, k, :], pH[k // 4][:, (k % 4) * P:(k % 4 + 1) * P],
                                          ACT.Gelu_apprx_tanh, bias=fb1col[:, k:k + 1])
                last.then_inc(s_H, 1)

        @block.tensor
        def _(pe):
            pe.wait_ge(s_const, 3)
            for e in range(2):
                pe.wait_ge(s_rowsf, e + 1)
                rows = (dst_rows, src_rows)[e]
                for b in range(PAIR // 4):
                    i = e * (PAIR // 4) + b
                    if i >= 2:
                        pe.wait_ge(s_eTe, i - 1)
                    for c in range(4):
                        k = 4 * b + c
                        last = nc.tensor.transpose(bank[i % 2][:, c * PAIRS:(c + 1) * PAIRS],
                                                   rows[0:PAIRS, k * P:(k + 1) * P], ident[0:PAIRS, 0:PAIRS])
                    last.then_inc(s_eT, 1)
            pe.wait_ge(s_rngdone, 1)
            for i in range(4):
                last = nc.tensor.transpose(bank[6][0:1, i * P:i * P + PAIRS], rng[0:PAIRS, i:i + 1],
                                           ident[0:PAIRS, 0:PAIRS])
            last.then_inc(s_rngT, 1)
            pe.wait_ge(s_small, 16 * 12)

            def transposes_a(g, j, first):
                n = g * GROUP + j
                pe.wait_ge(s_xnA, n + 1)
                if not (first and j < 2):
                    pe.wait_ge(s_TAe, n - 1)
                for k in range(KD):
                    last = nc.tensor.transpose(bank[2 + j % 2][:, k * P:(k + 1) * P],
                                               xnA[:, j % 2, k * P:(k + 1) * P], ident[:, :])
                last.then_inc(s_TA, 1)

            def h1_a(g, j, first):
                n = g * GROUP + j
                pe.wait_ge(s_TAe, n + 1)
                if not (first and j < 2):
                    pe.wait_ge(s_hAe, n - 1)
                for k in range(KD):
                    last = nc.tensor.matmul(bank[4 + j % 2][:, 0:F], xTA[:, j % 2, k * P:(k + 1) * P], gW1[:, k, :],
                                            start=(k == 0), stop=(k == KD - 1))
                last.then_inc(s_hA, 1)

            def group(g, first):
                for j in range(GROUP + 1):
                    if j < GROUP:
                        transposes_a(g, j, first)
                    if j >= 1:
                        h1_a(g, j - 1, first)

            group(0, True)
            with pe.Fori(1, GROUPS) as g:
                group(g, False)

            def degrees(gg, first, last_gg):
                for par in range(2):
                    pe.wait_ge(s_oh, gg * 2 + par + 1)
                    for c in range(PAIR):
                        last = nc.tensor.matmul(pDeg[:, 0:TILES], oh_r[:, par, c, :], oh_q[:, par, c, :],
                                                start=(first and par == 0 and c == 0),
                                                stop=(last_gg and par == 1 and c == PAIR - 1))
                    last.then_inc(s_ohu, 1)
                return last

            degrees(0, True, False)
            with pe.Fori(1, PAIRS // 2 - 1) as gg:
                degrees(gg, False, False)
            degrees(PAIRS // 2 - 1, False, True)

            pe.wait_ge(s_ctl, 1)

            def visits(layer, g, h):
                lo, hi, v0 = read_ctl(pe, g, h)
                with pe.Fori(lo, hi) as t:
                    v = v0 + t
                    pe.wait_ge(s_gath[layer][h], g * (16 * HALF) + 16 * HALF)
                    pe.wait_ge(s_fl[layer], v + 1)
                    for k in range(HALF):
                        q = k // 4
                        if k % 4 == 0:
                            pe.wait_ge(s_S[layer][q], v + 1)
                        last = nc.tensor.matmul(visit_sum[h][:, 0:F], S[:, k, :], ring[:, h * HALF + k, :],
                                                start=(k == 0), stop=(k == HALF - 1))
                        if k == 3:
                            last.then_inc(s_Su[layer][0], 1)
                    last.then_inc(s_sum[layer], 1)

            def mix_1(t):
                pe.wait_ge(s_mxn, t + 1)
                for k in range(KD):
                    last = nc.tensor.transpose(pT[:, k * P:(k + 1) * P], xn[:, k * P:(k + 1) * P], ident[:, :])
                last.then_inc(s_mT, 1)
                pe.wait_ge(s_mTe, t + 1)
                for e in range(KD):
                    for k in range(KD):
                        last = nc.tensor.matmul(pK[:, e * P:(e + 1) * P], Wk[:, k, e * P:(e + 1) * P], xT[:, k, :],
                                                start=(k == 0), stop=(k == KD - 1))
                last.then_inc(s_mK, 1)

            def mix_2(t):
                pe.wait_ge(s_mE, t + 1)
                for k in range(KD):
                    last = nc.tensor.transpose(pE[:, k * P:(k + 1) * P], ET[:, k, :], ident[:, :])
                last.then_inc(s_mET, 1)

            def mix_3(t):
                pe.wait_ge(s_mEe, t + 1)
                for k in range(KD):
                    last = nc.tensor.matmul(pG[:, k * D:(k + 1) * D], En[:, k, :], xn, start=True, stop=True)
                last.then_inc(s_mG, 1)

            pe.wait_ge(s_mz, 16 * 4)
            pe.sem_inc(s_mG, 1)

            def pair_of_layer_1(g):
                mix_1(g)
                visits(0, g, 0)
                mix_2(g)
                visits(0, g, 1)
                mix_3(g)

            with pe.Fori(0, TILES) as g:
                pair_of_layer_1(g)

            pe.wait_ge(s_m3, 1)
            for c in range(KD):
                for k in range(KD):
                    last = nc.tensor.transpose(pT[:, k * D + c * P:k * D + (c + 1) * P], Gs[:, c, k * P:(k + 1) * P],
                                               ident[:, :])
            last.then_inc(s_m1, 1)
            for c in range(KD):
                for k in range(KD):
                    last = nc.tensor.transpose(pK[:, c * D + k * P:c * D + (k + 1) * P], Wq[:, k, c * P:(c + 1) * P],
                                               ident[:, :])
            last.then_inc(s_m1, 1)
            pe.wait_ge(s_m2, 1)
            for c in range(KD):
                for k in range(KD):
                    last = nc.tensor.matmul(pE[:, c * D:(c + 1) * D], GT[:, k, c * P:(c + 1) * P], Wv[:, k, :],
                                            start=(k == 0), stop=(k == KD - 1))
            last.then_inc(s_m1, 1)
            pe.wait_ge(s_m3, 3)
            for k in range(KD):
                for c in range(KD):
                    last = nc.tensor.matmul(pG[:, k * D:(k + 1) * D], WqT[:, c, k * P:(k + 1) * P], lam[:, c, :],
                                            start=(c == 0), stop=(c == KD - 1))
            last.then_inc(s_m1, 1)
            for c in range(KD):
                last = nc.tensor.matmul(pT[:, 0:D], bqb[:, c, :], lam[:, c, :], start=(c == 0), stop=(c == KD - 1))
            last.then_inc(s_m1, 1)

            with pe.Fori(TILES, PAIRS) as g:
                visits(0, g, 0)
                visits(0, g, 1)

            pe.wait_ge(s_mixed, 1)
            pe.wait_ge(s_fw, 32)

            def ff_1(t):
                pe.wait_ge(s_dxn, t + 1)
                pe.wait_ge(s_aggs, t + 1)
                nc.tensor.transpose(pT[:, 0:P], aggs, ident[:, :])
                for k in range(KD):
                    last = nc.tensor.transpose(pT[:, (k + 1) * P:(k + 2) * P], xnD[:, k * P:(k + 1) * P], ident[:, :])
                last.then_inc(s_dT, 1)
                pe.wait_ge(s_dTe, t + 1)
                nc.tensor.matmul(pY1[:, 0:D], T3[:, 0, :], gW2[:, :], start=True, stop=False)
                for k in range(KD):
                    last = nc.tensor.matmul(pY1[:, 0:D], T3[:, k + 1, :], Pmix[:, k, :], start=False,
                                            stop=(k == KD - 1))
                last.then_inc(s_y1, 1)

            def ff_2(t):
                pe.wait_ge(s_ln, t + 1)
                for k in range(KD):
                    last = nc.tensor.transpose(pT[:, k * P:(k + 1) * P], ln[:, k * P:(k + 1) * P], ident[:, :])
                last.then_inc(s_lT, 1)
                pe.wait_ge(s_lTe, t + 1)
                for h in range(KH):
                    for k in range(KD):
                        last = nc.tensor.matmul(pH[h // 4][:, (h % 4) * P:(h % 4 + 1) * P],
                                                fw1[:, k, h * P:(h + 1) * P], T3[:, k, :],
                                                start=(k == 0), stop=(k == KD - 1))
                last.then_inc(s_h, 1)

            def ff_3(t):
                pe.wait_ge(s_H, t + 1)
                for h in range(KH):
                    last = nc.tensor.matmul(pY[:, 0:D], H[:, h, :], fw2[:, h, :], start=(h == 0), stop=(h == KH - 1))
                last.then_inc(s_y, 1)

            with pe.Fori(0, PAIRS) as g:
                t0, t1 = read_released(pe, g)
                with pe.If(t1 > t0):
                    ff_1(t0)
                visits(1, g, 0)
                with pe.If(t1 > t0):
                    ff_2(t0)
                visits(1, g, 1)
                with pe.If(t1 > t0):
                    ff_3(t0)
            tend, _unused = read_released(pe, PAIRS - 1) if False else (
                pe.value_load(released[0:1, PAIRS:PAIRS + 1], min_val=0, max_val=TILES - 1), None)
            with pe.Fori(tend, TILES) as t:
                ff_1(t)
                ff_2(t)
                ff_3(t)

            pe.wait_ge(s_sel, 2)
            for i in range(32):
                pe.wait_ge(s_sel, 4 + 4 * i)
                nc.tensor.matmul(bank[2][:, 0:1], ones_m, sm[:, 50:51], start=True, stop=True).then_inc(s_cnt, 1)
            pe.wait_ge(s_sel, 2 + 4 * 32 + 3)
            nc.tensor.matmul(bank[2][:, 0:TILES], ones_m, eq, start=True, stop=True)
            nc.tensor.matmul(bank[3][:, 0:TILES], lower, eq, start=True, stop=True)
            nc.tensor.matmul(bank[4][:, 0:1], ones_m, sm[:, 51:52], start=True, stop=True).then_inc(s_cnt, 1)

        @block.vector
        def _(dve):
            steps = [0]

            def link(ins):
                steps[0] += 1
                ins.then_inc(s_dve, 1)
                dve.wait_ge(s_dve, steps[0])

            dve.memset(epscol[:, :], EPS)
            dve.wait_ge(s_edges, 16 * 4)
            dve.tensor_copy(dst_rows[0:PAIRS, :], dst_rows_i[0:PAIRS, :]).then_inc(s_rowsf, 1)
            dve.wait_ge(s_rowsf, 1)
            dve.tensor_copy(src_rows[0:PAIRS, :], src_rows_i[0:PAIRS, :]).then_inc(s_rowsf, 1)
            halves = dst_rows[0:PAIRS, :].rearrange("p (h e) -> p h e", h=2)
            dve.tensor_reduce(rng[0:PAIRS, 0:2], halves, AX.X, ALU.min)
            link(dve.tensor_reduce(rng[0:PAIRS, 2:4], halves, AX.X, ALU.max))
            link(dve.tensor_copy(rng_i[0:PAIRS, :], rng[0:PAIRS, :]))
            link(dve.tensor_scalar(rng_i[0:PAIRS, :], rng_i[0:PAIRS, :], 7, None, ALU.arith_shift_right))
            dve.tensor_copy(rng[0:PAIRS, :], rng_i[0:PAIRS, :]).then_inc(s_rngdone, 1)
            dve.wait_ge(s_rngT, 1)
            lo_r, hi_r, cnt_r, zero_r, vin_r = (rrow[:, i, :] for i in range(5))
            m_r, done_r, one_r = rrow[:, 5, 0:PAIRS], rrow[:, 6, 0:PAIRS], rrow[:, 7, 0:PAIRS]
            rel_r = rrow[:, 7, PAIRS:2 * PAIRS]
            for h in range(2):
                dve.tensor_copy(lo_r.rearrange("p (g h) -> p g h", h=2)[:, :, h], bank[6][0:1, h * P:h * P + PAIRS])
                link(dve.tensor_copy(hi_r.rearrange("p (g h) -> p g h", h=2)[:, :, h],
                                     bank[6][0:1, (2 + h) * P:(2 + h) * P + PAIRS]))
            dve.memset(zero_r, 0.0)
            dve.memset(one_r, 1.0)
            link(dve.scalar_tensor_tensor(cnt_r, hi_r, 1.0, lo_r, ALU.add, ALU.subtract))
            link(dve.tensor_tensor_scan(vin_r, cnt_r, zero_r, 0.0, ALU.add, ALU.add))
            lo2 = lo_r.rearrange("p (g h) -> p g h", h=2)
            link(dve.tensor_tensor(m_r, lo2[:, :, 0], lo2[:, :, 1], ALU.min))
            link(dve.tensor_tensor_scan(done_r[:, ::-1], m_r[:, ::-1], m_r[:, ::-1], 1e9, ALU.min, ALU.min))
            link(dve.tensor_tensor_scan(rel_r, one_r, done_r, 0.0, ALU.add, ALU.min))
            cview = ctl[:, :, :].rearrange("p g (h c) -> p g h c", h=2)
            dve.tensor_copy(cview[:, :, :, 0], lo2)
            dve.tensor_scalar(cview[:, :, :, 1], hi_r.rearrange("p (g h) -> p g h", h=2), 1.0, None, ALU.add)
            link(dve.tensor_tensor(vin_r, vin_r, cnt_r, ALU.subtract))
            link(dve.tensor_scalar(vin_r, vin_r, float(TILES), None, ALU.add))
            dve.tensor_tensor(cview[:, :, :, 2], vin_r.rearrange("p (g h) -> p g h", h=2), lo2, ALU.subtract)
            dve.memset(released[:, 0:1], 0)
            dve.tensor_copy(released[:, 1:PAIRS + 1], rel_r).then_inc(s_ctl, 1)

            dve.wait_ge(s_xtail, 16)

            def stats_of_group(g):
                dve.wait_ge(s_x, g * 16 + 16)
                for j in range(GROUP):
                    last = dve.bn_stats(statsA[:, j, :],
                                        xs[:, ds(g * GROUP + j, 1), :].rearrange("p a d -> p (a d)"))
                last.then_inc(s_bn, 1)
                dve.wait_ge(s_bn, g * 3 + 1)
                me, se, mo, so = (statsA[:, :, i] for i in (1, 2, 4, 5))
                dve.tensor_tensor(mean2[:, :], me, mo, ALU.add)
                dve.tensor_tensor(ssq[:, :], se, so, ALU.add)
                dve.tensor_tensor(dif[:, :], me, mo, ALU.subtract).then_inc(s_bn, 1)
                dve.wait_ge(s_bn, g * 3 + 2)
                dve.scalar_tensor_tensor(dif[:, :], dif[:, :], float(D) / 4, dif[:, :], ALU.mult, ALU.mult)\
                   .then_inc(s_bn, 1)
                dve.wait_ge(s_bn, g * 3 + 3)
                dve.tensor_tensor(ssq[:, :], ssq[:, :], dif[:, :], ALU.add).then_inc(s_mvA, 1)
                dve.wait_ge(s_sdA, g + 1)
                gs = ds(g * GROUP, GROUP)
                dve.reciprocal(rstd[:, gs], rstd[:, gs]).then_inc(s_drel[0], 1)
                dve.wait_ge(s_drel[0], g + 1)
                dve.scalar_tensor_tensor(nmr[:, gs], mean2[:, :], -0.5, rstd[:, gs],
                                         ALU.mult, ALU.mult).then_inc(s_rstd, 1)

            with dve.Fori(0, GROUPS) as g:
                stats_of_group(g)

            dve.wait_ge(s_eTe, 4)
            r_i, q_i = r_of.bitcast(i32), q_of.bitcast(i32)
            link(dve.tensor_copy(r_i, dst_of[:, :]))
            link(dve.tensor_scalar(q_i, r_i, 7, None, ALU.arith_shift_right))
            link(dve.tensor_scalar(r_i, r_i, 127, None, ALU.bitwise_and))
            link(dve.tensor_copy(q_of, q_i))
            link(dve.tensor_copy(r_of, r_i))
            dve.wait_ge(s_const, 4)

            def one_hots(gg, first):
                for par in range(2):
                    if not first:
                        dve.wait_ge(s_ohu, gg * 2 + par - 1)
                    for c in range(PAIR):
                        col = ds(gg * (2 * PAIR) + (par * PAIR + c), 1)
                        dve.tensor_scalar(oh_r[:, par, c, :], iota_n[:, :], r_of[:, col], None, ALU.is_equal)
                        last = dve.tensor_scalar(oh_q[:, par, c, :], iota_n[:, 0:TILES], q_of[:, col], None,
                                                 ALU.is_equal)
                    last.then_inc(s_oh, 1)

            one_hots(0, True)
            with dve.Fori(1, PAIRS // 2) as gg:
                one_hots(gg, False)
            dve.wait_ge(s_sq, 1)
            link(dve.reciprocal(dinv[:, :], dinv[:, :]))
            dve.wait_ge(s_hAe, TILES)
            for g in range(GROUPS):
                gs = slice(g * GROUP, (g + 1) * GROUP)
                dve.tensor_tensor(acc[:, gs, :], acc[:, gs, :],
                                  bc(dinv[:, gs].rearrange("p (t a) -> p t a", a=1), [P, GROUP, F]),
                                  ALU.mult).then_inc(s_scaled, 1)
            dve.wait_ge(s_eTe, 8)
            dve.tensor_copy(idx_now[:, 0, :], src_idx[:, 0:PAIR]).then_inc(s_idx, 1)
            dve.memset(sm[:, 16:18], -3.0e38)
            dve.memset(sm[:, 18:20], 0.0)
            link(dve.memset(Gs, 0.0))
            dve.wait_ge(s_tab1, 16 * GROUPS)
            for layer in range(2):
                for q in range(2):
                    dve.sem_inc(s_Su[layer][q], TILES + 1)
                    dve.sem_inc(s_S[layer][q], TILES)
                dve.sem_inc(s_sum[layer], TILES)
                dve.sem_inc(s_drel[layer], TILES)
                dve.sem_inc(s_fl[layer], TILES + 1)
                dve.sem_inc(s_free[layer], 2)
            GROUPS_DONE = GROUPS

            def visits(layer, g, h):
                lo, hi, v0 = read_ctl(dve, g, h)
                done = GROUPS_DONE if layer == 0 else 0
                with dve.Fori(lo, hi) as t:
                    v = v0 + t
                    dve.tensor_scalar(drel[:, :], dst_of[:, ds(g * PAIR + h * HALF, HALF)], tile_base[:, ds(t, 1)], None,
                                      ALU.subtract).then_inc(s_drel[layer], 1)
                    dve.wait_ge(s_drel[layer], v + (done + 1))
                    for q in range(2):
                        if q == 0:
                            dve.wait_ge(s_Su[layer][0], v + 1)
                        else:
                            dve.wait_ge(s_fl[layer], v + 1)
                        dve.tensor_tensor(S[:, 4 * q:4 * q + 4, :],
                                          bc(iota_n[:, :].rearrange("p (a n) -> p a n", a=1), [P, 4, P]),
                                          bc(drel[:, 4 * q:4 * q + 4].rearrange("p (c a) -> p c a", a=1), [P, 4, P]),
                                          ALU.is_equal).then_inc(s_S[layer][q], 1)
                    dve.wait_ge(s_sum[layer], v + 1)
                    a = acc[:, ds(t, 1), :].rearrange("p a f -> p (a f)")
                    dve.tensor_tensor(a, visit_sum[h][:, 0:F], a, ALU.add).then_inc(s_fl[layer], 1)
                dve.sem_inc(s_free[layer], 1)

            def next_indices(g):
                dve.tensor_copy(idx_now[:, ds((g + 1) % 2, 1), :].rearrange("p a c -> p (a c)"),
                                src_idx[:, ds(g * PAIR + PAIR, PAIR)]).then_inc(s_idx, 1)

            def finish_layer_1(t):
                a = acc[:, ds(t, 1), :].rearrange("p a f -> p (a f)")
                di = dinv[:, ds(t, 1)]
                dve.scalar_tensor_tensor(a, a, di, b1row[:, :], ALU.mult, ALU.add).then_inc(s_fin0, 1)
                dve.wait_ge(s_fin0, t + 1)
                dve.tensor_scalar(a, a, 0.0, di, ALU.max, ALU.mult).then_inc(s_fin, 1)

            def mix_1(t, n):
                k = [0]

                def step(ins):
                    k[0] += 1
                    ins.then_inc(s_mch, 1)
                    dve.wait_ge(s_mch, t * 5 + k[0])

                dve.wait_ge(s_mK, t + 1)
                step(dve.tensor_reduce(sm[:, 28:30], pK[:, 0:D].rearrange("p (k n) -> p k n", k=KD)[:, :, 0:n], AX.X,
                                       ALU.max))
                step(dve.tensor_tensor(sm[:, 28:30], sm[:, 28:30], sm[:, 14:16], ALU.add))
                step(dve.tensor_tensor(sm[:, 30:32], sm[:, 28:30], sm[:, 16:18], ALU.max))
                dve.tensor_tensor(sm[:, 20:22], sm[:, 16:18], sm[:, 30:32], ALU.subtract)
                step(dve.tensor_tensor(sm[:, 24:26], sm[:, 14:16], sm[:, 30:32], ALU.subtract))
                step(dve.tensor_copy(sm[:, 16:18], sm[:, 30:32]))
                dve.sem_inc(s_mb, 1)

            def mix_3(t):
                dve.wait_ge(s_mE, t + 1)
                dve.tensor_tensor(sm[:, 18:20], sm[:, 18:20], sm[:, 22:24], ALU.mult).then_inc(s_mch2, 1)
                dve.wait_ge(s_mch2, t + 1)
                dve.tensor_tensor(sm[:, 18:20], sm[:, 18:20], sm[:, 26:28], ALU.add)
                dve.wait_ge(s_mG, t + 2)
                for k in range(KD):
                    last = dve.scalar_tensor_tensor(Gs[:, k, :], Gs[:, k, :], sm[:, 22 + k:23 + k],
                                                    pG[:, k * D:(k + 1) * D], ALU.mult, ALU.add)
                last.then_inc(s_mu, 1)

            def pair_of_layer_1(g, n):
                if n is not None:
                    mix_1(g, n)
                next_indices(g)
                visits(0, g, 0)
                t0, t1 = read_released(dve, g)
                with dve.If(t1 > t0):
                    finish_layer_1(t0)
                visits(0, g, 1)
                if n is not None:
                    mix_3(g)

            with dve.Fori(0, TILES - 1) as g:
                pair_of_layer_1(g, P)
            dve.memset(ET[:, :, LAST:P], 0.0)
            with dve.Fori(TILES - 1, TILES) as g:
                pair_of_layer_1(g, LAST)

            dve.wait_ge(s_mu, TILES)
            link(dve.reciprocal(sm[:, 18:20], sm[:, 18:20]))
            for c in range(KD):
                last = dve.tensor_scalar(Gs[:, c, :], Gs[:, c, :], sm[:, 18 + c:19 + c], None, ALU.mult)
            last.then_inc(s_m3, 1)
            dve.tensor_copy(bqb, bc(sm[:, 12:14].rearrange("p (k a) -> p k a", a=1), [P, KD, P]))
            dve.wait_ge(s_m1, 3)
            link(dve.tensor_tensor(lam, pE[:, :].rearrange("p (c d) -> p c d", c=KD),
                                   bc(bvrow.rearrange("p (a d) -> p a d", a=1), [P, KD, D]), ALU.add))
            for c in range(KD):
                link(dve.bn_stats(stats2[:, c, :], lam[:, c, :]))
                link(dve.bn_aggr(mv[:, :], stats2[:, c, :]))
                dve.tensor_copy(sm[:, 36 + c:37 + c], mv[:, 0:1])
                link(dve.tensor_copy(sm[:, 32 + c:33 + c], mv[:, 1:2]))
            dve.sem_inc(s_m3, 1)
            dve.wait_ge(s_m2, 3)
            link(dve.reciprocal(sm[:, 34:36], sm[:, 34:36]))
            link(dve.tensor_tensor(sm[:, 34:36], sm[:, 34:36], sm[:, 8:10], ALU.mult))
            link(dve.tensor_tensor(sm[:, 36:38], sm[:, 36:38], sm[:, 34:36], ALU.mult))
            link(dve.tensor_tensor(sm[:, 36:38], sm[:, 10:12], sm[:, 36:38], ALU.subtract))
            for c in range(KD):
                last = dve.tensor_scalar(lam[:, c, :], lam[:, c, :], sm[:, 34 + c:35 + c], sm[:, 36 + c:37 + c],
                                         ALU.mult, ALU.add)
            last.then_inc(s_m3, 1)
            dve.wait_ge(s_m1, 5)
            dve.wait_ge(s_m2, 4)
            dve.tensor_tensor(crow[:, :], crow[:, :], pT[:, 0:D], ALU.add).then_inc(s_mixed, 1)

            with dve.Fori(TILES, PAIRS) as g:
                pair_of_layer_1(g, None)
            tend = dve.value_load(released[0:1, PAIRS:PAIRS + 1], min_val=0, max_val=TILES - 1)
            with dve.Fori(tend, TILES) as t:
                finish_layer_1(t)

            dve.tensor_copy(idx_now[:, 0, :], src_idx[:, 0:PAIR]).then_inc(s_idx, 1)
            dve.wait_ge(s_tab2, 16 * TILES)

            class Chain:
                PER = 8

                def __init__(self):
                    self.k = 0

                def step(self, t, ins):
                    self.k += 1
                    assert self.k <= Chain.PER
                    ins.then_inc(s_dch, 1)
                    dve.wait_ge(s_dch, t * Chain.PER + self.k)

            def ff_1(t, ch):
                ch.step(t, dve.tensor_scalar(aggs, acc[:, ds(t, 1), :].rearrange("p a f -> p (a f)"), dinv[:, ds(t, 1)],
                                             None, ALU.mult))
                dve.sem_inc(s_aggs, 1)
                ch.step(t, dve.tensor_tensor(x1, xs[:, ds(t, 1), :].rearrange("p a f -> p (a f)"), crow[:, :],
                                             ALU.add))
                dve.wait_ge(s_y1, t + 1)
                ch.step(t, dve.tensor_tensor(x1, x1, pY1[:, 0:D], ALU.add))
                ch.step(t, dve.bn_stats(stats[:, :], x1))
                dve.sem_inc(s_passed, 1)
                dve.bn_aggr(mv[:, :], stats[:, :]).then_inc(s_var, 1)
                dve.wait_ge(s_sd, t + 1)
                ch.step(t, dve.reciprocal(sm[:, 41:42], sm[:, 40:41]))
                dve.tensor_scalar(ln, x1, mv[:, 0:1], sm[:, 41:42], ALU.subtract, ALU.mult).then_inc(s_ln, 1)
                dve.wait_ge(s_ln, t + 1)
                dve.wait_ge(s_basew, t * 16 + 16)
                dve.tensor_tensor(base, x1, ln, ALU.add).then_inc(s_base, 1)
                dve.wait_ge(s_base, t + 1)
                ch.step(t, dve.tensor_tensor_reduce(out=x1, in0=ln, in1=wrrow[:, :], scale=1.0, scalar=0.0,
                                                    op0=ALU.mult, op1=ALU.add, accum_out=sm[:, 42:43]))
                ch.step(t, dve.tensor_tensor(sm[:, 43:44], sm[:, 42:43], brcol[:, :], ALU.add))
                dve.tensor_copy(wts[:, ds(t, 1)], sm[:, 43:44])

            def ff_3(t, ch):
                dve.wait_ge(s_y, t + 1)
                ch.step(t, dve.tensor_tensor(x1, pY[:, 0:D], fb2row[:, :], ALU.add))
                assert ch.k == Chain.PER
                dve.tensor_scalar(xs[:, ds(t, 1), :].rearrange("p a f -> p (a f)"), x1, sm[:, 43:44], None,
                                  ALU.mult).then_inc(s_wd, 1)

            with dve.Fori(0, PAIRS) as g:
                t0, t1 = read_released(dve, g)
                ch = Chain()
                with dve.If(t1 > t0):
                    ff_1(t0, ch)
                next_indices(g)
                visits(1, g, 0)
                visits(1, g, 1)
                with dve.If(t1 > t0):
                    ff_3(t0, ch)
            tend = dve.value_load(released[0:1, PAIRS:PAIRS + 1], min_val=0, max_val=TILES - 1)
            with dve.Fori(tend, TILES) as t:
                ch = Chain()
                ff_1(t, ch)
                ff_3(t, ch)

            n_sel = [0]

            def sel(ins):
                n_sel[0] += 1
                ins.then_inc(s_sel, 1)
                dve.wait_ge(s_sel, n_sel[0])

            key, cand, bits, msk = (sb_i for sb_i in (
                sm[:, 52:53].bitcast(i32), sm[:, 53:54].bitcast(i32), sm[:, 54:55].bitcast(i32),
                sm[:, 55:56].bitcast(i32)))
            dve.wait_ge(s_wd, TILES)
            dve.memset(ones_m, 1.0)
            dve.memset(zer, 0.0)
            dve.tensor_scalar(sm[:, 56:57], tile_base[:, TILES - 1:TILES], 0.0, None, ALU.mult)
            link(dve.tensor_copy(lower, ident[:, :]))
            link(dve.tensor_tensor_scan(lower, ident[:, :], bc(zer[:, 0:1], [P, P]), 0.0, ALU.add, ALU.add))
            link(dve.tensor_tensor(lower, lower, ident[:, :], ALU.subtract))
            link(dve.tensor_scalar(sm[:, 57:58], lower[:, LAST:LAST + 1], 1.0, 3.0e38, ALU.subtract, ALU.mult))
            link(dve.tensor_tensor(wts[:, TILES - 1:TILES], wts[:, TILES - 1:TILES], lower[:, LAST:LAST + 1], ALU.mult))
            sel(dve.tensor_tensor(wts[:, TILES - 1:TILES], wts[:, TILES - 1:TILES], sm[:, 57:58], ALU.add))
            sel(dve.memset(key, 0))
            for i in range(32):
                b = 31 - i
                bit = (1 << b) if b < 31 else -(1 << 31)
                link(dve.tensor_scalar(cand, key, bit, None, ALU.bitwise_or))
                link(dve.tensor_scalar(msk, cand, 31, None, ALU.arith_shift_right))
                link(dve.tensor_scalar(msk, msk, 0x7FFFFFFF, -1, ALU.bitwise_and, ALU.bitwise_xor))
                sel(dve.tensor_tensor(bits, cand, msk, ALU.bitwise_xor))
                sel(dve.tensor_scalar(cmp_, wts[:, :], bits.bitcast(f32), 0.0, ALU.is_ge, ALU.add,
                                      accum_out=sm[:, 50:51]))
                dve.wait_ge(s_cnt, i + 1)
                sel(dve.tensor_scalar(sm[:, 58:59], bank[2][:, 0:1], float(KSEL), None, ALU.is_ge))
                link(dve.tensor_scalar(msk, sm[:, 58:59], -1.0, None, ALU.mult))
                link(dve.tensor_scalar(msk, msk, bit, None, ALU.bitwise_and))
                sel(dve.tensor_tensor(key, key, msk, ALU.bitwise_or))
            link(dve.tensor_scalar(msk, key, 31, None, ALU.arith_shift_right))
            link(dve.tensor_scalar(msk, msk, 0x7FFFFFFF, -1, ALU.bitwise_and, ALU.bitwise_xor))
            link(dve.tensor_tensor(bits, key, msk, ALU.bitwise_xor))
            thr = bits.bitcast(f32)
            sel(dve.tensor_scalar(gt, wts[:, :], thr, 0.0, ALU.is_gt, ALU.add, accum_out=sm[:, 51:52]))
            sel(dve.tensor_scalar(eq, wts[:, :], thr, None, ALU.is_equal))
            sel(dve.memset(colsum, 0.0))
            dve.wait_ge(s_cnt, 33)
            link(dve.tensor_copy(colsum, bank[2][:, 0:TILES]))
            link(dve.tensor_tensor_scan(before, colsum, zer, 0.0, ALU.add, ALU.add))
            link(dve.tensor_tensor(before, before, colsum, ALU.subtract))
            link(dve.tensor_tensor(before, before, bank[3][:, 0:TILES], ALU.add))
            link(dve.tensor_scalar(sm[:, 59:60], bank[4][:, 0:1], -1.0, float(KSEL), ALU.mult, ALU.add))
            link(dve.scalar_tensor_tensor(selw, before, sm[:, 59:60], eq, ALU.is_lt, ALU.mult))
            link(dve.tensor_tensor(selw, selw, gt, ALU.add))
            for i in range(STEPS):
                dve.wait_ge(s_tl[i % SLOTS], 16 * (i // SLOTS + 1))
                for j in range(HG):
                    t = i * HG + j
                    last = dve.scalar_tensor_tensor(tail[:, i % SLOTS, j, :], xs[:, t, :], selw[:, t:t + 1],
                                                    tail[:, i % SLOTS, j, :], ALU.mult, ALU.add)
                last.then_inc(s_tf, 1)


_INS = ['x', 'src', 'dst', 'L0_gnn_W1', 'L0_gnn_b1', 'L0_gnn_W2', 'L0_gnn_b2', 'L0_mix_W_qk', 'L0_mix_b_qk',
        'L0_mix_W_v', 'L0_mix_b_v', 'L0_mix_gamma', 'L0_mix_beta', 'L0_ffn_attention_mask', 'L0_ffn_wr', 'L0_ffn_br',
        'L0_ffn_w1', 'L0_ffn_b1', 'L0_ffn_w2', 'L0_ffn_b2']
_OUTS = [((12500, 256), 'float32')]


def kernel(**inputs):
    import numpy as _np
    import concourse.bacc as _bacc
    from concourse import mybir as _mybir
    from concourse.bass_utils import run_bass_kernel_spmd as _run

    nc = _bacc.Bacc("TRN2", target_bir_lowering=False, num_devices=1, dynamic_dma_scratch_size=8192)
    arrays, args = {}, []
    for name in _INS:
        a = _np.ascontiguousarray(inputs[name])
        arrays[f"in_{name}_dram"] = a
        args.append(nc.dram_tensor(f"in_{name}_dram", a.shape, _mybir.dt.from_np(a.dtype), kind="ExternalInput").ap())
    for i, (shape, dtype) in enumerate(_OUTS):
        dt = _mybir.dt.from_np(_np.dtype(dtype))
        args.append(nc.dram_tensor(f"out_{i}_dram", shape, dt, kind="ExternalOutput").ap())
    gps_layer_kernel(nc, *args)
    r = _run(nc, [arrays], core_ids=[0])
    got = tuple(r.results[0][f"out_{i}_dram"] for i in range(len(_OUTS)))
    return got[0]
```

```python
import concourse.bass as bass
from concourse import mybir
from contextlib import ExitStack
import math


def gps_layer_kernel(nc, x, src, dst, W1, b1, W2, b2, W_qk, b_qk, W_v, b_v, gamma, beta, attention_mask, wr, br,
                     w1, fb1, w2, fb2, out):
    f32, bf16, i32, i16 = mybir.dt.float32, mybir.dt.bfloat16, mybir.dt.int32, mybir.dt.int16
    ALU, ACT, AX = mybir.AluOpType, mybir.ActivationFunctionType, mybir.AxisListType
    ds = bass.ds

    P = 128
    N, D = x.shape
    F = W1.shape[1]
    HID = w1.shape[1]
    E = src.shape[0]
    TILES = math.ceil(N / P)
    LAST = N - (TILES - 1) * P
    KD, KH = D // P, HID // P
    HALF = 8
    PAIR = 2 * HALF
    PAIRS = 4 * math.ceil(math.ceil(E / (PAIR * P)) / 4)
    WIN = 4
    SETS = 4
    ROW = PAIR * P
    CHUNKS = PAIRS * PAIR
    EDGES_IN_LAST = E - (PAIRS - 1) * ROW
    PAD_NODE = TILES * P - 1
    GROUP = 14
    GROUPS = TILES // GROUP
    KSEL = max(1, int(0.5 * N)) - 1
    EPS = 1e-5
    assert D == KD * P and F == P and HID == KH * P and GROUPS * GROUP == TILES and PAIRS <= P
    assert 0 < EDGES_IN_LAST <= ROW and PAD_NODE >= N

    ctx = ExitStack()
    with ctx:
        def sb(name, shape, dt=f32):
            return ctx.enter_context(nc.sbuf_tensor(name, shape, dt))

        def sem(name):
            return ctx.enter_context(nc.semaphore(name))

        table = [nc.dram_tensor(f"table{i}", [TILES * P, F], f32).ap() for i in range(2)]
        base_rows = nc.dram_tensor("base_rows", [TILES * P, D], f32).ap()

        xs = sb("xs", [P, TILES, D])
        acc = sb("acc", [P, TILES, F])
        src_idx = sb("src_idx", [P, CHUNKS + 2 * PAIR], i16)
        dst_of = sb("dst_of", [P, CHUNKS], i16)
        idx_now = sb("idx_now", [P, SETS, PAIR], i32)
        ident = sb("ident", [P, P])
        iota_n = sb("iota_n", [P, P])
        tile_base = sb("tile_base", [P, TILES])
        rstd = sb("rstd", [P, TILES])
        nmr = sb("nmr", [P, TILES])
        dinv = sb("dinv", [P, TILES])
        wts = sb("wts", [P, TILES])
        ctl = sb("ctl", [1, PAIRS + 1, 4], i32)
        gW1 = sb("gW1", [P, KD, F])
        gW2 = sb("gW2", [P, D])
        Pmix = sb("Pmix", [P, KD, D])
        crow = sb("crow", [P, D])
        b1row = sb("b1row", [P, F])
        wrrow = sb("wrrow", [P, D])
        fb2row = sb("fb2row", [P, D])
        fb1col = sb("fb1col", [P, KH])
        brcol = sb("brcol", [P, 1])
        wide = sb("wide", [1, 1], i32)
        epscol = sb("epscol", [P, 1])
        drel = sb("drel", [P, 2, HALF])
        sm = sb("sm", [P, 64])

        ARENA = 12160
        arena = sb("arena", [P, ARENA])
        at = [0]

        def carve(*dims, dt=f32, start=None):
            if start is not None:
                at[0] = start
            n = math.prod(dims)
            words = n if dt != bf16 else n // 2
            v = arena[:, at[0]:at[0] + words]
            at[0] += words
            assert at[0] <= ARENA, at[0]
            if dt != f32:
                v = v.bitcast(dt)
            names = " ".join("abcd"[:len(dims)])
            sizes = {"abcd"[i]: dims[i] for i in range(len(dims))}
            return v if len(dims) == 1 else v.rearrange(f"p ({names}) -> p {names}", **sizes)

        oh_r = carve(2, PAIR, P, dt=bf16, start=0)
        oh_q = carve(2, PAIR, TILES, dt=bf16)
        r_of = carve(CHUNKS)
        q_of = carve(CHUNKS)
        q_rel = carve(CHUNKS)
        xnA = carve(2, D)
        xTA = carve(2, D)
        ident_b = carve(P, dt=bf16)
        zeros_b = carve(TILES + WIN, dt=bf16)
        ones_row = carve(P)[0:1, :]
        ring = carve(2 * PAIR, F, start=0)
        S = carve(2, HALF, P)
        after_S = at[0]
        Wk = carve(KD, D)
        Wv = carve(KD, D)
        Wq = carve(KD, D)
        WqT = carve(KD, D)
        xn = carve(D)
        xT = carve(KD, P)
        ET = carve(KD, P)
        En = carve(KD, P)
        Gs = carve(KD, D)
        GT = carve(KD, D)
        lam = carve(KD, D)
        bvrow = carve(D)
        bqb = carve(KD, P)
        fw1 = carve(KD, HID, start=after_S)
        fw2 = carve(KH, D)
        xnD = gW1[:, :, :].rearrange("p k f -> p (k f)")
        x1 = carve(D)
        ln = carve(D)
        base = carve(D)
        aggs = carve(F)
        H = carve(KH, P)
        T3 = H[:, KH - 3:KH, :]
        ones_m = carve(P, start=0)
        lower = carve(P)
        cmp_ = carve(TILES)
        gt = carve(TILES)
        eq = carve(TILES)
        colsum = carve(TILES)
        BITS = 3
        CAND = (1 << BITS) - 1
        ROUNDS = [(b, min(BITS, 31 - b)) for b in range(0, 31, BITS)][::-1]
        part = carve(CAND)
        cand = carve(CAND)
        steps_of = carve(len(ROUNDS), CAND)
        reach = carve(CAND, TILES)
        ws = carve(TILES)
        before = carve(TILES)
        selw = carve(TILES)
        zer = carve(TILES)
        accf = acc[:, :, :].rearrange("p t f -> p (t f)")
        src_rows_i = accf[:, 0:ROW].bitcast(i32)
        src_rows = accf[:, ROW:2 * ROW]
        dst_rows_i = accf[:, 2 * ROW:3 * ROW].bitcast(i32)
        dst_rows = accf[:, 3 * ROW:4 * ROW]
        HG = GROUP // 2
        STEPS = TILES // HG
        SLOTS = TILES * F // (HG * D)
        tail = accf.rearrange("p (s j d) -> p s j d", s=SLOTS, j=HG)
        rng = sm[:, 0:4]
        rng_i = sb("rng_i", [P, 4], i32)
        rrow = accf[0:1, 4 * ROW:4 * ROW + 20 * PAIRS].rearrange("p (r n) -> p r n", r=10)
        low_row = rrow[:, 0, :]
        low_of = carve(2 * PAIRS, start=ARENA - 2 * PAIRS)
        stats = sb("stats", [P, 6])
        stats2 = sb("stats2", [P, 2, 6])
        mv = sb("mv", [P, 2])
        statsA = sb("statsA", [P, GROUP, 6])
        mean2 = sb("mean2", [P, GROUP])
        ssq = sb("ssq", [P, GROUP])
        dif = sb("dif", [P, GROUP])

        bank = [ctx.enter_context(nc.psum_tensor(f"bank{i}", [P, 512], f32)) for i in range(8)]
        visit_sum = [bank[0], bank[1]]
        pT, pK, pE, pG = bank[2], bank[3], bank[4], bank[5]
        pY1, pY = bank[3], bank[4]
        pH = [bank[5], bank[6]]
        pDeg = bank[7]

        s_tail_zero = sem("x_tail_zeroed")
        s_xtail = sem("x_tail_loaded")
        s_x = sem("x_group_loaded")
        s_pad = sem("edge_padding_set")
        s_edges = sem("edges_loaded")
        s_small = sem("small_inputs_loaded")
        s_const = sem("constants_made")
        s_rowsf = sem("edge_rows_as_float")
        s_eT = sem("edges_transposed")
        s_eTe = sem("transposed_edges_evacuated")
        s_rngdone = sem("ranges_ready")
        s_rngT = sem("ranges_transposed")
        s_rcpA = sem("x_reciprocal_chain")
        s_mvA = sem("x_stats_ready")
        s_sdA = sem("x_deviation_ready")
        s_rstd = sem("x_rstd_ready")
        s_xnA = sem("xn_ready_first_pass")
        s_TA = sem("xn_transposed_first_pass")
        s_TAe = sem("xnT_evacuated_first_pass")
        s_hA = sem("h1_ready")
        s_hAe = sem("h1_evacuated")
        s_oh = sem("one_hots_ready")
        s_ohu = sem("one_hots_used")
        s_zero = sem("zeros_made")
        s_deg = sem("degrees_summed")
        s_low = sem("first_tiles_broadcast")
        s_sq = sem("sqrt_degrees_ready")
        s_scaled = sem("table1_tiles_ready")
        s_tab1 = sem("table1_written")
        s_ctl = sem("control_table_ready")
        s_idx = [sem(f"indices_ready{i}") for i in range(2)]
        s_issue = sem("gathers_issued")
        s_dve = sem("vector_chain")
        s_bn = sem("x_stats_chain")
        s_passed_sp = sem("group_waits_passed")
        s_passed = sem("waits_passed")
        s_free = [sem(f"ring_half_free{i}") for i in range(2)]
        s_gath = [[sem(f"gathered{i}_{h}") for h in range(4)] for i in range(2)]
        s_drel = [[sem(f"relative_dst{i}_{h}") for h in range(2)] for i in range(2)]
        s_S = [[[sem(f"S_ready{i}_{h}_{q}") for q in range(2)] for h in range(2)] for i in range(2)]
        s_Su = [[sem(f"S_half_free{i}_{h}") for h in range(2)] for i in range(2)]
        s_sum = [[sem(f"visit_summed{i}_{h}") for h in range(2)] for i in range(2)]
        s_fl = [[sem(f"visits_added{i}_{h}") for h in range(2)] for i in range(2)]
        s_fin = sem("table2_tile_ready")
        s_fin0 = sem("table2_tile_biased")
        s_tab2 = sem("table2_written")
        s_mxn = sem("mix_xn_ready")
        s_mT = sem("mix_xn_transposed")
        s_mTe = sem("mix_xnT_evacuated")
        s_mK = sem("mix_keys_ready")
        s_mch = sem("mix_max_chain")
        s_mb = sem("mix_bias_ready")
        s_mE = sem("mix_exps_ready")
        s_mET = sem("mix_exps_transposed")
        s_mEe = sem("mix_exps_evacuated")
        s_mG = sem("mix_sums_ready")
        s_mu = sem("mix_sums_added")
        s_mch2 = sem("mix_sum_chain")
        s_mz = sem("mix_weights_loaded")
        s_m1, s_m2, s_m3 = sem("lambda_pe"), sem("lambda_evacuated"), sem("lambda_dve")
        s_mixed = sem("mixer_folded")
        s_fw = sem("ff_weights_loaded")
        s_aggs = sem("agg_scaled")
        s_dxn = sem("ff_xn_ready")
        s_dT = sem("ff_first_transposed")
        s_dTe = sem("ff_first_evacuated")
        s_y1 = sem("mixed_rows_ready")
        s_dch = sem("ff_vector_chain")
        s_var = sem("ff_variance_ready")
        s_sd = sem("ff_deviation_ready")
        s_ln = sem("ff_ln_ready")
        s_lT = sem("ff_ln_transposed")
        s_lTe = sem("ff_lnT_evacuated")
        s_h = sem("ff_hidden_ready")
        s_H = sem("ff_gelu_ready")
        s_y = sem("ff_rows_ready")
        s_yb = sem("ff_rows_biased")
        s_base = sem("base_rows_ready")
        s_basew = sem("base_rows_written")
        s_wd = sem("weighted_rows_ready")
        s_part = sem("selection_partials")
        s_cnt = sem("selection_counts")
        s_sel = sem("selection_chain")
        s_tl = [sem(f"base_back{i}") for i in range(SLOTS)]
        s_to = [sem(f"sums_out{i}") for i in range(SLOTS)]
        s_tf = sem("tail_rows_ready")

        block = ctx.enter_context(nc.Block())

        x_tiles = x[0:(TILES - 1) * P, :].rearrange("(t p) d -> p t d", p=P)
        base_t = base_rows.rearrange("(t p) d -> p t d", p=P)
        table_t = [t.rearrange("(t p) f -> p t f", p=P) for t in table]
        out_t = out[0:(TILES - 1) * P, :].rearrange("(t p) d -> p t d", p=P)
        SMALL_LOADS = 14

        def row(ap, n=P):
            return ap.rearrange("(a n) -> a n", a=1).broadcast_to([n, ap.shape[0]])

        def bc(ap, shape):
            return ap.broadcast_to(shape)

        def read_control(eng, engine_type, g):
            _, words = nc.values_load_multi_w_load_instructions(
                ctl[0:1, ds(g, 1), 0:3].rearrange("p a c -> p (a c)"), engines=[engine_type], min_val=0,
                max_val=(1 << 31) - 1)
            words = [eng.snap(w) for w in words]

            def within(value, least, most):
                return eng.snap(nc.s_assert_within(
                    value, least, most, skip_runtime_bounds_check_because="the kernel's own control table holds no other"))

            batches = []
            for w in words[0:2]:
                lo = within((w >> 16) & 0xFF, 0, TILES - 1)
                hi = within(w >> 24, 1, TILES)
                batches.append((lo, hi, eng.snap(w & 0xFFFF)))
            rel = words[2]
            t0 = within(rel & 0x7F, 0, TILES - 1)
            f0 = eng.snap((rel >> 7) & 1)
            t1 = within((rel >> 8) & 0x7F, 0, TILES - 1)
            f1 = eng.snap((rel >> 15) & 1)
            return batches, (t0, f0), (t1, f1)

        @block.sync
        def _(sp):
            sp.wait_ge(s_pad, 2)
            full = (PAIRS - 1) * ROW
            for rows_i, e in ((dst_rows_i, dst), (src_rows_i, src)):
                sp.dma_start(rows_i[0:PAIRS - 1, :], e[0:full].rearrange("(p e) -> p e", e=ROW)).then_inc(s_edges, 16)
                sp.dma_start(rows_i[PAIRS - 1:PAIRS, 0:EDGES_IN_LAST],
                             e[full:E].rearrange("(a e) -> a e", a=1)).then_inc(s_edges, 16)
            sp.wait_ge(s_tail_zero, 1)
            sp.dma_start(xs[0:LAST, TILES - 1, :], x[(TILES - 1) * P:N, :]).then_inc(s_xtail, 16)
            with sp.Fori(0, GROUPS - 1) as g:
                sp.dma_start(xs[:, ds(g * GROUP, GROUP), :], x_tiles[:, ds(g * GROUP, GROUP), :]).then_inc(s_x, 16)
                sp.wait_ge(s_x, g * 16 + 16)
                sp.sem_inc(s_passed_sp, 1)
            sp.dma_start(xs[:, TILES - GROUP:TILES - 1, :],
                         x_tiles[:, TILES - GROUP:TILES - 1, :]).then_inc(s_x, 16)
            with sp.Fori(0, GROUPS) as g:
                sp.wait_ge(s_scaled, g + 1)
                sp.dma_start(table_t[0][:, ds(g * GROUP, GROUP), :], acc[:, ds(g * GROUP, GROUP), :]).then_inc(s_tab1, 16)
            with sp.Fori(0, TILES) as t:
                sp.wait_ge(s_fin, t + 1)
                sp.dma_start(table_t[1][:, ds(t, 1), :], acc[:, ds(t, 1), :]).then_inc(s_tab2, 16)
            sp.wait_ge(s_mixed, 1)
            sp.dma_start(fw1, w1.rearrange("(k p) h -> p k h", p=P)).then_inc(s_fw, 16)
            sp.dma_start(fw2, w2.rearrange("(k p) d -> p k d", p=P)).then_inc(s_fw, 16)
            sp.sem_inc(s_basew, 16)
            with sp.Fori(0, TILES) as t:
                sp.wait_ge(s_base, t + 1)
                sp.dma_start(base_t[:, ds(t, 1), :], base.rearrange("p (a d) -> p a d", a=1)).then_inc(s_basew, 16)
            sp.wait_ge(s_basew, 16 * (TILES + 1))
            sp.wait_ge(s_wd, TILES)

            def load_base(i):
                if i >= SLOTS:
                    sp.wait_ge(s_to[i % SLOTS], 16)
                sp.dma_start(tail[:, i % SLOTS, :, :], base_t[:, i * HG:(i + 1) * HG, :]).then_inc(s_tl[i % SLOTS], 16)

            for i in range(SLOTS):
                load_base(i)
            for j in range(STEPS):
                sp.wait_ge(s_tf, j + 1)
                if j < STEPS - 1:
                    sp.dma_start(out_t[:, j * HG:(j + 1) * HG, :], tail[:, j % SLOTS, :, :])\
                      .then_inc(s_to[j % SLOTS], 16)
                else:
                    sp.dma_start(out_t[:, j * HG:TILES - 1, :], tail[:, j % SLOTS, 0:HG - 1, :])\
                      .then_inc(s_to[j % SLOTS], 16)
                    sp.dma_start(out[(TILES - 1) * P:N, :], tail[0:LAST, j % SLOTS, HG - 1, :])\
                      .then_inc(s_to[j % SLOTS], 16)
                if 2 <= j and j - 2 + SLOTS < STEPS:
                    load_base(j - 2 + SLOTS)
            for i in range(SLOTS):
                steps_here = len(range(i, STEPS, SLOTS))
                sp.wait_ge(s_to[i], 16 * (steps_here + (i == (STEPS - 1) % SLOTS)))

        @block.gpsimd
        def _(pool):
            pool.memset(dst_rows_i[0:PAIRS, EDGES_IN_LAST:ROW], PAD_NODE).then_inc(s_pad, 1)
            pool.memset(src_rows_i[0:PAIRS, EDGES_IN_LAST:ROW], 0).then_inc(s_pad, 1)
            pool.memset(xs[:, TILES - 1, :], 0.0).then_inc(s_tail_zero, 1)
            pool.memset(ident[:, :], 0.0).then_inc(s_issue, 1)
            pool.wait_ge(s_issue, 1)
            pool.affine_select(out=ident[:, :], in_=ident[:, :], compare_op=ALU.not_equal, fill=1.0, base=0,
                               pattern=[[-1, P]], channel_multiplier=1).then_inc(s_const, 1)
            pool.iota(iota_n[:, :], [[1, P]], base=0, channel_multiplier=0,
                      allow_small_or_imprecise_dtypes=True).then_inc(s_const, 1)
            pool.iota(tile_base[:, :], [[P, TILES]], base=0, channel_multiplier=0,
                      allow_small_or_imprecise_dtypes=True).then_inc(s_const, 1)
            pool.memset(src_idx[:, CHUNKS:CHUNKS + 2 * PAIR], 0).then_inc(s_const, 1)

            def gather_layer(layer):
                with pool.Fori(0, PAIRS // SETS) as gg:
                    for i in range(SETS):
                        pool.wait_ge(s_idx[layer], gg * SETS + (i + 1))
                        pool.sem_inc(s_issue, 1)
                        for h in range(2):
                            pool.wait_ge(s_free[layer], gg * (2 * SETS) + (2 * i + h + 1))
                            pool.sem_inc(s_issue, 1)
                            quarter = 2 * (i % 2) + h
                            for k in range(HALF):
                                c = h * HALF + k
                                pool.indirect_dma_start(
                                    ring[:, quarter * HALF + k, :], None, table[layer],
                                    bass.IndirectOffsetOnAxis(ap=idx_now[:, i, c:c + 1], axis=0),
                                ).then_inc(s_gath[layer][quarter], 16)

            pool.wait_ge(s_tab1, 16 * GROUPS)
            gather_layer(0)
            pool.wait_ge(s_tab2, 16 * TILES)
            gather_layer(1)

        @block.scalar
        def _(act):
            act.dma_start(gW1[:, :, :], W1.rearrange("(k p) f -> p k f", p=P)).then_inc(s_small, 16)
            act.dma_start(gW2[:, :], W2).then_inc(s_small, 16)
            act.dma_start(b1row[:, :], row(b1)).then_inc(s_small, 16)
            act.dma_start(crow[:, :], row(b2)).then_inc(s_small, 16)
            act.dma_start(wrrow[:, :], row(wr.rearrange("d o -> (d o)"))).then_inc(s_small, 16)
            act.dma_start(fb2row[:, :], row(fb2)).then_inc(s_small, 16)
            act.dma_start(brcol[:, :], row(br)).then_inc(s_small, 16)
            with nc.allow_non_contiguous_dma("per-partition biases"):
                act.dma_start(fb1col[:, :], fb1.rearrange("(k p) -> p k", p=P)).then_inc(s_small, 16)
                act.dma_start(sm[:, 8:10], gamma.rearrange("(k p) -> p k", p=P)).then_inc(s_small, 16)
                act.dma_start(sm[:, 10:12], beta.rearrange("(k p) -> p k", p=P)).then_inc(s_small, 16)
                act.dma_start(sm[:, 12:14], b_qk[0, :].rearrange("(k p) -> p k", p=P)).then_inc(s_small, 16)
                act.dma_start(sm[:, 14:16], b_qk[1, :].rearrange("(k p) -> p k", p=P)).then_inc(s_small, 16)
            for e in range(2):
                for b in range(PAIR // 4):
                    i = e * (PAIR // 4) + b
                    act.wait_ge(s_eT, i + 1)
                    view = bank[i % 2][:, 0:4 * PAIRS].rearrange("p (c g) -> p g c", g=PAIRS)
                    to = (dst_of if e == 0 else src_idx)[:, 0:CHUNKS].rearrange("p (g c) -> p g c", c=PAIR)
                    act.activation(to[:, :, 4 * b:4 * b + 4], view, ACT.Copy).then_inc(s_eTe, 1)

            def tile_a(g, j, first):
                n = g * GROUP + j
                if not (first and j < 2):
                    act.wait_ge(s_TA, n - 1)
                act.activation(xnA[:, j % 2, :], xs[:, ds(n, 1), :].rearrange("p a d -> p (a d)"), ACT.Identity,
                               bias=nmr[:, ds(n, 1)], scale=rstd[:, ds(n, 1)]).then_inc(s_xnA, 1)

            def tile_b(g, j, first):
                n = g * GROUP + j
                act.wait_ge(s_TA, n + 1)
                if not (first and j < 2):
                    act.wait_ge(s_hA, n - 1)
                act.activation(xTA[:, j % 2, :], bank[2 + j % 2][:, 0:D], ACT.Copy).then_inc(s_TAe, 1)

            def tile_c(g, j):
                n = g * GROUP + j
                act.wait_ge(s_hA, n + 1)
                act.activation(acc[:, ds(n, 1), :].rearrange("p a d -> p (a d)"), bank[4 + j % 2][:, 0:F],
                               ACT.Copy).then_inc(s_hAe, 1)

            def group(g, first):
                act.wait_ge(s_mvA, g + 1)
                act.activation(rstd[:, ds(g * GROUP, GROUP)], ssq[:, :], ACT.Sqrt, bias=epscol[:, 0:1],
                               scale=1.0 / D).then_inc(s_sdA, 1)
                act.wait_ge(s_rstd, g + 1)
                for j in range(GROUP + 2):
                    if j < GROUP:
                        tile_a(g, j, first)
                    if 1 <= j <= GROUP:
                        tile_b(g, j - 1, first)
                    if j >= 2:
                        tile_c(g, j - 2)

            group(0, True)
            with act.Fori(1, GROUPS) as g:
                group(g, False)
            act.wait_ge(s_deg, 1)
            act.activation(dinv[:, :], pDeg[:, 0:TILES], ACT.Sqrt, bias=1.0).then_inc(s_sq, 1)

            act.wait_ge(s_scaled, 1)
            act.dma_start(Wk, W_qk[1].rearrange("(k p) e -> p k e", p=P)).then_inc(s_mz, 16)
            act.dma_start(Wq, W_qk[0].rearrange("(k p) e -> p k e", p=P)).then_inc(s_mz, 16)
            act.dma_start(Wv, W_v.rearrange("(k p) e -> p k e", p=P)).then_inc(s_mz, 16)
            act.dma_start(bvrow, row(b_v)).then_inc(s_mz, 16)

            def mix(t, n):
                act.wait_ge(s_mG, t + 1)
                act.activation(xn, xs[:, ds(t, 1), :].rearrange("p a d -> p (a d)"), ACT.Identity,
                               bias=nmr[:, ds(t, 1)], scale=rstd[:, ds(t, 1)]).then_inc(s_mxn, 1)
                act.wait_ge(s_mT, t + 1)
                act.activation(xT.rearrange("p k n -> p (k n)"), pT[:, 0:D], ACT.Copy).then_inc(s_mTe, 1)
                act.wait_ge(s_mb, t + 1)
                act.activation(sm[:, 22:24], sm[:, 20:22], ACT.Exp)
                for k in range(KD):
                    last = act.activation(ET[:, k, 0:n], pK[:, k * P:k * P + n], ACT.Exp, bias=sm[:, 24 + k:25 + k],
                                          accum_out=sm[:, 26 + k:27 + k])
                last.then_inc(s_mE, 1)
                act.wait_ge(s_mET, t + 1)
                act.activation(En.rearrange("p k n -> p (k n)"), pE[:, 0:D], ACT.Copy).then_inc(s_mEe, 1)

            with act.Fori(0, TILES - 1) as t:
                mix(t, P)
            mix(TILES - 1, LAST)
            for i, (dsts, srcs) in enumerate(((GT, pT), (WqT, pK))):
                act.wait_ge(s_m1, i + 1)
                act.activation(dsts.rearrange("p k d -> p (k d)"), srcs[:, :], ACT.Copy).then_inc(s_m2, 1)
            act.wait_ge(s_m3, 2)
            act.activation(sm[:, 34:36], sm[:, 32:34], ACT.Sqrt, bias=epscol[:, 0:1]).then_inc(s_m2, 1)
            act.wait_ge(s_m1, 4)
            act.activation(Pmix[:, :, :].rearrange("p k d -> p (k d)"), pG[:, :], ACT.Copy).then_inc(s_m2, 1)

            act.wait_ge(s_mixed, 1)
            with act.Fori(0, TILES) as t:
                act.activation(xnD, xs[:, ds(t, 1), :].rearrange("p a d -> p (a d)"), ACT.Identity,
                               bias=nmr[:, ds(t, 1)], scale=rstd[:, ds(t, 1)]).then_inc(s_dxn, 1)
                act.wait_ge(s_dT, t + 1)
                act.activation(T3.rearrange("p k n -> p (k n)"), pT[:, 0:3 * P], ACT.Copy).then_inc(s_dTe, 1)
                act.wait_ge(s_var, t + 1)
                act.activation(sm[:, 40:41], mv[:, 1:2], ACT.Sqrt, bias=epscol[:, 0:1]).then_inc(s_sd, 1)
                act.wait_ge(s_lT, t + 1)
                act.activation(T3[:, 0:KD, :].rearrange("p k n -> p (k n)"), pT[:, 0:D], ACT.Copy).then_inc(s_lTe, 1)
                act.wait_ge(s_h, t + 1)
                for k in range(KH):
                    last = act.activation(H[:, k, :], pH[k // 4][:, (k % 4) * P:(k % 4 + 1) * P],
                                          ACT.Gelu_apprx_tanh, bias=fb1col[:, k:k + 1])
                last.then_inc(s_H, 1)

        @block.tensor
        def _(pe):
            pe.wait_ge(s_const, 3)
            for e in range(2):
                pe.wait_ge(s_rowsf, e + 1)
                rows = (dst_rows, src_rows)[e]
                for b in range(PAIR // 4):
                    i = e * (PAIR // 4) + b
                    if i >= 2:
                        pe.wait_ge(s_eTe, i - 1)
                    for c in range(4):
                        k = 4 * b + c
                        last = nc.tensor.transpose(bank[i % 2][:, c * PAIRS:(c + 1) * PAIRS],
                                                   rows[0:PAIRS, k * P:(k + 1) * P], ident[0:PAIRS, 0:PAIRS])
                    last.then_inc(s_eT, 1)
            pe.wait_ge(s_rngdone, 1)
            for i in range(4):
                last = nc.tensor.transpose(bank[6][0:1, i * P:i * P + PAIRS], rng[0:PAIRS, i:i + 1],
                                           ident[0:PAIRS, 0:PAIRS])
            last.then_inc(s_rngT, 1)
            pe.wait_ge(s_zero, 1)
            nc.tensor.matmul(bank[6][:, 0:2 * PAIRS], ones_row, low_row, start=True, stop=True)\
              .then_inc(s_low, 1)
            pe.wait_ge(s_small, 16 * 12)

            def transposes_a(g, j, first):
                n = g * GROUP + j
                pe.wait_ge(s_xnA, n + 1)
                if not (first and j < 2):
                    pe.wait_ge(s_TAe, n - 1)
                for k in range(KD):
                    last = nc.tensor.transpose(bank[2 + j % 2][:, k * P:(k + 1) * P],
                                               xnA[:, j % 2, k * P:(k + 1) * P], ident[:, :])
                last.then_inc(s_TA, 1)

            def h1_a(g, j, first):
                n = g * GROUP + j
                pe.wait_ge(s_TAe, n + 1)
                if not (first and j < 2):
                    pe.wait_ge(s_hAe, n - 1)
                for k in range(KD):
                    last = nc.tensor.matmul(bank[4 + j % 2][:, 0:F], xTA[:, j % 2, k * P:(k + 1) * P], gW1[:, k, :],
                                            start=(k == 0), stop=(k == KD - 1))
                last.then_inc(s_hA, 1)

            def group(g, first):
                for j in range(GROUP + 1):
                    if j < GROUP:
                        transposes_a(g, j, first)
                    if j >= 1:
                        h1_a(g, j - 1, first)

            group(0, True)
            with pe.Fori(1, GROUPS) as g:
                group(g, False)

            def degrees(gg, first, last_gg):
                for par in range(2):
                    pe.wait_ge(s_oh, gg * 2 + par + 1)
                    for c in range(PAIR):
                        last = nc.tensor.matmul(pDeg[:, 0:TILES], oh_r[:, par, c, :], oh_q[:, par, c, :],
                                                start=(first and par == 0 and c == 0),
                                                stop=(last_gg and par == 1 and c == PAIR - 1))
                    last.then_inc(s_ohu, 1)

            def degrees_in_windows(gg):
                for par in range(2):
                    (b0, b1), _, _ = read_control(pe, mybir.EngineType.PE, gg * 2 + par)
                    pe.wait_ge(s_oh, gg * 2 + par + 1)
                    for c in range(PAIR):
                        lo = (b0, b1)[c // HALF][0]
                        last = nc.tensor.matmul(pDeg[:, ds(lo, WIN)], oh_r[:, par, c, :],
                                                oh_q[:, par, c, 0:WIN], start=False, stop=False)
                    last.then_inc(s_ohu, 1)

            pe.wait_ge(s_ctl, 1)
            span = pe.value_load(wide[0:1, 0:1], min_val=0, max_val=TILES)
            with pe.If(span < WIN):
                pe.wait_ge(s_zero, 1)
                nc.tensor.matmul(pDeg[:, 0:TILES + WIN], ident_b, zeros_b, start=True, stop=False)
                with pe.Fori(0, PAIRS // 2) as gg:
                    degrees_in_windows(gg)
                nc.tensor.matmul(pDeg[:, 0:TILES + WIN], ident_b, zeros_b, start=False, stop=True).then_inc(s_deg, 1)
            with pe.Else():
                degrees(0, True, False)
                with pe.Fori(1, PAIRS // 2 - 1) as gg:
                    degrees(gg, False, False)
                degrees(PAIRS // 2 - 1, False, True)
                pe.wait_ge(s_ohu, PAIRS)
                pe.sem_inc(s_deg, 1)

            def visit(layer, batch, gg, quarter, t):
                v = batch[2] + t
                h = quarter % 2
                pe.wait_ge(s_gath[layer][quarter], gg * (16 * HALF) + 16 * HALF)
                pe.wait_ge(s_fl[layer][h], v + 1)
                for k in range(HALF):
                    q = k // 4
                    if k % 4 == 0:
                        pe.wait_ge(s_S[layer][h][q], v + 1)
                    last = nc.tensor.matmul(visit_sum[h][:, 0:F], S[:, h, k, :], ring[:, quarter * HALF + k, :],
                                            start=(k == 0), stop=(k == HALF - 1))
                    if k == 3:
                        last.then_inc(s_Su[layer][h], 1)
                last.then_inc(s_sum[layer][h], 1)

            def other_visits(layer, batch, gg, quarter):
                lo, hi, _ = batch
                with pe.If(hi > lo + 1):
                    with pe.Fori(lo + 1, hi) as t:
                        visit(layer, batch, gg, quarter, t)

            def mix_1(t):
                pe.wait_ge(s_mxn, t + 1)
                for k in range(KD):
                    last = nc.tensor.transpose(pT[:, k * P:(k + 1) * P], xn[:, k * P:(k + 1) * P], ident[:, :])
                last.then_inc(s_mT, 1)

            def mix_keys(t):
                pe.wait_ge(s_mTe, t + 1)
                for e in range(KD):
                    for k in range(KD):
                        last = nc.tensor.matmul(pK[:, e * P:(e + 1) * P], Wk[:, k, e * P:(e + 1) * P], xT[:, k, :],
                                                start=(k == 0), stop=(k == KD - 1))
                last.then_inc(s_mK, 1)

            def mix_2(t):
                pe.wait_ge(s_mE, t + 1)
                for k in range(KD):
                    last = nc.tensor.transpose(pE[:, k * P:(k + 1) * P], ET[:, k, :], ident[:, :])
                last.then_inc(s_mET, 1)

            def mix_3(t):
                pe.wait_ge(s_mEe, t + 1)
                for k in range(KD):
                    last = nc.tensor.matmul(pG[:, k * D:(k + 1) * D], En[:, k, :], xn, start=True, stop=True)
                last.then_inc(s_mG, 1)

            pe.wait_ge(s_mz, 16 * 4)
            pe.sem_inc(s_mG, 1)

            def pair_of_layer_1(gg, par, mixing):
                g = gg * 2 + par
                (b0, b1), _, _ = read_control(pe, mybir.EngineType.PE, g)
                if mixing:
                    mix_1(g)
                visit(0, b0, gg, 2 * par, b0[0])
                if mixing:
                    mix_keys(g)
                other_visits(0, b0, gg, 2 * par)
                visit(0, b1, gg, 2 * par + 1, b1[0])
                if mixing:
                    mix_2(g)
                other_visits(0, b1, gg, 2 * par + 1)
                if mixing:
                    mix_3(g)

            with pe.Fori(0, TILES // 2) as gg:
                for par in range(2):
                    pair_of_layer_1(gg, par, True)

            pe.wait_ge(s_m3, 1)
            for c in range(KD):
                for k in range(KD):
                    last = nc.tensor.transpose(pT[:, k * D + c * P:k * D + (c + 1) * P], Gs[:, c, k * P:(k + 1) * P],
                                               ident[:, :])
            last.then_inc(s_m1, 1)
            for c in range(KD):
                for k in range(KD):
                    last = nc.tensor.transpose(pK[:, c * D + k * P:c * D + (k + 1) * P], Wq[:, k, c * P:(c + 1) * P],
                                               ident[:, :])
            last.then_inc(s_m1, 1)
            pe.wait_ge(s_m2, 1)
            for c in range(KD):
                for k in range(KD):
                    last = nc.tensor.matmul(pE[:, c * D:(c + 1) * D], GT[:, k, c * P:(c + 1) * P], Wv[:, k, :],
                                            start=(k == 0), stop=(k == KD - 1))
            last.then_inc(s_m1, 1)

            for par in range(2):
                pair_of_layer_1(TILES // 2, par, False)
            pe.wait_ge(s_m3, 3)
            for k in range(KD):
                for c in range(KD):
                    last = nc.tensor.matmul(pG[:, k * D:(k + 1) * D], WqT[:, c, k * P:(k + 1) * P], lam[:, c, :],
                                            start=(c == 0), stop=(c == KD - 1))
            last.then_inc(s_m1, 1)
            for c in range(KD):
                last = nc.tensor.matmul(pT[:, 0:D], bqb[:, c, :], lam[:, c, :], start=(c == 0), stop=(c == KD - 1))
            last.then_inc(s_m1, 1)

            with pe.Fori(TILES // 2 + 1, PAIRS // 2) as gg:
                for par in range(2):
                    pair_of_layer_1(gg, par, False)

            pe.wait_ge(s_mixed, 1)
            pe.wait_ge(s_fw, 32)

            def ff_1(t):
                pe.wait_ge(s_dxn, t + 1)
                pe.wait_ge(s_aggs, t + 1)
                nc.tensor.transpose(pT[:, 0:P], aggs, ident[:, :])
                for k in range(KD):
                    last = nc.tensor.transpose(pT[:, (k + 1) * P:(k + 2) * P], xnD[:, k * P:(k + 1) * P], ident[:, :])
                last.then_inc(s_dT, 1)

            def ff_mixed(t):
                pe.wait_ge(s_dTe, t + 1)
                nc.tensor.matmul(pY1[:, 0:D], T3[:, 0, :], gW2[:, :], start=True, stop=False)
                for k in range(KD):
                    last = nc.tensor.matmul(pY1[:, 0:D], T3[:, k + 1, :], Pmix[:, k, :], start=False,
                                            stop=(k == KD - 1))
                last.then_inc(s_y1, 1)

            def ff_2(t):
                pe.wait_ge(s_ln, t + 1)
                for k in range(KD):
                    last = nc.tensor.transpose(pT[:, k * P:(k + 1) * P], ln[:, k * P:(k + 1) * P], ident[:, :])
                last.then_inc(s_lT, 1)

            def ff_hidden(t):
                pe.wait_ge(s_lTe, t + 1)
                for h in range(KH):
                    for k in range(KD):
                        last = nc.tensor.matmul(pH[h // 4][:, (h % 4) * P:(h % 4 + 1) * P],
                                                fw1[:, k, h * P:(h + 1) * P], T3[:, k, :],
                                                start=(k == 0), stop=(k == KD - 1))
                last.then_inc(s_h, 1)

            def ff_3(t):
                pe.wait_ge(s_H, t + 1)
                for h in range(KH):
                    last = nc.tensor.matmul(pY[:, 0:D], H[:, h, :], fw2[:, h, :], start=(h == 0), stop=(h == KH - 1))
                last.then_inc(s_y, 1)

            with pe.Fori(0, PAIRS // 2) as gg:
                for par in range(2):
                    g = gg * 2 + par
                    (b0, b1), (t0, f0), (t1, f1) = read_control(pe, mybir.EngineType.PE, g)
                    visit(1, b0, gg, 2 * par, b0[0])
                    with pe.If(f1 > 0):
                        ff_3(t1)
                    with pe.If(f0 > 0):
                        ff_1(t0)
                    other_visits(1, b0, gg, 2 * par)
                    with pe.If(f0 > 0):
                        ff_mixed(t0)
                    visit(1, b1, gg, 2 * par + 1, b1[0])
                    with pe.If(f0 > 0):
                        ff_2(t0)
                    other_visits(1, b1, gg, 2 * par + 1)
                    with pe.If(f0 > 0):
                        ff_hidden(t0)
            _, (tend, _), (t1, f1) = read_control(pe, mybir.EngineType.PE, PAIRS)
            with pe.If(f1 > 0):
                ff_3(t1)
            with pe.Fori(tend, TILES) as t:
                ff_1(t)
                ff_mixed(t)
                ff_2(t)
                ff_hidden(t)
                ff_3(t)

            for i in range(1 + len(ROUNDS)):
                pe.wait_ge(s_part, i + 1)
                nc.tensor.matmul(bank[2][:, 0:CAND], ones_m, part, start=True, stop=True).then_inc(s_cnt, 1)
            pe.wait_ge(s_part, 2 + len(ROUNDS))
            nc.tensor.matmul(bank[2][:, 0:TILES], ones_m, eq, start=True, stop=True)
            nc.tensor.matmul(bank[3][:, 0:TILES], lower, eq, start=True, stop=True)
            nc.tensor.matmul(bank[4][:, 0:1], ones_m, sm[:, 51:52], start=True, stop=True).then_inc(s_cnt, 1)

        @block.vector
        def _(dve):
            steps = [0]

            def link(ins):
                steps[0] += 1
                ins.then_inc(s_dve, 1)
                dve.wait_ge(s_dve, steps[0])

            dve.memset(epscol[:, :], EPS)
            dve.wait_ge(s_edges, 16 * 4)
            dve.tensor_copy(dst_rows[0:PAIRS, :], dst_rows_i[0:PAIRS, :]).then_inc(s_rowsf, 1)
            dve.wait_ge(s_rowsf, 1)
            dve.tensor_copy(src_rows[0:PAIRS, :], src_rows_i[0:PAIRS, :]).then_inc(s_rowsf, 1)
            halves = dst_rows[0:PAIRS, :].rearrange("p (h e) -> p h e", h=2)
            dve.tensor_reduce(rng[0:PAIRS, 0:2], halves, AX.X, ALU.min)
            link(dve.tensor_reduce(rng[0:PAIRS, 2:4], halves, AX.X, ALU.max))
            link(dve.tensor_copy(rng_i[0:PAIRS, :], rng[0:PAIRS, :]))
            link(dve.tensor_scalar(rng_i[0:PAIRS, :], rng_i[0:PAIRS, :], 7, None, ALU.arith_shift_right))
            dve.tensor_copy(rng[0:PAIRS, :], rng_i[0:PAIRS, :]).then_inc(s_rngdone, 1)
            dve.wait_ge(s_rngT, 1)
            lo_r, hi_r, cnt_r, zero_r, vin_r = (rrow[:, i, :] for i in range(5))
            m_r, done_r, one_r = rrow[:, 5, 0:PAIRS], rrow[:, 6, 0:PAIRS], rrow[:, 7, 0:PAIRS]
            rel_r = rrow[:, 8, 0:PAIRS + 2]
            flag_r = rrow[:, 9, 0:PAIRS + 2]
            wi = ctl[:, 0:PAIRS, 0:2]
            hi_i = rrow[:, 7, :].bitcast(i32).rearrange("p (g h) -> p g h", h=2)
            for h in range(2):
                dve.tensor_copy(lo_r.rearrange("p (g h) -> p g h", h=2)[:, :, h], bank[6][0:1, h * P:h * P + PAIRS])
                link(dve.tensor_copy(hi_r.rearrange("p (g h) -> p g h", h=2)[:, :, h],
                                     bank[6][0:1, (2 + h) * P:(2 + h) * P + PAIRS]))
            dve.memset(zero_r, 0.0)
            dve.memset(ones_row, 1.0)
            dve.memset(zeros_b, 0.0)
            dve.wait_ge(s_const, 1)
            dve.tensor_copy(ident_b, ident[:, :])
            link(dve.memset(one_r, 1.0))
            dve.sem_inc(s_zero, 1)
            link(dve.scalar_tensor_tensor(cnt_r, hi_r, 1.0, lo_r, ALU.add, ALU.subtract))
            for h in range(2):
                of_h = [r.rearrange("p (g h) -> p g h", h=2)[:, :, h] for r in (vin_r, cnt_r, zero_r)]
                link(dve.tensor_tensor_scan(of_h[0], of_h[1], of_h[2], 0.0, ALU.add, ALU.add))
            link(dve.tensor_reduce(sm[0:1, 60:61], cnt_r, AX.X, ALU.max))
            link(dve.tensor_scalar(wide[:, :], sm[0:1, 60:61], -1.0, None, ALU.add))
            lo2 = lo_r.rearrange("p (g h) -> p g h", h=2)
            link(dve.tensor_tensor(m_r, lo2[:, :, 0], lo2[:, :, 1], ALU.min))
            link(dve.tensor_tensor_scan(done_r[:, ::-1], m_r[:, ::-1], m_r[:, ::-1], 1e9, ALU.min, ALU.min))
            link(dve.memset(rel_r, 0.0))
            link(dve.memset(ctl[:, :, :], 0))
            link(dve.tensor_tensor_scan(rel_r[:, 2:PAIRS + 2], one_r, done_r, 0.0, ALU.add, ALU.min))
            link(dve.memset(flag_r, 0.0))
            link(dve.tensor_tensor(flag_r[:, 0:PAIRS + 1], rel_r[:, 1:PAIRS + 2], rel_r[:, 0:PAIRS + 1], ALU.subtract))
            link(dve.tensor_tensor(vin_r, vin_r, cnt_r, ALU.subtract))
            link(dve.scalar_tensor_tensor(vin_r, vin_r, float(TILES), lo_r, ALU.add, ALU.subtract))
            link(dve.scalar_tensor_tensor(vin_r, lo_r, 65536.0, vin_r, ALU.mult, ALU.add))
            link(dve.tensor_copy(wi, vin_r.rearrange("p (g h) -> p g h", h=2)))
            link(dve.tensor_scalar(hi_i, hi_r.rearrange("p (g h) -> p g h", h=2), 1.0, None, ALU.add))
            link(dve.tensor_scalar(hi_i, hi_i, 24, None, ALU.logical_shift_left))
            link(dve.tensor_tensor(wi, wi, hi_i, ALU.bitwise_or))
            tmp_r = rrow[:, 3, 0:PAIRS + 2]
            done_w = rrow[:, 1, 0:PAIRS + 1]
            link(dve.scalar_tensor_tensor(tmp_r, flag_r, 128.0, rel_r, ALU.mult, ALU.add))
            link(dve.scalar_tensor_tensor(done_w, tmp_r[:, 0:PAIRS + 1], 256.0, tmp_r[:, 1:PAIRS + 2], ALU.mult,
                                          ALU.add))
            dve.tensor_copy(ctl[:, :, 2:3].rearrange("p g a -> p (g a)"), done_w).then_inc(s_ctl, 1)

            dve.wait_ge(s_xtail, 16)

            def stats_of_group(g):
                dve.wait_ge(s_x, g * 16 + 16)
                for j in range(GROUP):
                    last = dve.bn_stats(statsA[:, j, :],
                                        xs[:, ds(g * GROUP + j, 1), :].rearrange("p a d -> p (a d)"))
                last.then_inc(s_bn, 1)
                dve.wait_ge(s_bn, g * 3 + 1)
                me, se, mo, so = (statsA[:, :, i] for i in (1, 2, 4, 5))
                dve.tensor_tensor(mean2[:, :], me, mo, ALU.add)
                dve.tensor_tensor(ssq[:, :], se, so, ALU.add)
                dve.tensor_tensor(dif[:, :], me, mo, ALU.subtract).then_inc(s_bn, 1)
                dve.wait_ge(s_bn, g * 3 + 2)
                dve.scalar_tensor_tensor(dif[:, :], dif[:, :], float(D) / 4, dif[:, :], ALU.mult, ALU.mult)\
                   .then_inc(s_bn, 1)
                dve.wait_ge(s_bn, g * 3 + 3)
                dve.tensor_tensor(ssq[:, :], ssq[:, :], dif[:, :], ALU.add).then_inc(s_mvA, 1)
                dve.wait_ge(s_sdA, g + 1)
                gs = ds(g * GROUP, GROUP)
                dve.reciprocal(rstd[:, gs], rstd[:, gs]).then_inc(s_rcpA, 1)
                dve.wait_ge(s_rcpA, g + 1)
                dve.scalar_tensor_tensor(nmr[:, gs], mean2[:, :], -0.5, rstd[:, gs],
                                         ALU.mult, ALU.mult).then_inc(s_rstd, 1)

            with dve.Fori(0, GROUPS) as g:
                stats_of_group(g)

            dve.wait_ge(s_eTe, 4)
            r_i, q_i = r_of.bitcast(i32), q_of.bitcast(i32)
            link(dve.tensor_copy(r_i, dst_of[:, :]))
            link(dve.tensor_scalar(q_i, r_i, 7, None, ALU.arith_shift_right))
            link(dve.tensor_scalar(r_i, r_i, 127, None, ALU.bitwise_and))
            link(dve.tensor_copy(q_of, q_i))
            link(dve.tensor_copy(r_of, r_i))
            dve.wait_ge(s_const, 4)
            dve.wait_ge(s_low, 1)
            link(dve.tensor_copy(low_of, bank[6][:, 0:2 * PAIRS]))
            link(dve.tensor_tensor(q_rel.rearrange("p (b k) -> p b k", k=HALF),
                                   q_of.rearrange("p (b k) -> p b k", k=HALF),
                                   bc(low_of.rearrange("p (b a) -> p b a", a=1), [P, 2 * PAIRS, HALF]), ALU.subtract))

            def one_hots(gg, first, kinds):
                for par in range(2):
                    if not first:
                        dve.wait_ge(s_ohu, gg * 2 + par - 1)
                    cols = ds(gg * (2 * PAIR) + par * PAIR, PAIR)
                    for to, of, width in kinds:
                        last = dve.tensor_tensor(
                            to[:, par, :, 0:width], bc(iota_n[:, 0:width].rearrange("p (a n) -> p a n", a=1), [P, PAIR, width]),
                            bc(of[:, cols].rearrange("p (c a) -> p c a", a=1), [P, PAIR, width]), ALU.is_equal)
                    last.then_inc(s_oh, 1)

            both = ((oh_r, r_of, P), (oh_q, q_of, TILES))
            in_windows = (both[0], (oh_q, q_rel, WIN))
            span = dve.value_load(wide[0:1, 0:1], min_val=0, max_val=TILES)
            with dve.If(span < WIN):
                one_hots(0, True, in_windows)
                with dve.Fori(1, PAIRS // 2) as gg:
                    one_hots(gg, False, in_windows)
            with dve.Else():
                one_hots(0, True, both)
                with dve.Fori(1, PAIRS // 2) as gg:
                    one_hots(gg, False, both)
            dve.wait_ge(s_sq, 1)
            link(dve.reciprocal(dinv[:, :], dinv[:, :]))
            dve.wait_ge(s_hAe, TILES)
            for g in range(GROUPS):
                gs = slice(g * GROUP, (g + 1) * GROUP)
                dve.tensor_tensor(acc[:, gs, :], acc[:, gs, :],
                                  bc(dinv[:, gs].rearrange("p (t a) -> p t a", a=1), [P, GROUP, F]),
                                  ALU.mult).then_inc(s_scaled, 1)
            dve.wait_ge(s_eTe, 8)
            dve.tensor_copy(idx_now[:, 0:2, :], src_idx[:, 0:2 * PAIR].rearrange("p (a c) -> p a c", a=2))\
               .then_inc(s_idx[0], 2)
            dve.memset(sm[:, 16:18], -3.0e38)
            dve.memset(sm[:, 18:20], 0.0)
            link(dve.memset(Gs, 0.0))
            dve.wait_ge(s_tab1, 16 * GROUPS)
            for layer in range(2):
                for h in range(2):
                    dve.sem_inc(s_Su[layer][h], TILES + 1)
                    dve.sem_inc(s_fl[layer][h], TILES + 1)
                    for started in (s_S[layer][h][0], s_S[layer][h][1], s_sum[layer][h], s_drel[layer][h]):
                        dve.sem_inc(started, TILES)
                dve.sem_inc(s_free[layer], 4)

            def build(layer, batch, g, h, t):
                v = batch[2] + t
                dve.tensor_scalar(drel[:, h, :], dst_of[:, ds(g * PAIR + h * HALF, HALF)], tile_base[:, ds(t, 1)],
                                  None, ALU.subtract).then_inc(s_drel[layer][h], 1)
                dve.wait_ge(s_drel[layer][h], v + 1)
                for q in range(2):
                    if q == 0:
                        dve.wait_ge(s_Su[layer][h], v + 1)
                    else:
                        dve.wait_ge(s_fl[layer][h], v + 1)
                    dve.tensor_tensor(S[:, h, 4 * q:4 * q + 4, :],
                                      bc(iota_n[:, :].rearrange("p (a n) -> p a n", a=1), [P, 4, P]),
                                      bc(drel[:, h, 4 * q:4 * q + 4].rearrange("p (c a) -> p c a", a=1), [P, 4, P]),
                                      ALU.is_equal).then_inc(s_S[layer][h][q], 1)

            def add(layer, batch, h, t):
                v = batch[2] + t
                dve.wait_ge(s_sum[layer][h], v + 1)
                a = acc[:, ds(t, 1), :].rearrange("p a f -> p (a f)")
                dve.tensor_tensor(a, visit_sum[h][:, 0:F], a, ALU.add).then_inc(s_fl[layer][h], 1)

            def other_visits(layer, batch, g, h):
                lo, hi, _ = batch
                with dve.If(hi > lo + 1):
                    with dve.Fori(lo + 1, hi) as t:
                        build(layer, batch, g, h, t)
                        add(layer, batch, h, t)
                dve.wait_ge(s_fl[layer][h], batch[2] + hi + 1)
                dve.sem_inc(s_free[layer], 1)

            def next_indices(layer, g):
                dve.tensor_copy(idx_now[:, ds((g + 2) % SETS, 1), :].rearrange("p a c -> p (a c)"),
                                src_idx[:, ds(g * PAIR + 2 * PAIR, PAIR)]).then_inc(s_idx[layer], 1)

            def finish_layer_1(t):
                a = acc[:, ds(t, 1), :].rearrange("p a f -> p (a f)")
                di = dinv[:, ds(t, 1)]
                dve.scalar_tensor_tensor(a, a, di, b1row[:, :], ALU.mult, ALU.add).then_inc(s_fin0, 1)
                dve.wait_ge(s_fin0, t + 1)
                dve.tensor_scalar(a, a, 0.0, di, ALU.max, ALU.mult).then_inc(s_fin, 1)

            def mix_1(t, n):
                k = [0]

                def step(ins):
                    k[0] += 1
                    ins.then_inc(s_mch, 1)
                    dve.wait_ge(s_mch, t * 5 + k[0])

                dve.wait_ge(s_mK, t + 1)
                step(dve.tensor_reduce(sm[:, 28:30], pK[:, 0:D].rearrange("p (k n) -> p k n", k=KD)[:, :, 0:n], AX.X,
                                       ALU.max))
                step(dve.tensor_tensor(sm[:, 28:30], sm[:, 28:30], sm[:, 14:16], ALU.add))
                step(dve.tensor_tensor(sm[:, 30:32], sm[:, 28:30], sm[:, 16:18], ALU.max))
                dve.tensor_tensor(sm[:, 20:22], sm[:, 16:18], sm[:, 30:32], ALU.subtract)
                step(dve.tensor_tensor(sm[:, 24:26], sm[:, 14:16], sm[:, 30:32], ALU.subtract))
                step(dve.tensor_copy(sm[:, 16:18], sm[:, 30:32]))
                dve.sem_inc(s_mb, 1)

            def mix_3(t):
                dve.wait_ge(s_mE, t + 1)
                dve.tensor_tensor(sm[:, 18:20], sm[:, 18:20], sm[:, 22:24], ALU.mult).then_inc(s_mch2, 1)
                dve.wait_ge(s_mch2, t + 1)
                dve.tensor_tensor(sm[:, 18:20], sm[:, 18:20], sm[:, 26:28], ALU.add)
                dve.wait_ge(s_mG, t + 2)
                for k in range(KD):
                    last = dve.scalar_tensor_tensor(Gs[:, k, :], Gs[:, k, :], sm[:, 22 + k:23 + k],
                                                    pG[:, k * D:(k + 1) * D], ALU.mult, ALU.add)
                last.then_inc(s_mu, 1)

            def pair_of_layer_1(g, n, before):
                (b0, b1), (t0, f0), _ = read_control(dve, mybir.EngineType.DVE, g)
                next_indices(0, g)
                build(0, b0, g, 0, b0[0])
                build(0, b1, g, 1, b1[0])
                with dve.If(f0 > 0):
                    finish_layer_1(t0)
                if before is not None:
                    mix_3(before)
                add(0, b0, 0, b0[0])
                other_visits(0, b0, g, 0)
                if n is not None:
                    mix_1(g, n)
                add(0, b1, 1, b1[0])
                other_visits(0, b1, g, 1)

            pair_of_layer_1(0, P, None)
            with dve.Fori(1, TILES - 1) as g:
                pair_of_layer_1(g, P, g - 1)
            mix_3(TILES - 2)
            dve.memset(ET[:, :, LAST:P], 0.0)
            with dve.Fori(TILES - 1, TILES) as g:
                pair_of_layer_1(g, LAST, None)
            mix_3(TILES - 1)

            dve.wait_ge(s_mu, TILES)
            link(dve.reciprocal(sm[:, 18:20], sm[:, 18:20]))
            for c in range(KD):
                last = dve.tensor_scalar(Gs[:, c, :], Gs[:, c, :], sm[:, 18 + c:19 + c], None, ALU.mult)
            last.then_inc(s_m3, 1)
            dve.tensor_copy(bqb, bc(sm[:, 12:14].rearrange("p (k a) -> p k a", a=1), [P, KD, P]))
            dve.wait_ge(s_m1, 3)
            link(dve.tensor_tensor(lam, pE[:, :].rearrange("p (c d) -> p c d", c=KD),
                                   bc(bvrow.rearrange("p (a d) -> p a d", a=1), [P, KD, D]), ALU.add))
            for c in range(KD):
                link(dve.bn_stats(stats2[:, c, :], lam[:, c, :]))
                link(dve.bn_aggr(mv[:, :], stats2[:, c, :]))
                dve.tensor_copy(sm[:, 36 + c:37 + c], mv[:, 0:1])
                link(dve.tensor_copy(sm[:, 32 + c:33 + c], mv[:, 1:2]))
            dve.sem_inc(s_m3, 1)
            with dve.Fori(TILES, TILES + 1) as g:
                pair_of_layer_1(g, None, None)
            dve.wait_ge(s_m2, 3)
            link(dve.reciprocal(sm[:, 34:36], sm[:, 34:36]))
            link(dve.tensor_tensor(sm[:, 34:36], sm[:, 34:36], sm[:, 8:10], ALU.mult))
            link(dve.tensor_tensor(sm[:, 36:38], sm[:, 36:38], sm[:, 34:36], ALU.mult))
            link(dve.tensor_tensor(sm[:, 36:38], sm[:, 10:12], sm[:, 36:38], ALU.subtract))
            for c in range(KD):
                last = dve.tensor_scalar(lam[:, c, :], lam[:, c, :], sm[:, 34 + c:35 + c], sm[:, 36 + c:37 + c],
                                         ALU.mult, ALU.add)
            last.then_inc(s_m3, 1)
            with dve.Fori(TILES + 1, TILES + 2) as g:
                pair_of_layer_1(g, None, None)
            dve.wait_ge(s_m1, 5)
            dve.wait_ge(s_m2, 4)
            dve.tensor_tensor(crow[:, :], crow[:, :], pT[:, 0:D], ALU.add).then_inc(s_mixed, 1)

            with dve.Fori(TILES + 2, PAIRS) as g:
                pair_of_layer_1(g, None, None)
            _, (tend, _), _ = read_control(dve, mybir.EngineType.DVE, PAIRS)
            with dve.Fori(tend, TILES) as t:
                finish_layer_1(t)

            dve.tensor_copy(idx_now[:, 0:2, :], src_idx[:, 0:2 * PAIR].rearrange("p (a c) -> p a c", a=2))\
               .then_inc(s_idx[1], 2)
            dve.wait_ge(s_tab2, 16 * TILES)

            class Chain:
                PER = 7

                def __init__(self, k=0):
                    self.k = k

                def step(self, t, ins):
                    self.k += 1
                    assert self.k <= Chain.PER
                    ins.then_inc(s_dch, 1)
                    dve.wait_ge(s_dch, t * Chain.PER + self.k)

            def ff_1(t, ch):
                ch.step(t, dve.tensor_scalar(aggs, acc[:, ds(t, 1), :].rearrange("p a f -> p (a f)"), dinv[:, ds(t, 1)],
                                             None, ALU.mult))
                dve.sem_inc(s_aggs, 1)
                ch.step(t, dve.tensor_tensor(x1, xs[:, ds(t, 1), :].rearrange("p a f -> p (a f)"), crow[:, :],
                                             ALU.add))
                dve.sem_inc(s_passed, 1)

            def ff_norm(t, ch):
                dve.wait_ge(s_y1, t + 1)
                ch.step(t, dve.tensor_tensor(x1, x1, pY1[:, 0:D], ALU.add))
                ch.step(t, dve.bn_stats(stats[:, :], x1))
                dve.sem_inc(s_passed, 1)
                dve.bn_aggr(mv[:, :], stats[:, :]).then_inc(s_var, 1)
                dve.wait_ge(s_sd, t + 1)
                ch.step(t, dve.reciprocal(sm[:, 41:42], sm[:, 40:41]))
                dve.tensor_scalar(ln, x1, mv[:, 0:1], sm[:, 41:42], ALU.subtract, ALU.mult).then_inc(s_ln, 1)

            def ff_route(t, ch):
                dve.wait_ge(s_ln, t + 1)
                dve.wait_ge(s_basew, t * 16 + 16)
                dve.tensor_tensor(base, x1, ln, ALU.add).then_inc(s_base, 1)
                dve.wait_ge(s_base, t + 1)
                ch.step(t, dve.tensor_tensor_reduce(out=x1, in0=ln, in1=wrrow[:, :], scale=1.0, scalar=0.0,
                                                    op0=ALU.mult, op1=ALU.add, accum_out=sm[:, 42:43]))
                ch.step(t, dve.tensor_tensor(sm[:, 43:44], sm[:, 42:43], brcol[:, :], ALU.add))
                dve.tensor_copy(wts[:, ds(t, 1)], sm[:, 43:44])
                assert ch.k == Chain.PER

            def ff_3(t):
                rows = xs[:, ds(t, 1), :].rearrange("p a f -> p (a f)")
                dve.wait_ge(s_y, t + 1)
                dve.tensor_tensor(rows, pY[:, 0:D], fb2row[:, :], ALU.add).then_inc(s_yb, 1)
                dve.wait_ge(s_yb, t + 1)
                dve.tensor_scalar(rows, rows, sm[:, 43:44], None, ALU.mult).then_inc(s_wd, 1)

            def ff_route_and_3(t):
                ff_route(t, Chain(Chain.PER - 2))
                ff_3(t)

            with dve.Fori(0, PAIRS) as g:
                (b0, b1), (t0, f0), (t1, f1) = read_control(dve, mybir.EngineType.DVE, g)
                ch = Chain()
                next_indices(1, g)
                build(1, b0, g, 0, b0[0])
                with dve.If(f1 > 0):
                    ff_route(t1, Chain(Chain.PER - 2))
                with dve.If(f0 > 0):
                    ff_1(t0, ch)
                build(1, b1, g, 1, b1[0])
                add(1, b0, 0, b0[0])
                other_visits(1, b0, g, 0)
                with dve.If(f1 > 0):
                    ff_3(t1)
                with dve.If(f0 > 0):
                    ff_norm(t0, ch)
                add(1, b1, 1, b1[0])
                other_visits(1, b1, g, 1)
            _, (tend, _), (t1, f1) = read_control(dve, mybir.EngineType.DVE, PAIRS)
            with dve.If(f1 > 0):
                ff_route_and_3(t1)
            with dve.Fori(tend, TILES) as t:
                ch = Chain()
                ff_1(t, ch)
                ff_norm(t, ch)
                ff_route(t, ch)
                ff_3(t)

            key, add_bits, rb = (sm[:, c:c + 1] for c in (52, 53, 54))
            key_i, add_i, cand_i = key.bitcast(i32), add_bits.bitcast(i32), cand.bitcast(i32)
            dve.wait_ge(s_wd, TILES)
            dve.memset(ones_m, 1.0)
            dve.memset(zer, 0.0)
            dve.tensor_scalar(sm[:, 56:57], tile_base[:, TILES - 1:TILES], 0.0, None, ALU.mult)
            link(dve.tensor_copy(lower, ident[:, :]))
            link(dve.tensor_tensor_scan(lower, ident[:, :], bc(zer[:, 0:1], [P, P]), 0.0, ALU.add, ALU.add))
            link(dve.tensor_tensor(lower, lower, ident[:, :], ALU.subtract))
            link(dve.tensor_scalar(sm[:, 57:58], lower[:, LAST:LAST + 1], 1.0, 3.0e38, ALU.subtract, ALU.mult))
            link(dve.tensor_tensor(wts[:, TILES - 1:TILES], wts[:, TILES - 1:TILES], lower[:, LAST:LAST + 1], ALU.mult))
            link(dve.tensor_tensor(wts[:, TILES - 1:TILES], wts[:, TILES - 1:TILES], sm[:, 57:58], ALU.add))
            link(dve.memset(part, 0.0))
            for i, (b, n) in enumerate(ROUNDS):
                for c in range((1 << n) - 1):
                    dve.memset(steps_of[:, i, c:c + 1].bitcast(i32), (c + 1) << b)
            link(dve.memset(key_i, 0))
            link(dve.tensor_scalar(eq, wts[:, :], 0.0, 0.0, ALU.is_ge, ALU.add, accum_out=part[:, 0:1]))
            dve.sem_inc(s_part, 1)
            dve.wait_ge(s_cnt, 1)
            link(dve.tensor_scalar(sm[:, 55:56], bank[2][:, 0:1], float(KSEL), None, ALU.is_ge))
            link(dve.tensor_scalar(sm[:, 58:59], sm[:, 55:56], 2.0, -1.0, ALU.mult, ALU.add))
            link(dve.tensor_scalar(sm[:, 56:57], sm[:, 55:56], float(KSEL - (N - KSEL + 1)), float(N - KSEL + 1),
                                   ALU.mult, ALU.add))
            link(dve.tensor_scalar(ws, wts[:, :], sm[:, 58:59], None, ALU.mult))
            link(dve.tensor_tensor(ws[:, TILES - 1:TILES], ws[:, TILES - 1:TILES], lower[:, LAST:LAST + 1], ALU.mult))
            link(dve.tensor_tensor(ws[:, TILES - 1:TILES], ws[:, TILES - 1:TILES], sm[:, 57:58], ALU.add))
            for i, (b, n) in enumerate(ROUNDS):
                m = (1 << n) - 1
                link(dve.tensor_tensor(cand_i[:, 0:m], steps_of[:, i, 0:m].bitcast(i32), bc(key_i, [P, m]),
                                       ALU.bitwise_or))
                link(dve.tensor_tensor(reach[:, 0:m, :], bc(ws.rearrange("p (a t) -> p a t", a=1), [P, m, TILES]),
                                       bc(cand[:, 0:m].rearrange("p (c a) -> p c a", a=1), [P, m, TILES]),
                                       ALU.is_ge))
                dve.tensor_reduce(part[:, 0:m], reach[:, 0:m, :], AX.X, ALU.add).then_inc(s_part, 1)
                dve.wait_ge(s_cnt, i + 2)
                link(dve.tensor_scalar(cand[:, 0:m], bank[2][:, 0:m], sm[:, 56:57], 0.0, ALU.is_ge, ALU.add,
                                       accum_out=rb))
                link(dve.tensor_scalar(add_i, rb, float(1 << b), None, ALU.mult))
                link(dve.tensor_tensor(key_i, key_i, add_i, ALU.bitwise_or))
            link(dve.tensor_scalar(key, key, sm[:, 58:59], None, ALU.mult))
            thr = key
            link(dve.tensor_scalar(gt, wts[:, :], thr, 0.0, ALU.is_gt, ALU.add, accum_out=sm[:, 51:52]))
            link(dve.memset(colsum, 0.0))
            link(dve.tensor_scalar(eq, wts[:, :], thr, None, ALU.is_equal))
            dve.sem_inc(s_part, 1)
            dve.wait_ge(s_cnt, 2 + len(ROUNDS))
            link(dve.tensor_copy(colsum, bank[2][:, 0:TILES]))
            link(dve.tensor_tensor_scan(before, colsum, zer, 0.0, ALU.add, ALU.add))
            link(dve.tensor_tensor(before, before, colsum, ALU.subtract))
            link(dve.tensor_tensor(before, before, bank[3][:, 0:TILES], ALU.add))
            link(dve.tensor_scalar(sm[:, 59:60], bank[4][:, 0:1], -1.0, float(KSEL), ALU.mult, ALU.add))
            link(dve.scalar_tensor_tensor(selw, before, sm[:, 59:60], eq, ALU.is_lt, ALU.mult))
            link(dve.tensor_tensor(selw, selw, gt, ALU.add))
            for i in range(STEPS):
                dve.wait_ge(s_tl[i % SLOTS], 16 * (i // SLOTS + 1))
                for j in range(HG):
                    t = i * HG + j
                    last = dve.scalar_tensor_tensor(tail[:, i % SLOTS, j, :], xs[:, t, :], selw[:, t:t + 1],
                                                    tail[:, i % SLOTS, j, :], ALU.mult, ALU.add)
                last.then_inc(s_tf, 1)


_INS = ['x', 'src', 'dst', 'L0_gnn_W1', 'L0_gnn_b1', 'L0_gnn_W2', 'L0_gnn_b2', 'L0_mix_W_qk', 'L0_mix_b_qk',
        'L0_mix_W_v', 'L0_mix_b_v', 'L0_mix_gamma', 'L0_mix_beta', 'L0_ffn_attention_mask', 'L0_ffn_wr', 'L0_ffn_br',
        'L0_ffn_w1', 'L0_ffn_b1', 'L0_ffn_w2', 'L0_ffn_b2']
_OUTS = [((12500, 256), 'float32')]


def kernel(**inputs):
    import numpy as _np
    import concourse.bacc as _bacc
    from concourse import mybir as _mybir
    from concourse.bass_utils import run_bass_kernel_spmd as _run

    nc = _bacc.Bacc("TRN2", target_bir_lowering=False, num_devices=1, dynamic_dma_scratch_size=8192)
    arrays, args = {}, []
    for name in _INS:
        a = _np.ascontiguousarray(inputs[name])
        arrays[f"in_{name}_dram"] = a
        args.append(nc.dram_tensor(f"in_{name}_dram", a.shape, _mybir.dt.from_np(a.dtype), kind="ExternalInput").ap())
    for i, (shape, dtype) in enumerate(_OUTS):
        dt = _mybir.dt.from_np(_np.dtype(dtype))
        args.append(nc.dram_tensor(f"out_{i}_dram", shape, dt, kind="ExternalOutput").ap())
    gps_layer_kernel(nc, *args)
    r = _run(nc, [arrays], core_ids=[0])
    got = tuple(r.results[0][f"out_{i}_dram"] for i in range(len(_OUTS)))
    return got[0]
```

```python
import concourse.bass as bass
from concourse import mybir
from contextlib import ExitStack
import math


def gps_layer_kernel(nc, x, src, dst, W1, b1, W2, b2, W_qk, b_qk, W_v, b_v, gamma, beta, attention_mask, wr, br,
                     w1, fb1, w2, fb2, out):
    f32, bf16, i32, i16 = mybir.dt.float32, mybir.dt.bfloat16, mybir.dt.int32, mybir.dt.int16
    ALU, ACT, AX = mybir.AluOpType, mybir.ActivationFunctionType, mybir.AxisListType
    ds = bass.ds

    P = 128
    N, D = x.shape
    F = W1.shape[1]
    HID = w1.shape[1]
    E = src.shape[0]
    TILES = math.ceil(N / P)
    LAST = N - (TILES - 1) * P
    KD, KH = D // P, HID // P
    HALF = 8
    PAIR = 2 * HALF
    PAIRS = 4 * math.ceil(math.ceil(E / (PAIR * P)) / 4)
    WIN = 3
    SUB = 32
    SUBS = P // SUB
    UNIT = 2
    OH_BUFS = 4
    XN_BUFS = 4
    SETS = 4
    ROW = PAIR * P
    CHUNKS = PAIRS * PAIR
    EDGES_IN_LAST = E - (PAIRS - 1) * ROW
    PAD_NODE = TILES * P - 1
    GROUP = 14
    GROUPS = TILES // GROUP
    DEG_GROUPS = 4
    UNITS = PAIRS // UNIT // DEG_GROUPS
    KSEL = max(1, int(0.5 * N)) - 1
    EPS = 1e-5
    assert D == KD * P and F == P and HID == KH * P and GROUPS * GROUP == TILES and PAIRS <= P
    assert DEG_GROUPS * UNITS * UNIT == PAIRS and 1 < DEG_GROUPS < GROUPS - 2
    assert GROUP % XN_BUFS == 2 and 3 < UNITS < GROUP and UNITS % OH_BUFS == 1
    assert 0 < EDGES_IN_LAST <= ROW and PAD_NODE >= N

    ctx = ExitStack()
    with ctx:
        def sb(name, shape, dt=f32):
            return ctx.enter_context(nc.sbuf_tensor(name, shape, dt))

        def sem(name):
            return ctx.enter_context(nc.semaphore(name))

        table = [nc.dram_tensor(f"table{i}", [TILES * P, F], f32).ap() for i in range(2)]
        base_rows = nc.dram_tensor("base_rows", [TILES * P, D], f32).ap()

        xs = sb("xs", [P, TILES, D])
        acc = sb("acc", [P, TILES, F])
        src_idx = sb("src_idx", [P, CHUNKS + 2 * PAIR], i16)
        dst_of = sb("dst_of", [P, CHUNKS], i16)
        idx_now = sb("idx_now", [P, SETS, PAIR], i32)
        ident = sb("ident", [P, P])
        iota_n = sb("iota_n", [P, P])
        tile_base = sb("tile_base", [P, TILES])
        rstd = sb("rstd", [P, TILES])
        nmr = sb("nmr", [P, TILES])
        dinv = sb("dinv", [P, TILES])
        wts = sb("wts", [P, TILES])
        ctl = sb("ctl", [1, PAIRS + 1, 4], i32)
        gW1 = sb("gW1", [P, KD, F])
        gW2 = sb("gW2", [P, D])
        Pmix = sb("Pmix", [P, KD, D])
        crow = sb("crow", [P, D])
        b1row = sb("b1row", [P, F])
        wrrow = sb("wrrow", [P, D])
        fb2row = sb("fb2row", [P, D])
        fb1col = sb("fb1col", [P, KH])
        brcol = sb("brcol", [P, 1])
        wide = sb("wide", [1, 1], i32)
        epscol = sb("epscol", [P, 1])
        drel = sb("drel", [P, 2, HALF])
        sm = sb("sm", [P, 64])

        ARENA = 12160
        arena = sb("arena", [P, ARENA])
        at = [0]

        def carve(*dims, dt=f32, start=None):
            if start is not None:
                at[0] = start
            n = math.prod(dims)
            words = n if dt != bf16 else n // 2
            v = arena[:, at[0]:at[0] + words]
            at[0] += words
            assert at[0] <= ARENA, at[0]
            if dt != f32:
                v = v.bitcast(dt)
            names = " ".join("abcd"[:len(dims)])
            sizes = {"abcd"[i]: dims[i] for i in range(len(dims))}
            return v if len(dims) == 1 else v.rearrange(f"p ({names}) -> p {names}", **sizes)

        oh_r = carve(OH_BUFS, UNIT * PAIR, SUB, dt=bf16, start=0)
        oh_q = carve(OH_BUFS, UNIT * PAIR, SUBS * WIN, dt=bf16)
        wide_r = carve(2, HALF, SUB, dt=bf16, start=0)
        wide_q = carve(2, HALF, SUBS * TILES, dt=bf16)
        r_of = carve(CHUNKS)
        q_of = carve(CHUNKS)
        q_rel = carve(CHUNKS)
        xnA = carve(XN_BUFS, D)
        xTA = carve(2, D)
        zeros_b = carve(SUBS * (TILES + WIN), dt=bf16)
        cols_row = carve(PAIRS // UNIT)[0:1, :].bitcast(i32)
        ones_row = carve(P)[0:1, :]
        ring = carve(2 * PAIR, F, start=0)
        S = carve(2, HALF, P)
        after_S = at[0]
        Wk = carve(KD, D)
        Wv = carve(KD, D)
        Wq = carve(KD, D)
        WqT = carve(KD, D)
        xn = carve(D)
        xT = carve(KD, P)
        ET = carve(KD, P)
        En = carve(KD, P)
        Gs = carve(KD, D)
        GT = carve(KD, D)
        lam = carve(KD, D)
        bvrow = carve(D)
        bqb = carve(KD, P)
        fw1 = carve(KD, HID, start=after_S)
        fw2 = carve(KH, D)
        xnD = gW1[:, :, :].rearrange("p k f -> p (k f)")
        x1 = carve(D)
        ln = carve(D)
        base = carve(D)
        aggs = carve(F)
        H = carve(KH, P)
        T3 = H[:, KH - 3:KH, :]
        ones_m = carve(P, start=0)
        lower = carve(P)
        gt = carve(TILES)
        eq = carve(TILES)
        colsum = carve(TILES)
        BITS = 3
        CAND = (1 << BITS) - 1
        ROUNDS = [(b, min(BITS, 31 - b)) for b in range(0, 31, BITS)][::-1]
        part = carve(CAND)
        cand = carve(CAND)
        steps_of = carve(len(ROUNDS), CAND)
        reach = carve(CAND, TILES)
        ws = carve(TILES)
        before = carve(TILES)
        selw = carve(TILES)
        zer = carve(TILES)
        selection_end = at[0]
        accf = acc[:, :, :].rearrange("p t f -> p (t f)")
        src_rows_i = accf[:, 0:ROW].bitcast(i32)
        src_rows = accf[:, ROW:2 * ROW]
        dst_rows_i = accf[:, 2 * ROW:3 * ROW].bitcast(i32)
        dst_rows = accf[:, 3 * ROW:4 * ROW]
        HG = GROUP // 2
        STEPS = TILES // HG
        acc_slots = TILES * F // (HG * D)
        arena_slots = (ARENA - selection_end) // (HG * D)
        SLOTS = acc_slots + arena_slots
        in_acc = accf.rearrange("p (s j d) -> p s j d", s=acc_slots, j=HG)
        in_arena = arena[:, ARENA - arena_slots * HG * D:ARENA].rearrange("p (s j d) -> p s j d", s=arena_slots, j=HG)
        slots = [in_acc[:, i] for i in range(acc_slots)] + [in_arena[:, i] for i in range(arena_slots)]
        rng = sm[:, 0:4]
        rng_i = sb("rng_i", [P, 4], i32)
        rrow = accf[0:1, 4 * ROW:4 * ROW + 20 * PAIRS].rearrange("p (r n) -> p r n", r=10)
        low_row = rrow[:, 5, PAIRS:2 * PAIRS]
        low_of = carve(PAIRS, start=ARENA - PAIRS)
        steps32 = carve(SUBS * TILES, start=ARENA - PAIRS - SUBS * TILES)
        stats = sb("stats", [P, 6])
        stats2 = sb("stats2", [P, 2, 6])
        mv = sb("mv", [P, 2])
        statsA = sb("statsA", [P, GROUP, 6])
        mean2 = sb("mean2", [P, GROUP])
        ssq = sb("ssq", [P, GROUP])
        dif = sb("dif", [P, GROUP])

        bank = [ctx.enter_context(nc.psum_tensor(f"bank{i}", [P, 512], f32)) for i in range(8)]
        visit_sum = [bank[0], bank[1]]
        pT, pK, pE, pG = bank[2], bank[3], bank[4], bank[5]
        pY1, pY = bank[3], bank[4]
        pH = [bank[5], bank[6]]
        pDeg = bank[7]

        s_tail_zero = sem("x_tail_zeroed")
        s_xtail = sem("x_tail_loaded")
        s_x = sem("x_group_loaded")
        s_pad = sem("edge_padding_set")
        s_edges = sem("edges_loaded")
        s_small = sem("small_inputs_loaded")
        s_const = sem("constants_made")
        s_rowsf = sem("edge_rows_as_float")
        s_eT = sem("edges_transposed")
        s_eTe = sem("transposed_edges_evacuated")
        s_rngdone = sem("ranges_ready")
        s_rngT = sem("ranges_transposed")
        s_rcpA = sem("x_reciprocal_chain")
        s_mvA = sem("x_stats_ready")
        s_sdA = sem("x_deviation_ready")
        s_rstd = sem("x_rstd_ready")
        s_xrA = sem("scaled_x_first_pass")
        s_xnA = [sem(f"xn_ready_first_pass{i}") for i in range(2)]
        s_TA = sem("xn_transposed_first_pass")
        s_TAe = sem("xnT_evacuated_first_pass")
        s_hA = sem("h1_ready")
        s_hAe = sem("h1_evacuated")
        s_oh = sem("one_hots_ready")
        s_ohu = sem("one_hots_used")
        s_zero = sem("zeros_made")
        s_deg = sem("degrees_summed")
        s_low = sem("first_columns_broadcast")
        s_win = sem("windows_ready")
        s_sq = sem("sqrt_degrees_ready")
        s_scaled = sem("table1_tiles_ready")
        s_tab1 = sem("table1_written")
        s_ctl = sem("control_table_ready")
        s_idx = [sem(f"indices_ready{i}") for i in range(2)]
        s_issue = sem("gathers_issued")
        s_dve = sem("vector_chain")
        s_bn = sem("x_stats_chain")
        s_passed_sp = sem("group_waits_passed")
        s_passed = sem("waits_passed")
        s_free = [sem(f"ring_half_free{i}") for i in range(2)]
        s_gath = [[sem(f"gathered{i}_{h}") for h in range(4)] for i in range(2)]
        s_drel = [[sem(f"relative_dst{i}_{h}") for h in range(2)] for i in range(2)]
        s_S = [[[sem(f"S_ready{i}_{h}_{q}") for q in range(2)] for h in range(2)] for i in range(2)]
        s_Su = [[sem(f"S_half_free{i}_{h}") for h in range(2)] for i in range(2)]
        s_sum = [[sem(f"visit_summed{i}_{h}") for h in range(2)] for i in range(2)]
        s_fl = [[sem(f"visits_added{i}_{h}") for h in range(2)] for i in range(2)]
        s_fin = sem("table2_tile_ready")
        s_fin0 = sem("table2_tile_biased")
        s_tab2 = sem("table2_written")
        s_mxn = sem("mix_xn_ready")
        s_mT = sem("mix_xn_transposed")
        s_mTe = sem("mix_xnT_evacuated")
        s_mK = sem("mix_keys_ready")
        s_mch = sem("mix_max_chain")
        s_mb = sem("mix_bias_ready")
        s_mE = sem("mix_exps_ready")
        s_mET = sem("mix_exps_transposed")
        s_mEe = sem("mix_exps_evacuated")
        s_mG = sem("mix_sums_ready")
        s_mu = sem("mix_sums_added")
        s_mch2 = sem("mix_sum_chain")
        s_mz = sem("mix_weights_loaded")
        s_m1, s_m2, s_m3 = sem("lambda_pe"), sem("lambda_evacuated"), sem("lambda_dve")
        s_mixed = sem("mixer_folded")
        s_fw = sem("ff_weights_loaded")
        s_aggs = sem("agg_scaled")
        s_dxn = sem("ff_xn_ready")
        s_dT = sem("ff_first_transposed")
        s_dTe = sem("ff_first_evacuated")
        s_y1 = sem("mixed_rows_ready")
        s_dch = sem("ff_vector_chain")
        s_var = sem("ff_variance_ready")
        s_sd = sem("ff_deviation_ready")
        s_ln = sem("ff_ln_ready")
        s_lT = sem("ff_ln_transposed")
        s_lTe = sem("ff_lnT_evacuated")
        s_h = sem("ff_hidden_halves_ready")
        s_H = sem("ff_gelu_halves_ready")
        s_y = sem("ff_rows_ready")
        s_yb = sem("ff_rows_biased")
        s_base = sem("base_rows_ready")
        s_basew = sem("base_rows_written")
        s_wd = sem("weighted_rows_ready")
        s_part = sem("selection_partials")
        s_cnt = sem("selection_counts")
        s_tl = [sem(f"base_back{i}") for i in range(SLOTS)]
        s_to = [sem(f"sums_out{i}") for i in range(SLOTS)]
        s_tf = sem("tail_rows_ready")

        block = ctx.enter_context(nc.Block())

        x_tiles = x[0:(TILES - 1) * P, :].rearrange("(t p) d -> p t d", p=P)
        base_t = base_rows.rearrange("(t p) d -> p t d", p=P)
        table_t = [t.rearrange("(t p) f -> p t f", p=P) for t in table]
        out_t = out[0:(TILES - 1) * P, :].rearrange("(t p) d -> p t d", p=P)

        def row(ap, n=P):
            return ap.rearrange("(a n) -> a n", a=1).broadcast_to([n, ap.shape[0]])

        def bc(ap, shape):
            return ap.broadcast_to(shape)

        def read_control(eng, engine_type, g):
            _, words = nc.values_load_multi_w_load_instructions(
                ctl[0:1, ds(g, 1), 0:3].rearrange("p a c -> p (a c)"), engines=[engine_type], min_val=0,
                max_val=(1 << 31) - 1)
            words = [eng.snap(w) for w in words]

            def within(value, least, most):
                return eng.snap(nc.s_assert_within(
                    value, least, most, skip_runtime_bounds_check_because="the kernel's own control table holds no other"))

            batches = []
            for w in words[0:2]:
                lo = within((w >> 16) & 0xFF, 0, TILES - 1)
                hi = within(w >> 24, 1, TILES)
                batches.append((lo, hi, eng.snap(w & 0xFFFF)))
            rel = words[2]
            t0 = within(rel & 0x7F, 0, TILES - 1)
            f0 = eng.snap((rel >> 7) & 1)
            t1 = within((rel >> 8) & 0x7F, 0, TILES - 1)
            f1 = eng.snap((rel >> 15) & 1)
            return batches, (t0, f0), (t1, f1)

        @block.sync
        def _(sp):
            sp.wait_ge(s_pad, 2)
            full = (PAIRS - 1) * ROW
            for rows_i, e in ((dst_rows_i, dst), (src_rows_i, src)):
                sp.dma_start(rows_i[0:PAIRS - 1, :], e[0:full].rearrange("(p e) -> p e", e=ROW)).then_inc(s_edges, 16)
                sp.dma_start(rows_i[PAIRS - 1:PAIRS, 0:EDGES_IN_LAST],
                             e[full:E].rearrange("(a e) -> a e", a=1)).then_inc(s_edges, 16)
            sp.wait_ge(s_tail_zero, 1)
            sp.dma_start(xs[0:LAST, TILES - 1, :], x[(TILES - 1) * P:N, :]).then_inc(s_xtail, 16)
            with sp.Fori(0, GROUPS - 1) as g:
                sp.dma_start(xs[:, ds(g * GROUP, GROUP), :], x_tiles[:, ds(g * GROUP, GROUP), :]).then_inc(s_x, 16)
                sp.wait_ge(s_x, g * 16 + 16)
                sp.sem_inc(s_passed_sp, 1)
            sp.dma_start(xs[:, TILES - GROUP:TILES - 1, :],
                         x_tiles[:, TILES - GROUP:TILES - 1, :]).then_inc(s_x, 16)
            with sp.Fori(0, GROUPS) as g:
                sp.wait_ge(s_scaled, g + 1)
                sp.dma_start(table_t[0][:, ds(g * GROUP, GROUP), :], acc[:, ds(g * GROUP, GROUP), :]).then_inc(s_tab1, 16)
            with sp.Fori(0, TILES) as t:
                sp.wait_ge(s_fin, t + 1)
                sp.dma_start(table_t[1][:, ds(t, 1), :], acc[:, ds(t, 1), :]).then_inc(s_tab2, 16)
            sp.wait_ge(s_mixed, 1)
            sp.dma_start(fw1, w1.rearrange("(k p) h -> p k h", p=P)).then_inc(s_fw, 16)
            sp.dma_start(fw2, w2.rearrange("(k p) d -> p k d", p=P)).then_inc(s_fw, 16)
            sp.sem_inc(s_basew, 16)
            with sp.Fori(0, TILES) as t:
                sp.wait_ge(s_base, t + 1)
                sp.dma_start(base_t[:, ds(t, 1), :], base.rearrange("p (a d) -> p a d", a=1)).then_inc(s_basew, 16)
            sp.wait_ge(s_basew, 16 * (TILES + 1))
            sp.wait_ge(s_wd, TILES)

            def load_base(i):
                if i >= SLOTS:
                    sp.wait_ge(s_to[i % SLOTS], 16)
                sp.dma_start(slots[i % SLOTS], base_t[:, i * HG:(i + 1) * HG, :]).then_inc(s_tl[i % SLOTS], 16)

            for i in range(SLOTS):
                load_base(i)
            for j in range(STEPS):
                sp.wait_ge(s_tf, j + 1)
                if j < STEPS - 1:
                    sp.dma_start(out_t[:, j * HG:(j + 1) * HG, :], slots[j % SLOTS])\
                      .then_inc(s_to[j % SLOTS], 16)
                else:
                    sp.dma_start(out_t[:, j * HG:TILES - 1, :], slots[j % SLOTS][:, 0:HG - 1, :])\
                      .then_inc(s_to[j % SLOTS], 16)
                    sp.dma_start(out[(TILES - 1) * P:N, :], slots[j % SLOTS][0:LAST, HG - 1, :])\
                      .then_inc(s_to[j % SLOTS], 16)
                if 2 <= j and j - 2 + SLOTS < STEPS:
                    load_base(j - 2 + SLOTS)
            for i in range(SLOTS):
                steps_here = len(range(i, STEPS, SLOTS))
                sp.wait_ge(s_to[i], 16 * (steps_here + (i == (STEPS - 1) % SLOTS)))

        @block.gpsimd
        def _(pool):
            pool.memset(dst_rows_i[0:PAIRS, EDGES_IN_LAST:ROW], PAD_NODE).then_inc(s_pad, 1)
            pool.memset(src_rows_i[0:PAIRS, EDGES_IN_LAST:ROW], 0).then_inc(s_pad, 1)
            pool.memset(xs[:, TILES - 1, :], 0.0).then_inc(s_tail_zero, 1)
            pool.memset(ident[:, :], 0.0).then_inc(s_issue, 1)
            pool.wait_ge(s_issue, 1)
            pool.affine_select(out=ident[:, :], in_=ident[:, :], compare_op=ALU.not_equal, fill=1.0, base=0,
                               pattern=[[-1, P]], channel_multiplier=1).then_inc(s_const, 1)
            pool.iota(iota_n[:, :], [[1, P]], base=0, channel_multiplier=0,
                      allow_small_or_imprecise_dtypes=True).then_inc(s_const, 1)
            pool.iota(steps32, [[1, SUBS * TILES]], base=0, channel_multiplier=0,
                      allow_small_or_imprecise_dtypes=True).then_inc(s_const, 1)
            pool.iota(tile_base[:, :], [[P, TILES]], base=0, channel_multiplier=0,
                      allow_small_or_imprecise_dtypes=True).then_inc(s_const, 1)
            pool.memset(src_idx[:, CHUNKS:CHUNKS + 2 * PAIR], 0).then_inc(s_const, 1)

            def xn_of_group(g, first):
                pool.wait_ge(s_rstd, g + 1)
                for j in range(0, GROUP, 2):
                    n = g * GROUP + j
                    if not (first and j < XN_BUFS):
                        pool.wait_ge(s_TA, n - (1 if j < 2 else XN_BUFS - 1))
                    pool.tensor_tensor(xnA[:, j % XN_BUFS, :], xs[:, ds(n, 1), :].rearrange("p a d -> p (a d)"),
                                       bc(rstd[:, ds(n, 1)], [P, D]), ALU.mult).then_inc(s_xrA, 1)
                    pool.wait_ge(s_xrA, g * (GROUP // 2) + (j // 2 + 1))
                    pool.tensor_tensor(xnA[:, j % XN_BUFS, :], xnA[:, j % XN_BUFS, :], bc(nmr[:, ds(n, 1)], [P, D]),
                                       ALU.add).then_inc(s_xnA[0], 1)

            xn_of_group(0, True)
            with pool.Fori(1, GROUPS) as g:
                xn_of_group(g, False)

            def gather_layer(layer):
                with pool.Fori(0, PAIRS // SETS) as gg:
                    for i in range(SETS):
                        pool.wait_ge(s_idx[layer], gg * SETS + (i + 1))
                        pool.sem_inc(s_issue, 1)
                        for h in range(2):
                            pool.wait_ge(s_free[layer], gg * (2 * SETS) + (2 * i + h + 1))
                            pool.sem_inc(s_issue, 1)
                            quarter = 2 * (i % 2) + h
                            for k in range(HALF):
                                c = h * HALF + k
                                pool.indirect_dma_start(
                                    ring[:, quarter * HALF + k, :], None, table[layer],
                                    bass.IndirectOffsetOnAxis(ap=idx_now[:, i, c:c + 1], axis=0),
                                ).then_inc(s_gath[layer][quarter], 16)

            pool.wait_ge(s_tab1, 16 * GROUPS)
            gather_layer(0)
            pool.wait_ge(s_tab2, 16 * TILES)
            gather_layer(1)

        @block.scalar
        def _(act):
            act.dma_start(gW1[:, :, :], W1.rearrange("(k p) f -> p k f", p=P)).then_inc(s_small, 16)
            act.dma_start(gW2[:, :], W2).then_inc(s_small, 16)
            act.dma_start(b1row[:, :], row(b1)).then_inc(s_small, 16)
            act.dma_start(crow[:, :], row(b2)).then_inc(s_small, 16)
            act.dma_start(wrrow[:, :], row(wr.rearrange("d o -> (d o)"))).then_inc(s_small, 16)
            act.dma_start(fb2row[:, :], row(fb2)).then_inc(s_small, 16)
            act.dma_start(brcol[:, :], row(br)).then_inc(s_small, 16)
            with nc.allow_non_contiguous_dma("per-partition biases"):
                act.dma_start(fb1col[:, :], fb1.rearrange("(k p) -> p k", p=P)).then_inc(s_small, 16)
                act.dma_start(sm[:, 8:10], gamma.rearrange("(k p) -> p k", p=P)).then_inc(s_small, 16)
                act.dma_start(sm[:, 10:12], beta.rearrange("(k p) -> p k", p=P)).then_inc(s_small, 16)
                act.dma_start(sm[:, 12:14], b_qk[0, :].rearrange("(k p) -> p k", p=P)).then_inc(s_small, 16)
                act.dma_start(sm[:, 14:16], b_qk[1, :].rearrange("(k p) -> p k", p=P)).then_inc(s_small, 16)
            for e in range(2):
                for b in range(PAIR // 4):
                    i = e * (PAIR // 4) + b
                    act.wait_ge(s_eT, i + 1)
                    view = bank[i % 2][:, 0:4 * PAIRS].rearrange("p (c g) -> p g c", g=PAIRS)
                    to = (dst_of if e == 0 else src_idx)[:, 0:CHUNKS].rearrange("p (g c) -> p g c", c=PAIR)
                    act.activation(to[:, :, 4 * b:4 * b + 4], view, ACT.Copy).then_inc(s_eTe, 1)

            def tile_a(g, j, first):
                n = g * GROUP + j
                if not (first and j < XN_BUFS):
                    act.wait_ge(s_TA, n - (1 if j < 2 else XN_BUFS - 1))
                act.activation(xnA[:, j % XN_BUFS, :], xs[:, ds(n, 1), :].rearrange("p a d -> p (a d)"), ACT.Identity,
                               bias=nmr[:, ds(n, 1)], scale=rstd[:, ds(n, 1)]).then_inc(s_xnA[1], 1)

            def tile_b(g, j, first):
                n = g * GROUP + j
                act.wait_ge(s_TA, n + 1)
                if not (first and j < 2):
                    act.wait_ge(s_hA, n - 1)
                act.activation(xTA[:, j % 2, :], bank[2 + j % 2][:, 0:D], ACT.Copy).then_inc(s_TAe, 1)

            def tile_c(g, j):
                n = g * GROUP + j
                act.wait_ge(s_hA, n + 1)
                act.activation(acc[:, ds(n, 1), :].rearrange("p a d -> p (a d)"), bank[4 + j % 2][:, 0:F],
                               ACT.Copy).then_inc(s_hAe, 1)

            def deviations(g):
                act.wait_ge(s_mvA, g + 1)
                act.activation(rstd[:, ds(g * GROUP, GROUP)], ssq[:, :], ACT.Sqrt, bias=epscol[:, 0:1],
                               scale=1.0 / D).then_inc(s_sdA, 1)

            def group(g, first, last):
                act.wait_ge(s_rstd, g + 1)
                for j in range(GROUP + 1):
                    if j < GROUP and j % 2 == 0:
                        tile_a(g, j + 1, first)
                    if j < GROUP:
                        tile_b(g, j, first)
                    if j >= 1:
                        tile_c(g, j - 1)
                    if j == GROUP // 3 and not last:
                        deviations(g + 1)

            deviations(0)
            group(0, True, False)
            with act.Fori(1, DEG_GROUPS) as g:
                group(g, False, False)
            act.wait_ge(s_deg, 1)
            for j in range(SUBS):
                last = act.activation(dinv[j * SUB:(j + 1) * SUB, :], pDeg[0:SUB, j:SUBS * TILES:SUBS], ACT.Sqrt, bias=1.0)
            last.then_inc(s_sq, 1)
            with act.Fori(DEG_GROUPS, GROUPS - 1) as g:
                group(g, False, False)
            group(GROUPS - 1, False, True)

            act.wait_ge(s_tab1, 16 * GROUPS)
            act.dma_start(Wk, W_qk[1].rearrange("(k p) e -> p k e", p=P)).then_inc(s_mz, 16)
            act.dma_start(Wq, W_qk[0].rearrange("(k p) e -> p k e", p=P)).then_inc(s_mz, 16)
            act.dma_start(Wv, W_v.rearrange("(k p) e -> p k e", p=P)).then_inc(s_mz, 16)
            act.dma_start(bvrow, row(b_v)).then_inc(s_mz, 16)

            def mix(t, n):
                act.wait_ge(s_mG, t + 1)
                act.activation(xn, xs[:, ds(t, 1), :].rearrange("p a d -> p (a d)"), ACT.Identity,
                               bias=nmr[:, ds(t, 1)], scale=rstd[:, ds(t, 1)]).then_inc(s_mxn, 1)
                act.wait_ge(s_mT, t + 1)
                act.activation(xT.rearrange("p k n -> p (k n)"), pT[:, 0:D], ACT.Copy).then_inc(s_mTe, 1)
                act.wait_ge(s_mb, t + 1)
                act.activation(sm[:, 22:24], sm[:, 20:22], ACT.Exp)
                for k in range(KD):
                    last = act.activation(ET[:, k, 0:n], pK[:, k * P:k * P + n], ACT.Exp, bias=sm[:, 24 + k:25 + k],
                                          accum_out=sm[:, 26 + k:27 + k])
                last.then_inc(s_mE, 1)
                act.wait_ge(s_mET, t + 1)
                act.activation(En.rearrange("p k n -> p (k n)"), pE[:, 0:D], ACT.Copy).then_inc(s_mEe, 1)

            with act.Fori(0, TILES - 1) as t:
                mix(t, P)
            mix(TILES - 1, LAST)
            for i, (dsts, srcs) in enumerate(((GT, pT), (WqT, pK))):
                act.wait_ge(s_m1, i + 1)
                act.activation(dsts.rearrange("p k d -> p (k d)"), srcs[:, :], ACT.Copy).then_inc(s_m2, 1)
            act.wait_ge(s_m3, 2)
            act.activation(sm[:, 34:36], sm[:, 32:34], ACT.Sqrt, bias=epscol[:, 0:1]).then_inc(s_m2, 1)
            act.wait_ge(s_m1, 4)
            act.activation(Pmix[:, :, :].rearrange("p k d -> p (k d)"), pG[:, :], ACT.Copy).then_inc(s_m2, 1)

            act.wait_ge(s_mixed, 1)
            with act.Fori(0, TILES) as t:
                act.activation(xnD, xs[:, ds(t, 1), :].rearrange("p a d -> p (a d)"), ACT.Identity,
                               bias=nmr[:, ds(t, 1)], scale=rstd[:, ds(t, 1)]).then_inc(s_dxn, 1)
                act.wait_ge(s_dT, t + 1)
                act.activation(T3.rearrange("p k n -> p (k n)"), pT[:, 0:3 * P], ACT.Copy).then_inc(s_dTe, 1)
                act.wait_ge(s_var, t + 1)
                act.activation(sm[:, 40:41], mv[:, 1:2], ACT.Sqrt, bias=epscol[:, 0:1]).then_inc(s_sd, 1)
                act.wait_ge(s_lT, t + 1)
                act.activation(T3[:, 0:KD, :].rearrange("p k n -> p (k n)"), pT[:, 0:D], ACT.Copy).then_inc(s_lTe, 1)
                for half in range(2):
                    act.wait_ge(s_h, t * 2 + (half + 1))
                    for k in range(half * (KH // 2), (half + 1) * (KH // 2)):
                        last = act.activation(H[:, k, :], pH[half][:, (k % 4) * P:(k % 4 + 1) * P],
                                              ACT.Gelu_apprx_tanh, bias=fb1col[:, k:k + 1])
                    last.then_inc(s_H, 1)

        @block.tensor
        def _(pe):
            pe.wait_ge(s_const, 4)
            for e in range(2):
                pe.wait_ge(s_rowsf, e + 1)
                rows = (dst_rows, src_rows)[e]
                for b in range(PAIR // 4):
                    i = e * (PAIR // 4) + b
                    if i >= 2:
                        pe.wait_ge(s_eTe, i - 1)
                    for c in range(4):
                        k = 4 * b + c
                        last = nc.tensor.transpose(bank[i % 2][:, c * PAIRS:(c + 1) * PAIRS],
                                                   rows[0:PAIRS, k * P:(k + 1) * P], ident[0:PAIRS, 0:PAIRS])
                    last.then_inc(s_eT, 1)
            pe.wait_ge(s_rngdone, 1)
            for i in range(4):
                last = nc.tensor.transpose(bank[6][0:1, i * P:i * P + PAIRS], rng[0:PAIRS, i:i + 1],
                                           ident[0:PAIRS, 0:PAIRS])
            last.then_inc(s_rngT, 1)
            pe.wait_ge(s_zero, 1)
            nc.tensor.matmul(bank[6][:, 0:PAIRS], ones_row, low_row, start=True, stop=True)\
              .then_inc(s_low, 1)
            pe.wait_ge(s_small, 16 * 12)

            def transposes_a(g, j, first):
                n = g * GROUP + j
                pe.wait_ge(s_xnA[j % 2], g * (GROUP // 2) + (j // 2 + 1))
                if not (first and j < 2):
                    pe.wait_ge(s_TAe, n - 1)
                for k in range(KD):
                    last = nc.tensor.transpose(bank[2 + j % 2][:, k * P:(k + 1) * P],
                                               xnA[:, j % XN_BUFS, k * P:(k + 1) * P], ident[:, :])
                last.then_inc(s_TA, 1)

            def h1_a(g, j, first):
                n = g * GROUP + j
                pe.wait_ge(s_TAe, n + 1)
                if not (first and j < 2):
                    pe.wait_ge(s_hAe, n - 1)
                for k in range(KD):
                    last = nc.tensor.matmul(bank[4 + j % 2][:, 0:F], xTA[:, j % 2, k * P:(k + 1) * P], gW1[:, k, :],
                                            start=(k == 0), stop=(k == KD - 1))
                last.then_inc(s_hA, 1)

            def first_columns(g):
                _, words = nc.values_load_multi_w_load_instructions(
                    cols_row[0:1, ds(g * UNITS, UNITS)], engines=[mybir.EngineType.PE], min_val=0,
                    max_val=(1 << 31) - 1)
                cols = []
                for w in words:
                    w = pe.snap(w)
                    for col in (w & 0xFFFF, w >> 16):
                        cols.append(pe.snap(nc.s_assert_within(
                            pe.snap(col), 0, SUBS * (TILES - 1),
                            skip_runtime_bounds_check_because="the kernel's own table of columns holds no other")))
                return cols

            def degrees_of_unit(g, i, cols):
                pe.wait_ge(s_oh, g * UNITS + (i + 1))
                windows_of = [pDeg[0:SUB, ds(cols[i * UNIT + k], SUBS * WIN)] for k in range(UNIT)]
                for c in range(UNIT * PAIR):
                    last = nc.tensor.matmul(windows_of[c // PAIR], oh_r[:, i % OH_BUFS, c, :],
                                            oh_q[:, i % OH_BUFS, c, :], start=False, stop=False)
                last.then_inc(s_ohu, 1)

            def group(g, first, windows):
                for j in range(GROUP + 1):
                    if j < GROUP:
                        transposes_a(g, j, first)
                    if windows and j == 0:
                        cols = first_columns(g)
                    if j >= 1:
                        h1_a(g, j - 1, first)
                    if windows and j > GROUP - UNITS:
                        degrees_of_unit(g, j - 1 - (GROUP - UNITS), cols)

            def degrees_in_full(gg, first, last_gg):
                for par in range(2):
                    pe.wait_ge(s_oh, gg * 2 + par + 1)
                    for c in range(HALF):
                        last = nc.tensor.matmul(pDeg[0:SUB, 0:SUBS * TILES], wide_r[:, par, c, :], wide_q[:, par, c, :],
                                                start=(first and par == 0 and c == 0),
                                                stop=(last_gg and par == 1 and c == HALF - 1))
                    last.then_inc(s_ohu, 1)

            pe.wait_ge(s_win, 1)
            span = pe.value_load(wide[0:1, 0:1], min_val=0, max_val=TILES)
            with pe.If(span < WIN):
                nc.tensor.matmul(pDeg[0:SUB, 0:SUBS * (TILES + WIN)], zeros_b[:, 0:SUB], zeros_b, start=True, stop=False)
                group(0, True, True)
                with pe.Fori(1, DEG_GROUPS) as g:
                    group(g, False, True)
                nc.tensor.matmul(pDeg[0:SUB, 0:SUBS * (TILES + WIN)], zeros_b[:, 0:SUB], zeros_b, start=False,
                                 stop=True).then_inc(s_deg, 1)
            with pe.Else():
                group(0, True, False)
                with pe.Fori(1, DEG_GROUPS) as g:
                    group(g, False, False)
                degrees_in_full(0, True, False)
                with pe.Fori(1, PAIRS - 1) as gg:
                    degrees_in_full(gg, False, False)
                degrees_in_full(PAIRS - 1, False, True)
                pe.wait_ge(s_ohu, 2 * PAIRS)
                pe.sem_inc(s_deg, 1)
            with pe.Fori(DEG_GROUPS, GROUPS) as g:
                group(g, False, False)

            def visit(layer, batch, gg, quarter, t):
                v = batch[2] + t
                h = quarter % 2
                pe.wait_ge(s_gath[layer][quarter], gg * (16 * HALF) + 16 * HALF)
                pe.wait_ge(s_fl[layer][h], v + 1)
                for k in range(HALF):
                    q = k // 4
                    if k % 4 == 0:
                        pe.wait_ge(s_S[layer][h][q], v + 1)
                    last = nc.tensor.matmul(visit_sum[h][:, 0:F], S[:, h, k, :], ring[:, quarter * HALF + k, :],
                                            start=(k == 0), stop=(k == HALF - 1))
                    if k == 3:
                        last.then_inc(s_Su[layer][h], 1)
                last.then_inc(s_sum[layer][h], 1)

            def other_visits(layer, batch, gg, quarter):
                lo, hi, _ = batch
                with pe.If(hi > lo + 1):
                    with pe.Fori(lo + 1, hi) as t:
                        visit(layer, batch, gg, quarter, t)

            def mix_1(t):
                pe.wait_ge(s_mxn, t + 1)
                for k in range(KD):
                    last = nc.tensor.transpose(pT[:, k * P:(k + 1) * P], xn[:, k * P:(k + 1) * P], ident[:, :])
                last.then_inc(s_mT, 1)

            def mix_keys(t):
                pe.wait_ge(s_mTe, t + 1)
                for e in range(KD):
                    for k in range(KD):
                        last = nc.tensor.matmul(pK[:, e * P:(e + 1) * P], Wk[:, k, e * P:(e + 1) * P], xT[:, k, :],
                                                start=(k == 0), stop=(k == KD - 1))
                last.then_inc(s_mK, 1)

            def mix_2(t):
                pe.wait_ge(s_mE, t + 1)
                for k in range(KD):
                    last = nc.tensor.transpose(pE[:, k * P:(k + 1) * P], ET[:, k, :], ident[:, :])
                last.then_inc(s_mET, 1)

            def mix_3(t):
                pe.wait_ge(s_mEe, t + 1)
                for k in range(KD):
                    last = nc.tensor.matmul(pG[:, k * D:(k + 1) * D], En[:, k, :], xn, start=True, stop=True)
                last.then_inc(s_mG, 1)

            pe.wait_ge(s_ctl, 1)
            pe.wait_ge(s_mz, 16 * 4)
            pe.sem_inc(s_mG, 1)

            def pair_of_layer_1(gg, par, mixing):
                g = gg * 2 + par
                (b0, b1), _, _ = read_control(pe, mybir.EngineType.PE, g)
                if mixing:
                    mix_1(g)
                visit(0, b0, gg, 2 * par, b0[0])
                if mixing:
                    mix_keys(g)
                other_visits(0, b0, gg, 2 * par)
                visit(0, b1, gg, 2 * par + 1, b1[0])
                if mixing:
                    mix_2(g)
                other_visits(0, b1, gg, 2 * par + 1)
                if mixing:
                    mix_3(g)

            with pe.Fori(0, TILES // 2) as gg:
                for par in range(2):
                    pair_of_layer_1(gg, par, True)

            pe.wait_ge(s_m3, 1)
            for c in range(KD):
                for k in range(KD):
                    last = nc.tensor.transpose(pT[:, k * D + c * P:k * D + (c + 1) * P], Gs[:, c, k * P:(k + 1) * P],
                                               ident[:, :])
            last.then_inc(s_m1, 1)
            for c in range(KD):
                for k in range(KD):
                    last = nc.tensor.transpose(pK[:, c * D + k * P:c * D + (k + 1) * P], Wq[:, k, c * P:(c + 1) * P],
                                               ident[:, :])
            last.then_inc(s_m1, 1)
            pe.wait_ge(s_m2, 1)
            for c in range(KD):
                for k in range(KD):
                    last = nc.tensor.matmul(pE[:, c * D:(c + 1) * D], GT[:, k, c * P:(c + 1) * P], Wv[:, k, :],
                                            start=(k == 0), stop=(k == KD - 1))
            last.then_inc(s_m1, 1)

            for par in range(2):
                pair_of_layer_1(TILES // 2, par, False)
            pe.wait_ge(s_m3, 3)
            for k in range(KD):
                for c in range(KD):
                    last = nc.tensor.matmul(pG[:, k * D:(k + 1) * D], WqT[:, c, k * P:(k + 1) * P], lam[:, c, :],
                                            start=(c == 0), stop=(c == KD - 1))
            last.then_inc(s_m1, 1)
            for c in range(KD):
                last = nc.tensor.matmul(pT[:, 0:D], bqb[:, c, :], lam[:, c, :], start=(c == 0), stop=(c == KD - 1))
            last.then_inc(s_m1, 1)

            with pe.Fori(TILES // 2 + 1, PAIRS // 2) as gg:
                for par in range(2):
                    pair_of_layer_1(gg, par, False)

            pe.wait_ge(s_mixed, 1)
            pe.wait_ge(s_fw, 32)

            def ff_1(t):
                pe.wait_ge(s_dxn, t + 1)
                pe.wait_ge(s_aggs, t + 1)
                nc.tensor.transpose(pT[:, 0:P], aggs, ident[:, :])
                for k in range(KD):
                    last = nc.tensor.transpose(pT[:, (k + 1) * P:(k + 2) * P], xnD[:, k * P:(k + 1) * P], ident[:, :])
                last.then_inc(s_dT, 1)

            def ff_mixed(t):
                pe.wait_ge(s_dTe, t + 1)
                nc.tensor.matmul(pY1[:, 0:D], T3[:, 0, :], gW2[:, :], start=True, stop=False)
                for k in range(KD):
                    last = nc.tensor.matmul(pY1[:, 0:D], T3[:, k + 1, :], Pmix[:, k, :], start=False,
                                            stop=(k == KD - 1))
                last.then_inc(s_y1, 1)

            def ff_2(t):
                pe.wait_ge(s_ln, t + 1)
                for k in range(KD):
                    last = nc.tensor.transpose(pT[:, k * P:(k + 1) * P], ln[:, k * P:(k + 1) * P], ident[:, :])
                last.then_inc(s_lT, 1)

            def ff_hidden(t):
                pe.wait_ge(s_lTe, t + 1)
                for h in range(KH):
                    for k in range(KD):
                        last = nc.tensor.matmul(pH[h // 4][:, (h % 4) * P:(h % 4 + 1) * P],
                                                fw1[:, k, h * P:(h + 1) * P], T3[:, k, :],
                                                start=(k == 0), stop=(k == KD - 1))
                    if h % (KH // 2) == KH // 2 - 1:
                        last.then_inc(s_h, 1)

            def ff_3(t):
                for h in range(KH):
                    if h % (KH // 2) == 0:
                        pe.wait_ge(s_H, t * 2 + (h // (KH // 2) + 1))
                    last = nc.tensor.matmul(pY[:, 0:D], H[:, h, :], fw2[:, h, :], start=(h == 0), stop=(h == KH - 1))
                last.then_inc(s_y, 1)

            with pe.Fori(0, PAIRS // 2) as gg:
                for par in range(2):
                    g = gg * 2 + par
                    (b0, b1), (t0, f0), (t1, f1) = read_control(pe, mybir.EngineType.PE, g)
                    visit(1, b0, gg, 2 * par, b0[0])
                    with pe.If(f1 > 0):
                        ff_3(t1)
                    with pe.If(f0 > 0):
                        ff_1(t0)
                    other_visits(1, b0, gg, 2 * par)
                    with pe.If(f0 > 0):
                        ff_mixed(t0)
                    visit(1, b1, gg, 2 * par + 1, b1[0])
                    with pe.If(f0 > 0):
                        ff_2(t0)
                    other_visits(1, b1, gg, 2 * par + 1)
                    with pe.If(f0 > 0):
                        ff_hidden(t0)
            _, (tend, _), (t1, f1) = read_control(pe, mybir.EngineType.PE, PAIRS)
            with pe.If(f1 > 0):
                ff_3(t1)
            with pe.Fori(tend, TILES) as t:
                ff_1(t)
                ff_mixed(t)
                ff_2(t)
                ff_hidden(t)
                ff_3(t)

            for i in range(1 + len(ROUNDS)):
                pe.wait_ge(s_part, i + 1)
                nc.tensor.matmul(bank[2][:, 0:CAND], ones_m, part, start=True, stop=True).then_inc(s_cnt, 1)
            pe.wait_ge(s_part, 2 + len(ROUNDS))
            nc.tensor.matmul(bank[2][:, 0:TILES], ones_m, eq, start=True, stop=True)
            nc.tensor.matmul(bank[3][:, 0:TILES], lower, eq, start=True, stop=True)
            nc.tensor.matmul(bank[4][:, 0:1], ones_m, sm[:, 51:52], start=True, stop=True).then_inc(s_cnt, 1)

        @block.vector
        def _(dve):
            steps = [0]

            def link(ins):
                steps[0] += 1
                ins.then_inc(s_dve, 1)
                dve.wait_ge(s_dve, steps[0])

            dve.memset(epscol[:, :], EPS)
            dve.wait_ge(s_edges, 16 * 4)
            dve.tensor_copy(dst_rows[0:PAIRS, :], dst_rows_i[0:PAIRS, :]).then_inc(s_rowsf, 1)
            dve.wait_ge(s_rowsf, 1)
            dve.tensor_copy(src_rows[0:PAIRS, :], src_rows_i[0:PAIRS, :]).then_inc(s_rowsf, 1)
            halves = dst_rows[0:PAIRS, :].rearrange("p (h e) -> p h e", h=2)
            dve.tensor_reduce(rng[0:PAIRS, 0:2], halves, AX.X, ALU.min)
            link(dve.tensor_reduce(rng[0:PAIRS, 2:4], halves, AX.X, ALU.max))
            link(dve.tensor_copy(rng_i[0:PAIRS, :], rng[0:PAIRS, :]))
            link(dve.tensor_scalar(rng_i[0:PAIRS, :], rng_i[0:PAIRS, :], 7, None, ALU.arith_shift_right))
            dve.tensor_copy(rng[0:PAIRS, :], rng_i[0:PAIRS, :]).then_inc(s_rngdone, 1)

            dve.wait_ge(s_xtail, 16)

            def stats_of_group(g):
                dve.wait_ge(s_x, g * 16 + 16)
                for j in range(GROUP):
                    last = dve.bn_stats(statsA[:, j, :],
                                        xs[:, ds(g * GROUP + j, 1), :].rearrange("p a d -> p (a d)"))
                last.then_inc(s_bn, 1)
                dve.wait_ge(s_bn, g * 3 + 1)
                me, se, mo, so = (statsA[:, :, i] for i in (1, 2, 4, 5))
                dve.tensor_tensor(mean2[:, :], me, mo, ALU.add)
                dve.tensor_tensor(ssq[:, :], se, so, ALU.add)
                dve.tensor_tensor(dif[:, :], me, mo, ALU.subtract).then_inc(s_bn, 1)
                dve.wait_ge(s_bn, g * 3 + 2)
                dve.scalar_tensor_tensor(dif[:, :], dif[:, :], float(D) / 4, dif[:, :], ALU.mult, ALU.mult)\
                   .then_inc(s_bn, 1)
                dve.wait_ge(s_bn, g * 3 + 3)
                dve.tensor_tensor(ssq[:, :], ssq[:, :], dif[:, :], ALU.add).then_inc(s_mvA, 1)

            def scales_of_group(g):
                dve.wait_ge(s_sdA, g + 1)
                gs = ds(g * GROUP, GROUP)
                dve.reciprocal(rstd[:, gs], rstd[:, gs]).then_inc(s_rcpA, 1)
                dve.wait_ge(s_rcpA, g + 1)
                dve.scalar_tensor_tensor(nmr[:, gs], mean2[:, :], -0.5, rstd[:, gs],
                                         ALU.mult, ALU.mult).then_inc(s_rstd, 1)

            stats_of_group(0)
            dve.wait_ge(s_rngT, 1)
            lo_r, hi_r, cnt_r, zero_r, vin_r = (rrow[:, i, :] for i in range(5))
            m_r, done_r, one_r = rrow[:, 5, 0:PAIRS], rrow[:, 6, 0:PAIRS], rrow[:, 7, 0:PAIRS]
            rel_r = rrow[:, 8, 0:PAIRS + 2]
            flag_r = rrow[:, 9, 0:PAIRS + 2]
            wi = ctl[:, 0:PAIRS, 0:2]
            hi_i = rrow[:, 7, :].bitcast(i32).rearrange("p (g h) -> p g h", h=2)
            for h in range(2):
                dve.tensor_copy(lo_r.rearrange("p (g h) -> p g h", h=2)[:, :, h], bank[6][0:1, h * P:h * P + PAIRS])
                link(dve.tensor_copy(hi_r.rearrange("p (g h) -> p g h", h=2)[:, :, h],
                                     bank[6][0:1, (2 + h) * P:(2 + h) * P + PAIRS]))
            dve.memset(zero_r, 0.0)
            dve.memset(ones_row, 1.0)
            link(dve.memset(zeros_b, 0.0))
            lo2, hi2 = (r.rearrange("p (g h) -> p g h", h=2) for r in (lo_r, hi_r))
            most_r, span_r = rrow[:, 6, PAIRS:2 * PAIRS], rrow[:, 7, PAIRS:2 * PAIRS]
            dve.tensor_tensor(m_r, lo2[:, :, 0], lo2[:, :, 1], ALU.min)
            link(dve.tensor_tensor(most_r, hi2[:, :, 0], hi2[:, :, 1], ALU.max))
            link(dve.tensor_scalar(low_row, m_r, float(SUBS), None, ALU.mult))
            dve.sem_inc(s_zero, 1)
            low2 = low_row.rearrange("p (u k) -> p u k", k=UNIT)
            dve.scalar_tensor_tensor(cols_row, low2[:, :, 1], 65536.0, low2[:, :, 0], ALU.mult, ALU.add)
            link(dve.tensor_tensor(span_r, most_r, m_r, ALU.subtract))
            link(dve.tensor_reduce(sm[0:1, 60:61], span_r, AX.X, ALU.max))
            link(dve.tensor_copy(wide[:, :], sm[0:1, 60:61]))
            dve.sem_inc(s_win, 1)
            scales_of_group(0)
            dve.wait_ge(s_eTe, 4)
            r_i, q_i = r_of.bitcast(i32), q_of.bitcast(i32)
            link(dve.tensor_copy(r_i, dst_of[:, :]))
            link(dve.tensor_scalar(q_i, r_i, 5, None, ALU.arith_shift_right))
            link(dve.tensor_scalar(r_i, r_i, SUB - 1, None, ALU.bitwise_and))
            link(dve.tensor_copy(q_of, q_i))
            link(dve.tensor_copy(r_of, r_i))
            dve.wait_ge(s_const, 5)
            dve.wait_ge(s_low, 1)
            link(dve.tensor_copy(low_of, bank[6][:, 0:PAIRS]))
            link(dve.tensor_tensor(q_rel.rearrange("p (b k) -> p b k", k=PAIR),
                                   q_of.rearrange("p (b k) -> p b k", k=PAIR),
                                   bc(low_of.rearrange("p (b a) -> p b a", a=1), [P, PAIRS, PAIR]), ALU.subtract))

            def one_hots(kinds, cols, chunks):
                for to, of, width in kinds:
                    last = dve.tensor_tensor(
                        to, bc(steps32[:, 0:width].rearrange("p (a n) -> p a n", a=1), [P, chunks, width]),
                        bc(of[:, cols].rearrange("p (c a) -> p c a", a=1), [P, chunks, width]), ALU.is_equal)
                last.then_inc(s_oh, 1)

            def unit(g, i, first):
                if not (first and i < OH_BUFS):
                    dve.wait_ge(s_ohu, g * UNITS + (i if i == 0 else i - 3))
                one_hots(((oh_r[:, i % OH_BUFS], r_of, SUB), (oh_q[:, i % OH_BUFS], q_rel, SUBS * WIN)),
                         ds((g * UNITS + i) * (UNIT * PAIR), UNIT * PAIR), UNIT * PAIR)

            def in_full(gg, first):
                for par in range(2):
                    if not first:
                        dve.wait_ge(s_ohu, gg * 2 + par - 1)
                    one_hots(((wide_r[:, par], r_of, SUB), (wide_q[:, par], q_of, SUBS * TILES)),
                             ds(gg * PAIR + par * HALF, HALF), HALF)

            def group(g, first):
                for i in range(UNITS):
                    if i == (2 if first else 0):
                        stats_of_group(g + 1)
                    unit(g, i, first)
                    if i == UNITS - 3:
                        scales_of_group(g + 1)

            def control_table():
                link(dve.memset(one_r, 1.0))
                link(dve.scalar_tensor_tensor(cnt_r, hi_r, 1.0, lo_r, ALU.add, ALU.subtract))
                for h in range(2):
                    of_h = [r.rearrange("p (g h) -> p g h", h=2)[:, :, h] for r in (vin_r, cnt_r, zero_r)]
                    link(dve.tensor_tensor_scan(of_h[0], of_h[1], of_h[2], 0.0, ALU.add, ALU.add))
                link(dve.tensor_tensor_scan(done_r[:, ::-1], m_r[:, ::-1], m_r[:, ::-1], 1e9, ALU.min, ALU.min))
                link(dve.memset(rel_r, 0.0))
                link(dve.memset(ctl[:, :, :], 0))
                link(dve.tensor_tensor_scan(rel_r[:, 2:PAIRS + 2], one_r, done_r, 0.0, ALU.add, ALU.min))
                link(dve.memset(flag_r, 0.0))
                link(dve.tensor_tensor(flag_r[:, 0:PAIRS + 1], rel_r[:, 1:PAIRS + 2], rel_r[:, 0:PAIRS + 1], ALU.subtract))
                link(dve.tensor_tensor(vin_r, vin_r, cnt_r, ALU.subtract))
                link(dve.scalar_tensor_tensor(vin_r, vin_r, float(TILES), lo_r, ALU.add, ALU.subtract))
                link(dve.scalar_tensor_tensor(vin_r, lo_r, 65536.0, vin_r, ALU.mult, ALU.add))
                link(dve.tensor_copy(wi, vin_r.rearrange("p (g h) -> p g h", h=2)))
                link(dve.tensor_scalar(hi_i, hi_r.rearrange("p (g h) -> p g h", h=2), 1.0, None, ALU.add))
                link(dve.tensor_scalar(hi_i, hi_i, 24, None, ALU.logical_shift_left))
                link(dve.tensor_tensor(wi, wi, hi_i, ALU.bitwise_or))
                tmp_r = rrow[:, 3, 0:PAIRS + 2]
                done_w = rrow[:, 1, 0:PAIRS + 1]
                link(dve.scalar_tensor_tensor(tmp_r, flag_r, 128.0, rel_r, ALU.mult, ALU.add))
                link(dve.scalar_tensor_tensor(done_w, tmp_r[:, 0:PAIRS + 1], 256.0, tmp_r[:, 1:PAIRS + 2], ALU.mult,
                                              ALU.add))
                dve.tensor_copy(ctl[:, :, 2:3].rearrange("p g a -> p (g a)"), done_w).then_inc(s_ctl, 1)

            span = dve.value_load(wide[0:1, 0:1], min_val=0, max_val=TILES)
            links_before = steps[0]
            with dve.If(span < WIN):
                group(0, True)
                control_table()
                with dve.Fori(1, DEG_GROUPS) as g:
                    group(g, False)
            with dve.Else():
                steps[0] = links_before
                control_table()
                with dve.Fori(1, DEG_GROUPS + 1) as g:
                    stats_of_group(g)
                    scales_of_group(g)
                in_full(0, True)
                with dve.Fori(1, PAIRS) as gg:
                    in_full(gg, False)
            def scale(g):
                gs = slice(g * GROUP, (g + 1) * GROUP)
                dve.wait_ge(s_hAe, (g + 1) * GROUP)
                dve.tensor_tensor(acc[:, gs, :], acc[:, gs, :],
                                  bc(dinv[:, gs].rearrange("p (t a) -> p t a", a=1), [P, GROUP, F]),
                                  ALU.mult).then_inc(s_scaled, 1)

            stats_of_group(DEG_GROUPS + 1)
            dve.wait_ge(s_sq, 1)
            link(dve.reciprocal(dinv[:, :], dinv[:, :]))
            scaled = 0
            for g in range(DEG_GROUPS + 1, GROUPS):
                if g > DEG_GROUPS + 1:
                    stats_of_group(g)
                scale(scaled)
                scaled += 1
                scales_of_group(g)
            for g in range(scaled, GROUPS):
                scale(g)
            dve.wait_ge(s_eTe, 8)
            dve.tensor_copy(idx_now[:, 0:2, :], src_idx[:, 0:2 * PAIR].rearrange("p (a c) -> p a c", a=2))\
               .then_inc(s_idx[0], 2)
            dve.memset(sm[:, 16:18], -3.0e38)
            dve.memset(sm[:, 18:20], 0.0)
            link(dve.memset(Gs, 0.0))
            dve.wait_ge(s_tab1, 16 * GROUPS)
            for layer in range(2):
                for h in range(2):
                    dve.sem_inc(s_Su[layer][h], TILES + 1)
                    dve.sem_inc(s_fl[layer][h], TILES + 1)
                    for started in (s_S[layer][h][0], s_S[layer][h][1], s_sum[layer][h], s_drel[layer][h]):
                        dve.sem_inc(started, TILES)
                dve.sem_inc(s_free[layer], 4)

            def build(layer, batch, g, h, t):
                v = batch[2] + t
                dve.tensor_scalar(drel[:, h, :], dst_of[:, ds(g * PAIR + h * HALF, HALF)], tile_base[:, ds(t, 1)],
                                  None, ALU.subtract).then_inc(s_drel[layer][h], 1)
                dve.wait_ge(s_drel[layer][h], v + 1)
                for q in range(2):
                    if q == 0:
                        dve.wait_ge(s_Su[layer][h], v + 1)
                    else:
                        dve.wait_ge(s_fl[layer][h], v + 1)
                    dve.tensor_tensor(S[:, h, 4 * q:4 * q + 4, :],
                                      bc(iota_n[:, :].rearrange("p (a n) -> p a n", a=1), [P, 4, P]),
                                      bc(drel[:, h, 4 * q:4 * q + 4].rearrange("p (c a) -> p c a", a=1), [P, 4, P]),
                                      ALU.is_equal).then_inc(s_S[layer][h][q], 1)

            def add(layer, batch, h, t):
                v = batch[2] + t
                dve.wait_ge(s_sum[layer][h], v + 1)
                a = acc[:, ds(t, 1), :].rearrange("p a f -> p (a f)")
                dve.tensor_tensor(a, visit_sum[h][:, 0:F], a, ALU.add).then_inc(s_fl[layer][h], 1)

            def other_visits(layer, batch, g, h):
                lo, hi, _ = batch
                with dve.If(hi > lo + 1):
                    with dve.Fori(lo + 1, hi) as t:
                        build(layer, batch, g, h, t)
                        add(layer, batch, h, t)
                dve.wait_ge(s_fl[layer][h], batch[2] + hi + 1)
                dve.sem_inc(s_free[layer], 1)

            def next_indices(layer, g):
                dve.tensor_copy(idx_now[:, ds((g + 2) % SETS, 1), :].rearrange("p a c -> p (a c)"),
                                src_idx[:, ds(g * PAIR + 2 * PAIR, PAIR)]).then_inc(s_idx[layer], 1)

            def finish_layer_1(t):
                a = acc[:, ds(t, 1), :].rearrange("p a f -> p (a f)")
                di = dinv[:, ds(t, 1)]
                dve.scalar_tensor_tensor(a, a, di, b1row[:, :], ALU.mult, ALU.add).then_inc(s_fin0, 1)
                dve.wait_ge(s_fin0, t + 1)
                dve.tensor_scalar(a, a, 0.0, di, ALU.max, ALU.mult).then_inc(s_fin, 1)

            def mix_1(t, n):
                k = [0]

                def step(ins):
                    k[0] += 1
                    ins.then_inc(s_mch, 1)
                    dve.wait_ge(s_mch, t * 5 + k[0])

                dve.wait_ge(s_mK, t + 1)
                step(dve.tensor_reduce(sm[:, 28:30], pK[:, 0:D].rearrange("p (k n) -> p k n", k=KD)[:, :, 0:n], AX.X,
                                       ALU.max))
                step(dve.tensor_tensor(sm[:, 28:30], sm[:, 28:30], sm[:, 14:16], ALU.add))
                step(dve.tensor_tensor(sm[:, 30:32], sm[:, 28:30], sm[:, 16:18], ALU.max))
                dve.tensor_tensor(sm[:, 20:22], sm[:, 16:18], sm[:, 30:32], ALU.subtract)
                step(dve.tensor_tensor(sm[:, 24:26], sm[:, 14:16], sm[:, 30:32], ALU.subtract))
                step(dve.tensor_copy(sm[:, 16:18], sm[:, 30:32]))
                dve.sem_inc(s_mb, 1)

            def mix_3(t):
                dve.wait_ge(s_mE, t + 1)
                dve.tensor_tensor(sm[:, 18:20], sm[:, 18:20], sm[:, 22:24], ALU.mult).then_inc(s_mch2, 1)
                dve.wait_ge(s_mch2, t + 1)
                dve.tensor_tensor(sm[:, 18:20], sm[:, 18:20], sm[:, 26:28], ALU.add)
                dve.wait_ge(s_mG, t + 2)
                for k in range(KD):
                    last = dve.scalar_tensor_tensor(Gs[:, k, :], Gs[:, k, :], sm[:, 22 + k:23 + k],
                                                    pG[:, k * D:(k + 1) * D], ALU.mult, ALU.add)
                last.then_inc(s_mu, 1)

            def pair_of_layer_1(g, n, before):
                (b0, b1), (t0, f0), _ = read_control(dve, mybir.EngineType.DVE, g)
                next_indices(0, g)
                build(0, b0, g, 0, b0[0])
                build(0, b1, g, 1, b1[0])
                with dve.If(f0 > 0):
                    finish_layer_1(t0)
                if before is not None:
                    mix_3(before)
                add(0, b0, 0, b0[0])
                other_visits(0, b0, g, 0)
                if n is not None:
                    mix_1(g, n)
                add(0, b1, 1, b1[0])
                other_visits(0, b1, g, 1)

            pair_of_layer_1(0, P, None)
            with dve.Fori(1, TILES - 1) as g:
                pair_of_layer_1(g, P, g - 1)
            mix_3(TILES - 2)
            dve.memset(ET[:, :, LAST:P], 0.0)
            with dve.Fori(TILES - 1, TILES) as g:
                pair_of_layer_1(g, LAST, None)
            mix_3(TILES - 1)

            dve.wait_ge(s_mu, TILES)
            link(dve.reciprocal(sm[:, 18:20], sm[:, 18:20]))
            for c in range(KD):
                last = dve.tensor_scalar(Gs[:, c, :], Gs[:, c, :], sm[:, 18 + c:19 + c], None, ALU.mult)
            last.then_inc(s_m3, 1)
            dve.tensor_copy(bqb, bc(sm[:, 12:14].rearrange("p (k a) -> p k a", a=1), [P, KD, P]))
            dve.wait_ge(s_m1, 3)
            link(dve.tensor_tensor(lam, pE[:, :].rearrange("p (c d) -> p c d", c=KD),
                                   bc(bvrow.rearrange("p (a d) -> p a d", a=1), [P, KD, D]), ALU.add))
            for c in range(KD):
                link(dve.bn_stats(stats2[:, c, :], lam[:, c, :]))
                link(dve.bn_aggr(mv[:, :], stats2[:, c, :]))
                dve.tensor_copy(sm[:, 36 + c:37 + c], mv[:, 0:1])
                link(dve.tensor_copy(sm[:, 32 + c:33 + c], mv[:, 1:2]))
            dve.sem_inc(s_m3, 1)
            with dve.Fori(TILES, TILES + 1) as g:
                pair_of_layer_1(g, None, None)
            dve.wait_ge(s_m2, 3)
            link(dve.reciprocal(sm[:, 34:36], sm[:, 34:36]))
            link(dve.tensor_tensor(sm[:, 34:36], sm[:, 34:36], sm[:, 8:10], ALU.mult))
            link(dve.tensor_tensor(sm[:, 36:38], sm[:, 36:38], sm[:, 34:36], ALU.mult))
            link(dve.tensor_tensor(sm[:, 36:38], sm[:, 10:12], sm[:, 36:38], ALU.subtract))
            for c in range(KD):
                last = dve.tensor_scalar(lam[:, c, :], lam[:, c, :], sm[:, 34 + c:35 + c], sm[:, 36 + c:37 + c],
                                         ALU.mult, ALU.add)
            last.then_inc(s_m3, 1)
            with dve.Fori(TILES + 1, TILES + 2) as g:
                pair_of_layer_1(g, None, None)
            dve.wait_ge(s_m1, 5)
            dve.wait_ge(s_m2, 4)
            dve.tensor_tensor(crow[:, :], crow[:, :], pT[:, 0:D], ALU.add).then_inc(s_mixed, 1)

            with dve.Fori(TILES + 2, PAIRS) as g:
                pair_of_layer_1(g, None, None)
            _, (tend, _), _ = read_control(dve, mybir.EngineType.DVE, PAIRS)
            with dve.Fori(tend, TILES) as t:
                finish_layer_1(t)

            dve.tensor_copy(idx_now[:, 0:2, :], src_idx[:, 0:2 * PAIR].rearrange("p (a c) -> p a c", a=2))\
               .then_inc(s_idx[1], 2)
            dve.wait_ge(s_tab2, 16 * TILES)

            class Chain:
                PER = 7

                def __init__(self, k=0):
                    self.k = k

                def step(self, t, ins):
                    self.k += 1
                    assert self.k <= Chain.PER
                    ins.then_inc(s_dch, 1)
                    dve.wait_ge(s_dch, t * Chain.PER + self.k)

            def ff_1(t, ch):
                ch.step(t, dve.tensor_scalar(aggs, acc[:, ds(t, 1), :].rearrange("p a f -> p (a f)"), dinv[:, ds(t, 1)],
                                             None, ALU.mult))
                dve.sem_inc(s_aggs, 1)
                ch.step(t, dve.tensor_tensor(x1, xs[:, ds(t, 1), :].rearrange("p a f -> p (a f)"), crow[:, :],
                                             ALU.add))
                dve.sem_inc(s_passed, 1)

            def ff_norm(t, ch):
                dve.wait_ge(s_y1, t + 1)
                ch.step(t, dve.tensor_tensor(x1, x1, pY1[:, 0:D], ALU.add))
                ch.step(t, dve.bn_stats(stats[:, :], x1))
                dve.sem_inc(s_passed, 1)
                dve.bn_aggr(mv[:, :], stats[:, :]).then_inc(s_var, 1)
                dve.wait_ge(s_sd, t + 1)
                ch.step(t, dve.reciprocal(sm[:, 41:42], sm[:, 40:41]))
                dve.tensor_scalar(ln, x1, mv[:, 0:1], sm[:, 41:42], ALU.subtract, ALU.mult).then_inc(s_ln, 1)

            def ff_route(t, ch):
                dve.wait_ge(s_ln, t + 1)
                dve.wait_ge(s_basew, t * 16 + 16)
                dve.tensor_tensor(base, x1, ln, ALU.add).then_inc(s_base, 1)
                dve.wait_ge(s_base, t + 1)
                ch.step(t, dve.tensor_tensor_reduce(out=x1, in0=ln, in1=wrrow[:, :], scale=1.0, scalar=0.0,
                                                    op0=ALU.mult, op1=ALU.add, accum_out=sm[:, 42:43]))
                ch.step(t, dve.tensor_tensor(sm[:, 43:44], sm[:, 42:43], brcol[:, :], ALU.add))
                dve.tensor_copy(wts[:, ds(t, 1)], sm[:, 43:44])
                assert ch.k == Chain.PER

            def ff_3(t):
                rows = xs[:, ds(t, 1), :].rearrange("p a f -> p (a f)")
                dve.wait_ge(s_y, t + 1)
                dve.tensor_tensor(rows, pY[:, 0:D], fb2row[:, :], ALU.add).then_inc(s_yb, 1)
                dve.wait_ge(s_yb, t + 1)
                dve.tensor_scalar(rows, rows, sm[:, 43:44], None, ALU.mult).then_inc(s_wd, 1)

            def ff_route_and_3(t):
                ff_route(t, Chain(Chain.PER - 2))
                ff_3(t)

            with dve.Fori(0, PAIRS) as g:
                (b0, b1), (t0, f0), (t1, f1) = read_control(dve, mybir.EngineType.DVE, g)
                ch = Chain()
                next_indices(1, g)
                build(1, b0, g, 0, b0[0])
                with dve.If(f1 > 0):
                    ff_route(t1, Chain(Chain.PER - 2))
                with dve.If(f0 > 0):
                    ff_1(t0, ch)
                build(1, b1, g, 1, b1[0])
                add(1, b0, 0, b0[0])
                other_visits(1, b0, g, 0)
                with dve.If(f1 > 0):
                    ff_3(t1)
                with dve.If(f0 > 0):
                    ff_norm(t0, ch)
                add(1, b1, 1, b1[0])
                other_visits(1, b1, g, 1)
            _, (tend, _), (t1, f1) = read_control(dve, mybir.EngineType.DVE, PAIRS)
            with dve.If(f1 > 0):
                ff_route_and_3(t1)

            def prepare_selection():
                dve.memset(ones_m, 1.0)
                dve.memset(part, 0.0)
                for i, (b, n) in enumerate(ROUNDS):
                    for c in range((1 << n) - 1):
                        dve.memset(steps_of[:, i, c:c + 1].bitcast(i32), (c + 1) << b)
                link(dve.memset(zer, 0.0))
                link(dve.tensor_tensor_scan(lower, ident[:, :], bc(zer[:, 0:1], [P, P]), 0.0, ALU.add, ALU.add))
                link(dve.tensor_tensor(lower, lower, ident[:, :], ALU.subtract))
                link(dve.tensor_scalar(sm[:, 57:58], lower[:, LAST:LAST + 1], 1.0, 3.0e38, ALU.subtract, ALU.mult))

            def leftover(t, before):
                ch = Chain()
                ff_1(t, ch)
                if before is not None:
                    ff_3(before)
                ff_norm(t, ch)
                ff_route(t, ch)
                if before is None:
                    prepare_selection()

            leftover(tend, None)
            with dve.If(tend + 1 < TILES):
                with dve.Fori(tend + 1, TILES) as t:
                    leftover(t, t - 1)
            ff_3(TILES - 1)

            key, add_bits, rb = (sm[:, c:c + 1] for c in (52, 53, 54))
            key_i, add_i, cand_i = key.bitcast(i32), add_bits.bitcast(i32), cand.bitcast(i32)
            dve.wait_ge(s_wd, TILES)
            link(dve.tensor_tensor(wts[:, TILES - 1:TILES], wts[:, TILES - 1:TILES], lower[:, LAST:LAST + 1], ALU.mult))
            link(dve.tensor_tensor(wts[:, TILES - 1:TILES], wts[:, TILES - 1:TILES], sm[:, 57:58], ALU.add))
            link(dve.memset(key_i, 0))
            link(dve.tensor_scalar(eq, wts[:, :], 0.0, 0.0, ALU.is_ge, ALU.add, accum_out=part[:, 0:1]))
            dve.sem_inc(s_part, 1)
            dve.wait_ge(s_cnt, 1)
            link(dve.tensor_scalar(sm[:, 55:56], bank[2][:, 0:1], float(KSEL), None, ALU.is_ge))
            link(dve.tensor_scalar(sm[:, 58:59], sm[:, 55:56], 2.0, -1.0, ALU.mult, ALU.add))
            link(dve.tensor_scalar(sm[:, 56:57], sm[:, 55:56], float(KSEL - (N - KSEL + 1)), float(N - KSEL + 1),
                                   ALU.mult, ALU.add))
            link(dve.tensor_scalar(ws, wts[:, :], sm[:, 58:59], None, ALU.mult))
            link(dve.tensor_tensor(ws[:, TILES - 1:TILES], ws[:, TILES - 1:TILES], lower[:, LAST:LAST + 1], ALU.mult))
            link(dve.tensor_tensor(ws[:, TILES - 1:TILES], ws[:, TILES - 1:TILES], sm[:, 57:58], ALU.add))
            for i, (b, n) in enumerate(ROUNDS):
                m = (1 << n) - 1
                link(dve.tensor_tensor(cand_i[:, 0:m], steps_of[:, i, 0:m].bitcast(i32), bc(key_i, [P, m]),
                                       ALU.bitwise_or))
                for c in range(m):
                    last = dve.tensor_scalar(reach[:, c, :], ws, cand[:, c:c + 1], 0.0, ALU.is_ge, ALU.add,
                                             accum_out=part[:, c:c + 1])
                last.then_inc(s_part, 1)
                dve.wait_ge(s_cnt, i + 2)
                link(dve.tensor_scalar(cand[:, 0:m], bank[2][:, 0:m], sm[:, 56:57], 0.0, ALU.is_ge, ALU.add,
                                       accum_out=rb))
                link(dve.tensor_scalar(add_i, rb, float(1 << b), None, ALU.mult))
                link(dve.tensor_tensor(key_i, key_i, add_i, ALU.bitwise_or))
            link(dve.tensor_scalar(key, key, sm[:, 58:59], None, ALU.mult))
            thr = key
            link(dve.tensor_scalar(gt, wts[:, :], thr, 0.0, ALU.is_gt, ALU.add, accum_out=sm[:, 51:52]))
            link(dve.memset(colsum, 0.0))
            link(dve.tensor_scalar(eq, wts[:, :], thr, None, ALU.is_equal))
            dve.sem_inc(s_part, 1)
            dve.wait_ge(s_cnt, 2 + len(ROUNDS))
            link(dve.tensor_copy(colsum, bank[2][:, 0:TILES]))
            link(dve.tensor_tensor_scan(before, colsum, zer, 0.0, ALU.add, ALU.add))
            link(dve.tensor_tensor(before, before, colsum, ALU.subtract))
            link(dve.tensor_tensor(before, before, bank[3][:, 0:TILES], ALU.add))
            link(dve.tensor_scalar(sm[:, 59:60], bank[4][:, 0:1], -1.0, float(KSEL), ALU.mult, ALU.add))
            link(dve.scalar_tensor_tensor(selw, before, sm[:, 59:60], eq, ALU.is_lt, ALU.mult))
            link(dve.tensor_tensor(selw, selw, gt, ALU.add))
            for i in range(STEPS):
                dve.wait_ge(s_tl[i % SLOTS], 16 * (i // SLOTS + 1))
                for j in range(HG):
                    t = i * HG + j
                    last = dve.scalar_tensor_tensor(slots[i % SLOTS][:, j, :], xs[:, t, :], selw[:, t:t + 1],
                                                    slots[i % SLOTS][:, j, :], ALU.mult, ALU.add)
                last.then_inc(s_tf, 1)


_INS = ['x', 'src', 'dst', 'L0_gnn_W1', 'L0_gnn_b1', 'L0_gnn_W2', 'L0_gnn_b2', 'L0_mix_W_qk', 'L0_mix_b_qk',
        'L0_mix_W_v', 'L0_mix_b_v', 'L0_mix_gamma', 'L0_mix_beta', 'L0_ffn_attention_mask', 'L0_ffn_wr', 'L0_ffn_br',
        'L0_ffn_w1', 'L0_ffn_b1', 'L0_ffn_w2', 'L0_ffn_b2']
_OUTS = [((12500, 256), 'float32')]


def kernel(**inputs):
    import numpy as _np
    import concourse.bacc as _bacc
    from concourse import mybir as _mybir
    from concourse.bass_utils import run_bass_kernel_spmd as _run

    nc = _bacc.Bacc("TRN2", target_bir_lowering=False, num_devices=1, dynamic_dma_scratch_size=8192)
    arrays, args = {}, []
    for name in _INS:
        a = _np.ascontiguousarray(inputs[name])
        arrays[f"in_{name}_dram"] = a
        args.append(nc.dram_tensor(f"in_{name}_dram", a.shape, _mybir.dt.from_np(a.dtype), kind="ExternalInput").ap())
    for i, (shape, dtype) in enumerate(_OUTS):
        dt = _mybir.dt.from_np(_np.dtype(dtype))
        args.append(nc.dram_tensor(f"out_{i}_dram", shape, dt, kind="ExternalOutput").ap())
    gps_layer_kernel(nc, *args)
    r = _run(nc, [arrays], core_ids=[0])
    got = tuple(r.results[0][f"out_{i}_dram"] for i in range(len(_OUTS)))
    return got[0]
```
